# Optimizing a Trainium2 kernel written in Bass

```python
import numpy as np
import jax
import jax.numpy as jnp

def _softmax(x, axis=-1):
    return jax.nn.softmax(x, axis=axis)

def _gelu(x):
    return jax.nn.gelu(x, approximate=True)

def _silu(x):
    return jax.nn.silu(x)

def _sigmoid(x):
    return jax.nn.sigmoid(x)

def _layernorm(x, axis=-1, eps=1e-05):
    m = jnp.mean(x, axis=axis, keepdims=True)
    v = jnp.var(x, axis=axis, keepdims=True)
    return (x - m) / jnp.sqrt(v + eps)

def _scatter_add(tgt, idx, src, axis=0):
    return tgt.at[idx].add(src)

def _segment_sum(src, seg, n):
    return jax.ops.segment_sum(src, seg, n)
kernel_name = 'mk_gps_d1_gnn_r8_b44b51'

def setup_inputs(seed: int=0):
    np.random.seed(seed)
    _w = jnp.asarray

    def _rec_inputs():
        import jax
        import jax.numpy as jnp
        _gk = jax.random.key(seed)
        x = -0.0002117 + 1 * jax.random.normal(jax.random.fold_in(_gk, 1), (6250, 256), jnp.float32)
        src = jax.random.randint(jax.random.fold_in(_gk, 2), (100000,), 0, 6250, jnp.int32)
        dst = jnp.minimum((6250 * jax.random.uniform(jax.random.fold_in(_gk, 3), (100000,)) ** 2.0).astype(jnp.int32), 49999)
        _o = jnp.argsort(dst, stable=True)
        src = src[_o]
        dst = dst[_o]
        edge_attr_64 = 0.000279952 + 1.00013 * jax.random.normal(jax.random.fold_in(_gk, 11), (100000, 64), jnp.float32)
        return (x, src, dst, edge_attr_64)
    x, src, dst, edge_attr_64 = _rec_inputs()

    def _L0_gnn_setup():
        import jax, jax.numpy as jnp
        import numpy as np
        N = 12500
        E = 40000
        CIN = 256
        EDIM = 64
        EEMB = 256
        H = 1024
        LN_EPS = 1e-05

        def _ln(x, g, b):
            m = jnp.mean(x, axis=-1, keepdims=True)
            v = jnp.var(x, axis=-1, keepdims=True)
            return (x - m) * jax.lax.rsqrt(v + LN_EPS) * g + b
        key = jax.random.key(seed)
        ks = jax.random.split(key, 16)

        def w(k, i, o):
            return (jax.random.normal(k, (i, o), jnp.float32) / np.sqrt(i)).astype(jnp.float32)
        return {'x': jax.random.normal(ks[0], (N, CIN), jnp.float32), 'edge_index': jax.random.randint(ks[1], (2, E), 0, N, dtype=jnp.int64), 'edge_attr': jax.random.normal(ks[2], (E, EDIM), jnp.float32), 'eps': jnp.float32(0.0), 'ee_w1': w(ks[3], EDIM, EEMB), 'ee_b1': jnp.zeros((EEMB,), jnp.float32), 'ee_w2': w(ks[4], EEMB, CIN), 'ee_b2': jnp.zeros((CIN,), jnp.float32), 'w1': w(ks[5], CIN, H), 'b1': jnp.zeros((H,), jnp.float32), 'g1': jnp.ones((H,), jnp.float32), 'be1': jnp.zeros((H,), jnp.float32), 'w2': w(ks[6], H, H), 'b2': jnp.zeros((H,), jnp.float32), 'g2': jnp.ones((H,), jnp.float32), 'be2': jnp.zeros((H,), jnp.float32), 'w3': w(ks[7], H, CIN), 'b3': jnp.zeros((CIN,), jnp.float32), 'bn_g': jnp.ones((CIN,), jnp.float32), 'bn_b': jnp.zeros((CIN,), jnp.float32)}
    _L0_gnn_all = _L0_gnn_setup()
    _L0_gnn_in = {k: v for k, v in _L0_gnn_all.items() if k in ('eps', 'ee_w1', 'ee_b1', 'ee_w2', 'ee_b2', 'w1', 'b1', 'g1', 'be1', 'w2', 'b2', 'g2', 'be2', 'w3', 'b3', 'bn_g', 'bn_b')}
    del _L0_gnn_all

    def _L0_mix_setup():
        import jax, jax.numpy as jnp
        import numpy as np
        NUM_HEADS = 8
        key = jax.random.key(seed)
        ks = jax.random.split(key, 5)
        B, N, C = (8, 2048, 256)
        x = jax.random.normal(ks[0], (B, N, C), dtype=jnp.float32)
        Wq = jax.random.normal(ks[1], (C, C), dtype=jnp.float32) * 0.02
        Wkv = jax.random.normal(ks[2], (2 * C, C), dtype=jnp.float32) * 0.02
        Wproj = jax.random.normal(ks[3], (C, C), dtype=jnp.float32) * 0.02
        bproj = jnp.zeros((C,), dtype=jnp.float32)
        return {'x': x, 'Wq': Wq, 'Wkv': Wkv, 'Wproj': Wproj, 'bproj': bproj}
    _L0_mix_all = _L0_mix_setup()
    _L0_mix_in = {k: v for k, v in _L0_mix_all.items() if k in ('Wq', 'Wkv', 'Wproj', 'bproj')}
    del _L0_mix_all

    def _L0_ffn_setup():
        import jax, jax.numpy as jnp
        import numpy as np
        B, S, D = (8, 512, 256)
        H = 4 * D
        CAPACITY = 0.5
        key = jax.random.key(seed)
        ks = jax.random.split(key, 6)
        x = jax.random.normal(ks[0], (B, S, D), dtype=jnp.float32)
        attention_mask = jnp.zeros((B, 1, 1, S), dtype=jnp.float32)
        wr = jax.random.normal(ks[1], (D, 1), dtype=jnp.float32) * 0.02
        br = jnp.zeros((1,), dtype=jnp.float32)
        w1 = jax.random.normal(ks[2], (D, H), dtype=jnp.float32) * 0.02
        b1 = jnp.zeros((H,), dtype=jnp.float32)
        w2 = jax.random.normal(ks[3], (H, D), dtype=jnp.float32) * 0.02
        b2 = jnp.zeros((D,), dtype=jnp.float32)
        return {'x': x, 'attention_mask': attention_mask, 'wr': wr, 'br': br, 'w1': w1, 'b1': b1, 'w2': w2, 'b2': b2}
    _L0_ffn_all = _L0_ffn_setup()
    _L0_ffn_in = {k: v for k, v in _L0_ffn_all.items() if k in ('attention_mask', 'wr', 'br', 'w1', 'b1', 'w2', 'b2')}
    del _L0_ffn_all
    return {'x': x, 'src': src, 'dst': dst, 'edge_attr_64': edge_attr_64, 'L0_gnn_eps': _L0_gnn_in['eps'], 'L0_gnn_ee_w1': _L0_gnn_in['ee_w1'], 'L0_gnn_ee_b1': _L0_gnn_in['ee_b1'], 'L0_gnn_ee_w2': _L0_gnn_in['ee_w2'], 'L0_gnn_ee_b2': _L0_gnn_in['ee_b2'], 'L0_gnn_w1': _L0_gnn_in['w1'], 'L0_gnn_b1': _L0_gnn_in['b1'], 'L0_gnn_g1': _L0_gnn_in['g1'], 'L0_gnn_be1': _L0_gnn_in['be1'], 'L0_gnn_w2': _L0_gnn_in['w2'], 'L0_gnn_b2': _L0_gnn_in['b2'], 'L0_gnn_g2': _L0_gnn_in['g2'], 'L0_gnn_be2': _L0_gnn_in['be2'], 'L0_gnn_w3': _L0_gnn_in['w3'], 'L0_gnn_b3': _L0_gnn_in['b3'], 'L0_gnn_bn_g': _L0_gnn_in['bn_g'], 'L0_gnn_bn_b': _L0_gnn_in['bn_b'], 'L0_mix_Wq': _L0_mix_in['Wq'], 'L0_mix_Wkv': _L0_mix_in['Wkv'], 'L0_mix_Wproj': _L0_mix_in['Wproj'], 'L0_mix_bproj': _L0_mix_in['bproj'], 'L0_ffn_attention_mask': _L0_ffn_in['attention_mask'], 'L0_ffn_wr': _L0_ffn_in['wr'], 'L0_ffn_br': _L0_ffn_in['br'], 'L0_ffn_w1': _L0_ffn_in['w1'], 'L0_ffn_b1': _L0_ffn_in['b1'], 'L0_ffn_w2': _L0_ffn_in['w2'], 'L0_ffn_b2': _L0_ffn_in['b2']}

def reference(x, src, dst, edge_attr_64, L0_gnn_eps, L0_gnn_ee_w1, L0_gnn_ee_b1, L0_gnn_ee_w2, L0_gnn_ee_b2, L0_gnn_w1, L0_gnn_b1, L0_gnn_g1, L0_gnn_be1, L0_gnn_w2, L0_gnn_b2, L0_gnn_g2, L0_gnn_be2, L0_gnn_w3, L0_gnn_b3, L0_gnn_bn_g, L0_gnn_bn_b, L0_mix_Wq, L0_mix_Wkv, L0_mix_Wproj, L0_mix_bproj, L0_ffn_attention_mask, L0_ffn_wr, L0_ffn_br, L0_ffn_w1, L0_ffn_b1, L0_ffn_w2, L0_ffn_b2):
    import jax
    import jax.numpy as jnp

    def _L0_gnn_ref(x, edge_index, edge_attr, eps, ee_w1, ee_b1, ee_w2, ee_b2, w1, b1, g1, be1, w2, b2, g2, be2, w3, b3, bn_g, bn_b):
        import jax, jax.numpy as jnp
        import numpy as np
        N = 12500
        E = 40000
        CIN = 256
        EDIM = 64
        EEMB = 256
        H = 1024
        LN_EPS = 1e-05

        def _ln(x, g, b):
            m = jnp.mean(x, axis=-1, keepdims=True)
            v = jnp.var(x, axis=-1, keepdims=True)
            return (x - m) * jax.lax.rsqrt(v + LN_EPS) * g + b
        n = x.shape[0]
        sl = jnp.arange(n, dtype=edge_index.dtype)
        ei = jnp.concatenate([edge_index, jnp.stack([sl, sl], axis=0)], axis=1)
        ea = jnp.concatenate([edge_attr, jnp.zeros((n, edge_attr.shape[1]), edge_attr.dtype)], axis=0)
        src, dst = (ei[0], ei[1])
        e = jax.nn.relu(ea @ ee_w1 + ee_b1) @ ee_w2 + ee_b2
        msg = x[src] + e
        agg = jax.ops.segment_sum(msg, dst, num_segments=n)
        h = (1.0 + eps) * x + agg
        h = jax.nn.relu(_ln(h @ w1 + b1, g1, be1))
        h = jax.nn.relu(_ln(h @ w2 + b2, g2, be2))
        y = h @ w3 + b3
        out = x + y
        out = _ln(out, bn_g, bn_b)
        return jax.nn.relu(out)

    def _L0_mix_ref(x, Wq, Wkv, Wproj, bproj):
        import jax, jax.numpy as jnp
        import numpy as np
        NUM_HEADS = 8
        B, N, C = x.shape
        h = NUM_HEADS
        d = C // h
        q = jnp.einsum('bnc,oc->bno', x, Wq).reshape(B, N, h, d).transpose(0, 2, 1, 3)
        kv = jnp.einsum('bnc,oc->bno', x, Wkv).reshape(B, N, 2, h, d)
        k = kv[:, :, 0].transpose(0, 2, 1, 3)
        v = kv[:, :, 1].transpose(0, 2, 1, 3)
        q = jax.nn.elu(q) + 1.0
        k = jax.nn.elu(k) + 1.0
        k_sum = k.sum(axis=2)
        D_inv = 1.0 / jnp.maximum(jnp.einsum('bhnd,bhd->bhn', q, k_sum), 1e-06)
        context = jnp.einsum('bhnd,bhne->bhde', k, v)
        attn = jnp.einsum('bhnd,bhde->bhne', q, context) * D_inv[..., None]
        out = attn.transpose(0, 2, 1, 3).reshape(B, N, C)
        out = jnp.einsum('bnc,oc->bno', out, Wproj) + bproj
        return out

    def _L0_ffn_ref(x, attention_mask, wr, br, w1, b1, w2, b2):
        import jax, jax.numpy as jnp
        import numpy as np
        B, S, D = (8, 512, 256)
        H = 4 * D
        CAPACITY = 0.5
        b, s, d = x.shape
        weights = (jnp.einsum('bsd,do->bso', x, wr) + br)[..., 0]
        k = max(1, int(CAPACITY * s))
        kk = k - 1 if k > 1 else 1
        _, idx = jax.lax.top_k(weights, k)
        sel_idx = idx[:, :kk]
        sel = jnp.take_along_axis(x, sel_idx[:, :, None], axis=1)
        h = jax.nn.gelu(jnp.einsum('bkd,dh->bkh', sel, w1) + b1)
        y = jnp.einsum('bkh,hd->bkd', h, w2) + b2
        w_sel = jnp.take_along_axis(weights, sel_idx, axis=1)
        y = y * w_sel[..., None]
        batch_idx = jnp.arange(b)[:, None]
        processed = jnp.zeros_like(x).at[batch_idx, sel_idx].set(y)
        return processed + x
    edge_index = jnp.stack([src, dst])
    xn = _layernorm(x, axis=-1)
    x = x + _L0_gnn_ref(xn, edge_index, edge_attr_64, L0_gnn_eps, L0_gnn_ee_w1, L0_gnn_ee_b1, L0_gnn_ee_w2, L0_gnn_ee_b2, L0_gnn_w1, L0_gnn_b1, L0_gnn_g1, L0_gnn_be1, L0_gnn_w2, L0_gnn_b2, L0_gnn_g2, L0_gnn_be2, L0_gnn_w3, L0_gnn_b3, L0_gnn_bn_g, L0_gnn_bn_b) + _L0_mix_ref(xn[None], L0_mix_Wq, L0_mix_Wkv, L0_mix_Wproj, L0_mix_bproj)[0]
    x = x + _L0_ffn_ref(_layernorm(x, axis=-1)[None], L0_ffn_attention_mask, L0_ffn_wr, L0_ffn_br, L0_ffn_w1, L0_ffn_b1, L0_ffn_w2, L0_ffn_b2)[0]
    return x

_drawn_inputs = setup_inputs


def setup_inputs(seed=0):
    import zlib

    import numpy as np

    out = dict(_drawn_inputs(seed))
    spreads = {'L0_gnn_ee_b1': (0.0, 0.282),
     'L0_gnn_ee_b2': (0.0, 0.1),
     'L0_gnn_b1': (0.0, 0.8),
     'L0_gnn_g1': (1.0, 0.2),
     'L0_gnn_be1': (0.0, 0.315),
     'L0_gnn_b2': (0.0, 0.1),
     'L0_gnn_g2': (1.0, 0.2),
     'L0_gnn_be2': (0.0, 0.303),
     'L0_gnn_b3': (0.0, 0.1),
     'L0_gnn_bn_g': (1.0, 0.2),
     'L0_gnn_bn_b': (0.0, 0.1),
     'L0_mix_bproj': (0.0, 0.1),
     'L0_ffn_b1': (0.0, 0.8),
     'L0_ffn_b2': (0.0, 0.8)}
    factors = {'L0_mix_Wq': 8.0,
     'L0_mix_Wkv': 8.0,
     'L0_mix_Wproj': 8.0,
     'L0_ffn_wr': 5.269,
     'L0_ffn_w1': 5.841,
     'L0_ffn_w2': 5.507}
    for name, (base, spread) in spreads.items():
        noise = np.random.default_rng([zlib.crc32(name.encode()), seed]).standard_normal(out[name].shape)
        drawn = base * np.exp(spread * noise) if base else spread * noise
        out[name] = jnp.asarray(drawn.astype(out[name].dtype))
    for name, factor in factors.items():
        out[name] = (out[name] * factor).astype(out[name].dtype)
    return out
```

```python
from collections import namedtuple
from contextlib import ExitStack

import numpy as np
import concourse.bass as bass
from concourse import mybir

P = 128
C = 256
CC = C // P
W = 64
GE = 2
HEADS = 8
ED = 64
LN_EPS = 1e-5
CAPACITY = 0.5


Plan = namedtuple("Plan", "n nt np gpt groups tiles nb gr batch wid")


def plan(n_nodes, n_edges):
    nt = -(-n_nodes // P)
    gpt = -(-n_edges // (GE * P * nt))
    gpt += gpt % 2
    groups = nt * gpt
    nb = -(-groups // P)
    gr = -(-groups // nb)
    batch = max(b for b in range(1, 9) if nt % b == 0 and nt > b)
    return Plan(n=n_nodes, nt=nt, np=nt * P, gpt=gpt, groups=groups, tiles=groups * GE,
                nb=nb, gr=gr, batch=batch, wid=nt * P + W)


def constants(pl):
    i = np.arange(P)
    valid = (np.arange(pl.nt)[None, :] * P + i[:, None] < pl.n).astype(np.float32)
    return {
        "ident": np.eye(P, dtype=np.float32),
        "ones": np.ones((P, P), np.float32),
        "before": (i[:, None] < i[None, :]).astype(np.float32),
        "head": (i[:, None] // (C // HEADS) == i[None, :] // (C // HEADS)).astype(np.float32),
        "iota": np.tile(np.arange(W, dtype=np.float32), (P, 1)),
        "valid": valid,
        "below": (valid - 1.0) * np.float32(3e38),
        "expo": np.full((P, pl.nt), -0.5, np.float32),
    }


def ge(eng, sem, value):
    if isinstance(value, int) and value <= 0:
        return
    eng.wait_ge(sem, value)


def in_own(eng, spare):
    eng.sem_inc(spare, 1)


def in_pairs(eng, first, last, body):
    pairs = max(last - first, 0) // 2
    if pairs:
        with eng.Fori(0, pairs) as h:
            body(2 * h + first, h + first // 2, first % 2)
            body(2 * h + first + 1, h + (first + 1) // 2, (first + 1) % 2)
    for t in range(first + 2 * pairs, last):
        body(t, t // 2, t % 2)


def gps_kernel(nc, A, out, pl):
    f32, f16, i32 = mybir.dt.float32, mybir.dt.float16, mybir.dt.int32
    ALU, ACT, AX = mybir.AluOpType, mybir.ActivationFunctionType, mybir.AxisListType
    ds = bass.ds
    NT, GPT, TPB = pl.nt, pl.gpt, pl.gpt * GE
    BATCH, NBATCH = pl.batch, pl.nt // pl.batch
    H = A.w1.shape[2]
    HC, HH = H // P, H // 512
    HALF = GPT // 2
    KSEL = max(1, int(CAPACITY * pl.n))
    KSEL = KSEL - 1 if KSEL > 1 else 1

    x_rows = A.x.rearrange("(t p) c -> t p c", p=P)
    xn_d = nc.dram_tensor("xn_rows", (NT, P, C), f32, kind="Internal").ap()
    xm_d = nc.dram_tensor("mix_rows", (NT, P, C), f32, kind="Internal").ap()
    table = nc.dram_tensor("gather_table", (pl.np, 2 * C), f16, kind="Internal").ap()
    table_rows = table.rearrange("(t p) c -> t p c", p=P)
    out_rows = out.rearrange("(t p) c -> t p c", p=P)

    ctx = ExitStack()
    with ctx:
        def sb(name, shape, dt=f32):
            return ctx.enter_context(nc.sbuf_tensor(name, shape, dt))

        def sem(name):
            return ctx.enter_context(nc.semaphore(name))

        acc = sb("acc", [P, 4, pl.wid])
        ident = sb("ident", [P, P])
        ones = sb("ones", [P, P])
        before = sb("before", [P, P])
        valid = sb("valid", [P, NT])
        below = sb("below", [P, NT])
        ee2 = sb("ee2", [P, CC, C])
        wr_all = sb("wr_all", [P, NT])
        epscol = sb("epscol", [P, 1])
        g1c, be1c, g2c, be2c, fb1c = [sb(n, [P, HC]) for n in ("g1c", "be1c", "g2c", "be2c", "fb1c")]
        bits = sb("bits", [P, 32], i32)
        brc = sb("brc", [P, 1])

        class Carver:
            def __init__(self, base):
                self.base, self.at = base, 0

            def __call__(self, *shape, dt=f32):
                n = int(np.prod(shape))
                words = n if dt in (f32, i32) else -(-n // 2)
                ap = self.base[:, self.at:self.at + words]
                self.at += words
                assert self.at <= self.base.shape[1], (self.at, self.base.shape)
                if dt is not f32:
                    ap = ap.bitcast(dt)
                if len(shape) == 2:
                    ap = ap.rearrange("p (a b) -> p a b", b=shape[1])
                if len(shape) == 3:
                    ap = ap.rearrange("p (a b c) -> p a b c", b=shape[1], c=shape[2])
                return ap

        big = sb("big", [P, CC * pl.np if CC * pl.np > 12288 else 12288])
        qT = Carver(big)(CC, pl.np)
        wts = Carver(big)
        w1, w2, w3 = wts(CC, H), wts(HC, H), wts(HC, C)

        arena = sb("arena", [P, 14100])
        a = Carver(arena)
        slab = Carver(big)(BATCH, C)
        xs, xn, xt, ek, eq, ks, vs = [[a(C) for _ in range(2)] for _ in range(7)]
        tab = [a(2 * C, dt=f16) for _ in range(2)]
        xb, b2row = a(C), a(C)
        wq, wkv, wproj = a(CC, C), a(CC, 2 * C), a(CC, C)
        ctm = a(CC, P)
        dsti = a(pl.nb, GE * P, dt=i32)
        stats, mean, var, tmp = a(NT, 6), a(NT), a(NT), a(NT)
        rstd, nmr, expo = a(NT), a(NT), a(NT)
        span = a(4)
        bases, spans = a(pl.nb), a(pl.nb)
        b2c, twoeps, b1h = a(CC), a(1), a(CC)
        front_end = a.at

        a = Carver(arena)
        xg = a(TPB, 2 * C, dt=f16)
        ea = a(GPT, GE * P)
        hm = [a(2, GE * C, dt=f16) for _ in range(2)]
        oh = [a(GE, W, dt=f16) for _ in range(2)]
        dcl, q2, xml, xmo = a(C), a(C), a(C), a(C)
        idx = a(TPB, dt=i32)
        a.at = max(a.at, front_end)
        mixw, ksb, ee1, iota, bprow, head = a(CC, C), a(CC, P), a(C), a(W), a(C), a(P)
        src, rel = a(pl.tiles, dt=i32), a(pl.tiles)
        brow = a(pl.nb * pl.gr)
        browi, npass = a(pl.groups, dt=i32), a(2, dt=i32)

        a = Carver(arena)
        fw1, fw2 = a(CC, H), a(HC, C)
        b1row, b2mrow = a(H), a(H)
        b3row, bngrow, bnbrow, fb2row, wrrow = [a(C) for _ in range(5)]
        z1, z2, aT1, aT2 = a(H), a(H), a(HC, P), a(HC, P)
        gT = z1.rearrange("p (a b) -> p a b", b=P)
        hT, u, x2, xn2, xres, xmix = [a(C) for _ in range(6)]
        xn2T = a(CC, P)
        st1, st2, st3, st4 = a(2, 6), a(2, 6), a(6), a(6)
        mv1, mv2, mv3, mv4 = [a(2) for _ in range(4)]
        rs1, rs2, rs3, rs4, nm1, nm2, nm3, nm4, mh, wcol = [a(1) for _ in range(10)]
        a = Carver(arena)
        ob = [a(C) for _ in range(BATCH)]
        wv, gtm, eqm, csum, incl, rank, mw, junk = [a(NT) for _ in range(8)]
        pfx, cand, t1, flt, m = [a(1, dt=i32) for _ in range(5)]
        cnt, need = a(1), a(1)

        ps = ctx.enter_context(nc.psum_tensor("ps", [P, 8, 512], f32))
        psT = [ps[:, b, 0:C] for b in (0, 7)]
        psKV = [ps[:, 1 + s, :] for s in range(2)]
        psQ = [ps[:, b, 0:C] for b in (3, 6)]
        psX = ps[:, 4, 0:C + CC]
        psR = [ps[:, 5, :], ps[:, 6, :]]
        psM = ps[:, 5, :]
        psH = [ps[:, s, :] for s in range(2)]
        psS = [ps[:, 2 + s, 0:4 * W] for s in range(2)]
        psD, psO = ps[:, 4, 0:C], ps[:, 5, 0:C]
        pA, pB, pC = ps[:, 0:2, :], ps[:, 2:4, :], ps[:, 4:6, :]
        pHT, pXT = ps[:, 6, 0:C], ps[:, 6, C:2 * C]
        pY, pY2 = ps[:, 7, 0:C], ps[:, 2, 0:C]
        psCnt = ps[:, 0, 0:1]
        psRank, psCol = ps[:, 1, 0:NT], ps[:, 2, 0:NT]

        names = """const_in stats_done mean_done var_done rstd_done nmr_done dst_in dstf_done base_done
          rel_done relT_ready relT_done brow_ready brow_done browi_done span_done pass_done
          twoeps_done relu_b1_done acc_zero acc_init xn_done xT_ready xt_done xT_used kv_ready
          ek_done em_done k_done v_done q_ready eq_done eqm_done q_done ctx_done xb_done hi16_done
          tab_done ctm_done ksb_done m_ready mh_done ob_done front_done ea_ones idx_done
          hid_done hi_done lo_done oh_done scat_done ev_done d_ready dcl_done rcp_done q2_done
          o_ready xpb_done xm_done win_done edges_done wts_in late_in hT_ready hT_done z1_ready
          z1_biased z1_stats z1_aggr z1_rstd z1_nmr z1_done t1_ready a1_done z2_ready z2_biased
          z2_stats z2_aggr z2_rstd z2_nmr z2_done t2_ready a2_done y_ready xres_done u_done
          u_stats u_aggr u_rstd u_nmr u_norm u_gain u_affine x2_done x2_stats x2_aggr x2_rstd
          x2_nmr xn2_done base_out w_done w_put x2T_ready xn2T_done f1_ready g_done y2_ready
          y3_done wv_done cnt_done cnt_ready thr_ready eqm2_done rank_ready bit_step pick_step pool_spare dve_spare""".split()
        sems = {n: sem(n) for n in names + ["xml_in", "xm_stored", "xres_in", "xmix_in"]}
        for n, count in (("slab_in", BATCH), ("x_in", 2), ("xn_stored", 2), ("tab_stored", 2),
                         ("ea_in", GPT), ("xg_in", GPT)):
            sems[n] = [sem(f"{n}{j}") for j in range(count)]
        s = namedtuple("Semaphores", sems)(**sems)
        LOADED = 16 * NBATCH

        resident_loads = [(ident, A.ident), (ones, A.ones), (before, A.before), (valid, A.valid),
                          (below, A.below), (ee2, A.ee_w2), (g1c, A.g1), (be1c, A.be1),
                          (g2c, A.g2), (be2c, A.be2), (fb1c, A.fb1), (bits, A.bits)]
        front_loads = [(wq, A.wq), (wkv, A.wkv), (wproj, A.wproj), (expo, A.expo), (b2c, A.ee_b2c),
                       (b1h, A.ee_b1c), (ee1[0:ED, :], A.ee_w1), (ee1[ED:ED + 1, :], A.ee_b1),
                       (iota, A.iota), (head, A.head), (src, A.src)]
        front_rows = [(epscol, A.eps), (brc, A.br), (b2row, A.ee_b2), (bprow, A.bproj)]
        late_loads = [(fw1, A.fw1), (fw2, A.fw2)]
        late_rows = [(b1row, A.b1), (b2mrow, A.b2), (b3row, A.b3), (bngrow, A.bn_g),
                     (bnbrow, A.bn_b), (fb2row, A.fb2), (wrrow, A.wr)]
        n_const = 16 * (len(resident_loads) + len(front_loads) + len(front_rows))
        n_late = 16 * (len(late_loads) + len(late_rows))

        def passes(eng, edge_body, between=None):
            eng.wait_ge(s.pass_done, 1)
            n = eng.value_load(npass[0:1, 0:1], min_val=1, max_val=2 + pl.np // W)
            with eng.If(n > 1):
                with eng.Fori(1, n) as p:
                    if between is not None:
                        between(p)
                    with eng.Fori(0, NT) as i:
                        edge_body(i, p * NT + i)

        def turns(eng, body):
            for t in range(4):
                body(t, [t - k >= 0 for k in range(4)])
            with eng.Fori(4, NT) as t:
                body(t, [True] * 4)
            for t in range(NT, NT + 3):
                body(t, [t - k < NT for k in range(4)])

        block = ctx.enter_context(nc.Block())

        @block.sync
        def _(sp):
            for j in range(BATCH):
                sp.dma_start(slab[:, j, :], x_rows[j]).then_inc(s.slab_in[j], 16)
            sp.dma_start(dsti[0:pl.gr, :, :], A.dst).then_inc(s.dst_in, 16)
            for dst_, src_ in resident_loads + front_loads:
                sp.dma_start(dst_[:], src_).then_inc(s.const_in, 16)
            for dst_, src_ in front_rows:
                sp.dma_start(dst_[:], src_.partition_broadcast(P)).then_inc(s.const_in, 16)
            with sp.Fori(1, NBATCH) as b:
                for j in range(BATCH):
                    sp.wait_ge(s.stats_done, (b - 1) * BATCH + j + 1)
                    sp.dma_start(slab[:, j, :], x_rows[b * BATCH + j]).then_inc(s.slab_in[j], 16)

            def load(t, sl):
                ge(sp, s.xn_done, t - 1)
                sp.dma_start(xs[sl], x_rows[t]).then_inc(s.x_in[sl], 16)

            def store(t, sl):
                sp.wait_ge(s.xn_done, t + 1)
                sp.dma_start(xn_d[t], xn[sl]).then_inc(s.xn_stored[sl], 16)
                sp.wait_ge(s.tab_done, t + 1)
                sp.dma_start(table_rows[t], tab[sl]).then_inc(s.tab_stored[sl], 16)

            def body(t, h, sl):
                load(t + 1, 1 - sl)
                store(t, sl)

            load(0, 0)
            body(0, 0, 0)
            body(1, 0, 1)
            in_pairs(sp, 2, NT - 1, body)
            store(NT - 1, (NT - 1) % 2)

            sp.wait_ge(s.front_done, 1)

            def edges(i, q):
                for j in range(GPT):
                    ge(sp, s.hid_done, (q - 1) * GPT + j + 1)
                    sp.dma_start(ea[0:ED, j, :], A.ea[:, ds((i * GPT + j) * GE * P, GE * P)])\
                        .then_inc(s.ea_in[j], 16)

            edges(0, 0)
            with sp.Fori(1, NT) as i:
                edges(i, i)
            passes(sp, edges)

            sp.wait_ge(s.q2_done, NT)
            for dst_, src_ in ((w1, A.w1), (w2, A.w2), (w3, A.w3)):
                sp.dma_start(dst_[:], src_).then_inc(s.wts_in, 16)
            sp.wait_ge(s.edges_done, 1)
            sp.wait_ge(s.xm_stored, 16 * NT)
            for dst_, src_ in late_loads:
                sp.dma_start(dst_[:], src_).then_inc(s.late_in, 16)
            for dst_, src_ in late_rows:
                sp.dma_start(dst_[:], src_.partition_broadcast(P)).then_inc(s.late_in, 16)

            def rows(t):
                ge(sp, s.u_done, t)
                sp.dma_start(xres, xn_d[t]).then_inc(s.xres_in, 16)
                ge(sp, s.x2_done, t)
                sp.dma_start(xmix, xm_d[t]).then_inc(s.xmix_in, 16)

            rows(0)
            with sp.Fori(1, NT) as t:
                rows(t)

            with sp.Fori(0, NBATCH) as b:
                for j in range(BATCH):
                    sp.wait_ge(s.ob_done, b * BATCH + j + 1)
                    sp.dma_start(out_rows[b * BATCH + j], ob[j]).then_inc(s.slab_in[j], 16)
            for j in range(BATCH):
                sp.wait_ge(s.slab_in[j], LOADED + 16 * NBATCH)

        @block.gpsimd
        def _(pool):
            g = nc.gpsimd
            pool.wait_ge(s.const_in, n_const)
            pool.wait_ge(s.var_done, 1)
            g.tensor_tensor(rstd, var, expo, ALU.pow).then_inc(s.rstd_done, 1)

            def tables(t, h, sl):
                pool.wait_ge(s.xn_done, t + 1)
                ge(pool, s.tab_done, t)
                g.tensor_tensor(xb, xn[sl], b2row, ALU.add).then_inc(s.xb_done, 1)
                ge(pool, s.tab_stored[sl], 16 * h)
                pool.wait_ge(s.xb_done, t + 1)
                in_own(pool, s.pool_spare)
                g.tensor_copy(tab[sl][:, 0:C], xb).then_inc(s.hi16_done, 1)
                pool.wait_ge(s.hi16_done, t + 1)
                g.tensor_tensor(tab[sl][:, C:2 * C], xb, tab[sl][:, 0:C], ALU.subtract)\
                    .then_inc(s.tab_done, 1)

            tables(0, 0, 0)
            tables(1, 0, 1)
            in_pairs(pool, 2, NT, tables)

            pool.wait_ge(s.front_done, 1)
            for sl in range(2):
                pool.wait_ge(s.tab_stored[sl], 16 * ((NT + 1 - sl) // 2))
            g.memset(ea[ED:ED + 1, :, :], 1.0).then_inc(s.ea_ones, 1)
            pool.wait_ge(s.ea_ones, 1)

            def edges(i, q):
                for half in range(GPT // HALF):
                    ge(pool, s.scat_done, (q - 1) * GPT + (half + 1) * HALF)
                    in_own(pool, s.pool_spare)
                    at = slice(half * HALF * GE, (half + 1) * HALF * GE)
                    g.tensor_copy(idx[:, at], src[:, ds(i * TPB + half * HALF * GE, HALF * GE)])\
                        .then_inc(s.idx_done, 1)
                    pool.wait_ge(s.idx_done, q * (GPT // HALF) + half + 1)
                    in_own(pool, s.pool_spare)
                    for j in range(half * HALF * GE, (half + 1) * HALF * GE):
                        g.indirect_dma_start(
                            xg[:, j, :], None, table,
                            bass.IndirectOffsetOnAxis(idx[:, j:j + 1].bitcast(mybir.dt.uint32), 0))\
                            .then_inc(s.xg_in[j // GE], 16)

            edges(0, 0)
            with pool.Fori(1, NT) as i:
                edges(i, i)
            passes(pool, edges)

            pool.wait_ge(s.late_in, n_late)

            def power(mv, rs, ready, done, t):
                pool.wait_ge(ready, t + 1)
                g.tensor_tensor(rs, mv[:, 1:2], mh, ALU.pow).then_inc(done, 1)

            g.memset(mh, -0.5).then_inc(s.mh_done, 1)
            pool.wait_ge(s.mh_done, 1)

            def body(t, do):
                if do[0]:
                    power(mv1, rs1, s.z1_aggr, s.z1_rstd, t)
                if do[1]:
                    power(mv2, rs2, s.z2_aggr, s.z2_rstd, t - 1)
                if do[2]:
                    r = t - 2
                    pool.wait_ge(s.xres_in, 16 * (r + 1))
                    g.tensor_tensor(xres, xres, b3row, ALU.add).then_inc(s.xres_done, 1)
                    power(mv3, rs3, s.u_aggr, s.u_rstd, r)
                    pool.wait_ge(s.u_norm, r + 1)
                    g.tensor_tensor(u, u, bngrow, ALU.mult).then_inc(s.u_gain, 1)
                    pool.wait_ge(s.u_gain, r + 1)
                    g.tensor_tensor(u, u, bnbrow, ALU.add).then_inc(s.u_affine, 1)
                    power(mv4, rs4, s.x2_aggr, s.x2_rstd, r)

            turns(pool, body)

        @block.scalar
        def _(act):
            a_ = nc.scalar
            act.wait_ge(s.const_in, n_const)
            for c in range(CC):
                a_.activation(b1h[:, c:c + 1], b1h[:, c:c + 1], ACT.Relu).then_inc(s.relu_b1_done, 1)
            act.wait_ge(s.nmr_done, 1)

            def normalize(t, h, sl):
                act.wait_ge(s.x_in[sl], 16 * (h + 1))
                ge(act, s.xT_ready, t - 1)
                ge(act, s.tab_done, t - 1)
                ge(act, s.xn_stored[sl], 16 * h)
                a_.activation(xn[sl], xs[sl], ACT.Identity, bias=nmr[:, ds(t, 1)],
                              scale=rstd[:, ds(t, 1)]).then_inc(s.xn_done, 1)

            def exps(t, sl):
                act.wait_ge(s.kv_ready, t + 1)
                ge(act, s.k_done, t - 1)
                a_.activation(ek[sl], psKV[sl][:, 0:C], ACT.Exp).then_inc(s.ek_done, 1)
                act.wait_ge(s.q_ready, t + 1)
                ge(act, s.q_done, t - 1)
                a_.activation(eq[sl], psQ[sl], ACT.Exp).then_inc(s.eq_done, 1)

            def body(t, h, sl):
                normalize(t + 1, h + sl, 1 - sl)
                exps(t, sl)

            normalize(0, 0, 0)
            body(0, 0, 0)
            body(1, 0, 1)
            in_pairs(act, 2, NT - 1, body)
            exps(NT - 1, (NT - 1) % 2)

            act.wait_ge(s.front_done, 1)

            def load_mix(i):
                ge(act, s.xpb_done, i)
                act.dma_start(xml, x_rows[i]).then_inc(s.xml_in, 16)

            def store_mix(i):
                act.wait_ge(s.xm_done, i + 1)
                act.dma_start(xm_d[i], xmo).then_inc(s.xm_stored, 16)

            def edges(i, q, mix=None):
                for j in range(GPT):
                    if mix is not None and j == 1:
                        mix(i)
                    n = q * GPT + j
                    act.wait_ge(s.hid_done, n + 1)
                    ge(act, s.scat_done, n - 1)
                    a_.activation(hm[j % 2][:, 0, :], psH[j % 2], ACT.Relu).then_inc(s.hi_done, 1)

            def move_mix(i):
                store_mix(i - 1)
                load_mix(i)

            edges(0, 0, load_mix)
            with act.Fori(1, NT) as i:
                edges(i, i, move_mix)
            store_mix(NT - 1)
            passes(act, edges)

            act.wait_ge(s.late_in, n_late)

            def affine(dst_, src_, gcol, bcol, done, func=ACT.Relu):
                for j in range(HC):
                    i_ = a_.activation(dst_[:, j, :], src_[:, j // 4, (j % 4) * P:(j % 4 + 1) * P],
                                       func, bias=bcol[:, j:j + 1],
                                       scale=1.0 if gcol is None else gcol[:, j:j + 1])
                    i_.then_inc(done, 1)

            def body_n(t, do):
                if do[2]:
                    act.wait_ge(s.t2_ready, t - 1)
                    ge(act, s.y_ready, t - 2)
                    affine(aT2, pC, g2c, be2c, s.a2_done)
                if do[0]:
                    act.wait_ge(s.z1_nmr, 2 * (t + 1))
                    a_.activation(z1, z1, ACT.Identity, bias=nm1, scale=rs1).then_inc(s.z1_done, 1)
                if do[0]:
                    act.wait_ge(s.t1_ready, t + 1)
                    ge(act, s.z2_ready, HH * t)
                    affine(aT1, pC, g1c, be1c, s.a1_done)
                if do[3]:
                    act.wait_ge(s.f1_ready, t - 2)
                    if do[0]:
                        act.wait_ge(s.t1_ready, t + 1)
                    affine(gT, pA, None, fb1c, s.g_done, ACT.Gelu_apprx_tanh)
                if do[1]:
                    act.wait_ge(s.z2_nmr, 2 * t)
                    a_.activation(z2, z2, ACT.Identity, bias=nm2, scale=rs2).then_inc(s.z2_done, 1)

            turns(act, body_n)

        @block.tensor
        def _(pe):
            mm = nc.tensor.matmul
            pe.wait_ge(s.const_in, n_const)
            pe.wait_ge(s.rel_done, pl.nb)
            pe.wait_ge(s.span_done, 1)
            for b in range(pl.nb):
                for h in range(GE):
                    n = b * GE + h
                    ge(pe, s.relT_done, n - 1)
                    nc.tensor.transpose(psR[n % 2][:, 0:pl.gr], dsti.bitcast(f32)[0:pl.gr, b, h * P:(h + 1) * P],
                                        ident[0:pl.gr, 0:pl.gr]).then_inc(s.relT_ready, 1)
            pe.wait_ge(s.relT_done, pl.nb * GE)
            for b in range(pl.nb):
                for k in range(2):
                    last = mm(psR[k][0:1, b * pl.gr:(b + 1) * pl.gr], (bases, spans)[k][0:pl.gr, b:b + 1],
                              ident[0:pl.gr, 0:pl.gr], start=True, stop=True)
            last.then_inc(s.brow_ready, 1)
            pe.wait_ge(s.brow_done, 2)

            def transposes(t, sl):
                pe.wait_ge(s.xn_done, t + 1)
                ge(pe, s.xT_used, t - 1)
                for c in range(CC):
                    i_ = nc.tensor.transpose(psT[sl][:, c * P:(c + 1) * P], xn[sl][:, c * P:(c + 1) * P], ident[:])
                i_.then_inc(s.xT_ready, 1)

            def project(t, sl):
                pe.wait_ge(s.xt_done, t + 1)
                ge(pe, s.v_done, t - 1)
                ge(pe, s.k_done, t - 1)
                for c in range(CC):
                    i_ = mm(psKV[sl], xt[sl][:, c * P:(c + 1) * P], wkv[:, c, :], start=c == 0, stop=c == CC - 1)
                i_.then_inc(s.kv_ready, 1)
                ge(pe, s.q_done, t - 1)
                for o in range(CC):
                    for c in range(CC):
                        i_ = mm(psQ[sl][:, o * P:(o + 1) * P], wq[:, c, o * P:(o + 1) * P],
                                xt[sl][:, c * P:(c + 1) * P], start=c == 0, stop=c == CC - 1)
                i_.then_inc(s.q_ready, 1)

            def context(t, sl, first=False, last=False):
                pe.wait_ge(s.k_done, t + 1)
                pe.wait_ge(s.v_done, t + 1)
                for c in range(CC):
                    half = slice(c * P, (c + 1) * P)
                    mm(psX[:, half], vs[sl][:, half], ks[sl][:, half], start=first and c == 0,
                       stop=False, skip_group_check=True)
                for c in range(CC):
                    i_ = mm(psX[:, C + c:C + c + 1], ks[sl][:, c * P:(c + 1) * P], valid[:, ds(t, 1)],
                            start=False, stop=last and c == CC - 1, skip_group_check=True)
                i_.then_inc(s.ctx_done, 1)

            transposes(0, 0)
            transposes(1, 1)
            project(0, 0)

            def body(t, h, sl):
                transposes(t + 1, 1 - sl)
                project(t, sl)
                context(t - 1, 1 - sl)

            transposes(2, 0)
            project(1, 1)
            context(0, 0, first=True)

            in_pairs(pe, 2, NT - 1, body)
            project(NT - 1, (NT - 1) % 2)
            context(NT - 2, (NT - 2) % 2)
            context(NT - 1, (NT - 1) % 2, last=True)

            pe.wait_ge(s.ctm_done, CC)
            for c in range(CC):
                i_ = mm(psM[:, c * C:(c + 1) * C], ctm[:, c, :], wproj[:, c, :], start=True, stop=True)
            i_.then_inc(s.m_ready, 1)
            pe.wait_ge(s.front_done, 1)
            pe.wait_ge(s.ea_ones, 1)

            def hidden(j, q):
                n = q * GPT + j
                pe.wait_ge(s.ea_in[j], 16 * (q + 1))
                ge(pe, s.lo_done, n - 1)
                for e in range(GE):
                    i_ = mm(psH[j % 2][:, e * C:(e + 1) * C], ea[0:ED + 1, j, e * P:(e + 1) * P],
                            ee1[0:ED + 1, :], start=True, stop=True)
                i_.then_inc(s.hid_done, 1)

            def scatter(j, q):
                n = q * GPT + j
                pe.wait_ge(s.xg_in[j], 16 * GE * (q + 1))
                pe.wait_ge(s.lo_done, n + 1)
                pe.wait_ge(s.oh_done, n + 1)
                ge(pe, s.ev_done, n - 1)
                for c in range(2 * CC):
                    for e in range(GE):
                        for part in range(2):
                            if c < CC:
                                rows = xg[:, j * GE + e, part * C + c * P:part * C + (c + 1) * P]
                            else:
                                at = e * C + (c - CC) * P
                                rows = hm[j % 2][:, part, at:at + P]
                            i_ = mm(psS[j % 2][:, c * W:(c + 1) * W], rows, oh[j % 2][:, e, :],
                                    start=e == 0 and part == 0, stop=e == GE - 1 and part == 1)
                i_.then_inc(s.scat_done, 1)

            def denominators(i):
                ge(pe, s.rcp_done, i)
                for c in range(CC):
                    i_ = mm(psD[:, c * P:(c + 1) * P], ksb[:, c, :], qT[:, c, ds(i * P, P)],
                            start=True, stop=True)
                i_.then_inc(s.d_ready, 1)

            def attention(i):
                pe.wait_ge(s.q2_done, i + 1)
                ge(pe, s.xm_done, i)
                for c in range(CC):
                    i_ = mm(psO, q2[:, c * P:(c + 1) * P], mixw[:, c, :], start=c == 0, stop=c == CC - 1)
                i_.then_inc(s.o_ready, 1)

            def edges(i, q, mix=False):
                hidden(0, q)
                if mix:
                    denominators(i)
                for j in range(1, GPT):
                    hidden(j, q)
                    scatter(j - 1, q)
                if mix:
                    attention(i)
                scatter(GPT - 1, q)

            edges(0, 0, True)
            with pe.Fori(1, NT) as i:
                edges(i, i, True)
            passes(pe, edges)

            pe.wait_ge(s.edges_done, 1)
            pe.wait_ge(s.wts_in, 48)
            pe.wait_ge(s.late_in, n_late)

            def body_n(t, do):
                if do[0]:
                    ge(pe, s.hT_done, t)
                    for o in range(CC):
                        for c in range(CC):
                            i_ = mm(pHT[:, o * P:(o + 1) * P], ee2[:, c, o * P:(o + 1) * P],
                                    acc[:, CC + c, ds(t * P, P)], start=c == 0, stop=c == CC - 1)
                    i_.then_inc(s.hT_ready, 1)
                    pe.wait_ge(s.hT_done, t + 1)
                    ge(pe, s.g_done, HC * (t - 3))
                    for n in range(HH):
                        for c in range(CC):
                            i_ = mm(pA[:, n, :], hT[:, c * P:(c + 1) * P], w1[:, c, n * 512:(n + 1) * 512],
                                    start=c == 0, stop=c == CC - 1)
                        i_.then_inc(s.z1_ready, 1)
                if do[2]:
                    pe.wait_ge(s.z2_done, t - 1)
                    pe.wait_ge(s.a1_done, HC * (min(t, NT) if isinstance(t, int) else t))
                    for j in range(HC):
                        i_ = nc.tensor.transpose(pC[:, j // 4, (j % 4) * P:(j % 4 + 1) * P],
                                                 z2[:, j * P:(j + 1) * P], ident[:])
                    i_.then_inc(s.t2_ready, 1)
                if do[3]:
                    pe.wait_ge(s.xn2_done, t - 2)
                    ge(pe, s.xn2T_done, t - 3)
                    for c in range(CC):
                        i_ = nc.tensor.transpose(pXT[:, c * P:(c + 1) * P], xn2[:, c * P:(c + 1) * P], ident[:])
                    i_.then_inc(s.x2T_ready, 1)
                if do[1]:
                    pe.wait_ge(s.a1_done, HC * t)
                    ge(pe, s.z2_biased, HH * (t - 1))
                    ge(pe, s.y3_done, t - 3)
                    for n in range(HH):
                        for k in range(HC):
                            i_ = mm(pB[:, n, :], aT1[:, k, :], w2[:, k, n * 512:(n + 1) * 512],
                                    start=k == 0, stop=k == HC - 1)
                        i_.then_inc(s.z2_ready, 1)
                if do[0]:
                    pe.wait_ge(s.z1_done, t + 1)
                    ge(pe, s.a1_done, HC * t)
                    if do[2]:
                        pe.wait_ge(s.a2_done, HC * (t - 1))
                    for j in range(HC):
                        i_ = nc.tensor.transpose(pC[:, j // 4, (j % 4) * P:(j % 4 + 1) * P],
                                                 z1[:, j * P:(j + 1) * P], ident[:])
                    i_.then_inc(s.t1_ready, 1)
                if do[3]:
                    pe.wait_ge(s.xn2T_done, t - 2)
                    if do[0]:
                        pe.wait_ge(s.z1_biased, HH * (t + 1))
                    for j in range(HC):
                        for c in range(CC):
                            i_ = mm(pA[:, j // 4, (j % 4) * P:(j % 4 + 1) * P], fw1[:, c, j * P:(j + 1) * P],
                                    xn2T[:, c, :], start=c == 0, stop=c == CC - 1)
                    i_.then_inc(s.f1_ready, 1)
                if do[2]:
                    ge(pe, s.u_done, t - 2)
                    for k in range(HC):
                        pe.wait_ge(s.a2_done, HC * (t - 2) + k + 1)
                        i_ = mm(pY, aT2[:, k, :], w3[:, k, :], start=k == 0, stop=k == HC - 1)
                    i_.then_inc(s.y_ready, 1)
                if do[3]:
                    ge(pe, s.y3_done, t - 3)
                    pe.wait_ge(s.z2_biased, HH * (min(t, NT) if isinstance(t, int) else t))
                    for k in range(HC):
                        pe.wait_ge(s.g_done, HC * (t - 3) + k + 1)
                        i_ = mm(pY2, gT[:, k, :], fw2[:, k, :], start=k == 0, stop=k == HC - 1)
                    i_.then_inc(s.y2_ready, 1)

            turns(pe, body_n)

            with pe.Fori(0, 32) as i:
                pe.wait_ge(s.cnt_done, i + 1)
                mm(psCnt, ones[:], cnt, start=True, stop=True).then_inc(s.cnt_ready, 1)
            pe.wait_ge(s.cnt_done, 33)
            mm(psCnt, ones[:], cnt, start=True, stop=True).then_inc(s.thr_ready, 1)
            pe.wait_ge(s.eqm2_done, 1)
            mm(psRank, before[:], eqm, start=True, stop=True)
            mm(psCol, ones[:], eqm, start=True, stop=True).then_inc(s.rank_ready, 1)

        @block.vector
        def _(dve):
            v = nc.vector
            dve.wait_ge(s.dst_in, 16)
            dve.wait_ge(s.const_in, n_const)
            dstf = dsti.bitcast(f32)[0:pl.gr]
            v.tensor_copy(dstf, dsti[0:pl.gr]).then_inc(s.dstf_done, 1)
            dve.wait_ge(s.dstf_done, 1)
            v.tensor_reduce(bases[0:pl.gr, :], dstf, AX.X, ALU.min).then_inc(s.base_done, 1)
            v.tensor_reduce(spans[0:pl.gr, :], dstf, AX.X, ALU.max).then_inc(s.base_done, 1)
            dve.wait_ge(s.base_done, 2)
            v.tensor_tensor(spans[0:pl.gr, :], spans[0:pl.gr, :], bases[0:pl.gr, :], ALU.subtract)\
                .then_inc(s.span_done, 1)
            for b in range(pl.nb):
                i_ = v.tensor_scalar(dstf[:, b, :], dstf[:, b, :], bases[0:pl.gr, b:b + 1], None, ALU.subtract)
                i_.then_inc(s.rel_done, 1)
            v.memset(acc[:], 0.0).then_inc(s.acc_zero, 1)
            relv = rel.rearrange("p (g e) -> p e g", e=GE)
            for b in range(pl.nb):
                for h in range(GE):
                    n = b * GE + h
                    gn = min(pl.gr, pl.groups - b * pl.gr)
                    dve.wait_ge(s.relT_ready, n + 1)
                    v.tensor_copy(relv[:, h, b * pl.gr:b * pl.gr + gn], psR[n % 2][:, 0:gn]).then_inc(s.relT_done, 1)
            dve.wait_ge(s.brow_ready, 1)
            v.tensor_copy(brow[0:1, :], psR[0][0:1, 0:pl.nb * pl.gr]).then_inc(s.brow_done, 1)
            v.tensor_reduce(span[0:1, 0:1], psR[1][0:1, 0:pl.nb * pl.gr], AX.X, ALU.max).then_inc(s.brow_done, 1)
            dve.wait_ge(s.brow_done, 2)
            v.tensor_copy(browi[0:1, :], brow[0:1, 0:pl.groups]).then_inc(s.browi_done, 1)
            v.tensor_copy(npass[0:1, 1:2], span[0:1, 0:1]).then_inc(s.browi_done, 1)
            dve.wait_ge(s.browi_done, 2)
            v.tensor_scalar(npass[0:1, 1:2], npass[0:1, 1:2], W.bit_length() - 1, None, ALU.arith_shift_right)\
                .then_inc(s.browi_done, 1)
            dve.wait_ge(s.browi_done, 3)
            v.tensor_scalar(npass[0:1, 0:1], npass[0:1, 1:2], 1.0, None, ALU.add).then_inc(s.pass_done, 1)
            v.tensor_scalar(twoeps, epscol[:], 2.0, None, ALU.add).then_inc(s.twoeps_done, 1)
            dve.wait_ge(s.twoeps_done, 1)
            dve.wait_ge(s.acc_zero, 1)
            dve.wait_ge(s.relu_b1_done, CC)
            for c in range(CC):
                v.tensor_scalar(acc[:, CC + c, :], acc[:, CC + c, :], b1h[:, c:c + 1], None, ALU.add)\
                    .then_inc(s.acc_init, 1)
            with dve.Fori(0, NBATCH) as b:
                for j in range(BATCH):
                    dve.wait_ge(s.slab_in[j], 16 * (b + 1))
                    v.bn_stats(stats[:, ds(b * BATCH + j, 1), :], slab[:, j, :]).then_inc(s.stats_done, 1)
            dve.wait_ge(s.stats_done, NT)
            me, ve, mo, vo = (stats[:, :, k] for k in (1, 2, 4, 5))
            v.tensor_tensor(mean, me, mo, ALU.add).then_inc(s.mean_done, 1)
            v.tensor_tensor(tmp, me, mo, ALU.subtract).then_inc(s.mean_done, 1)
            v.tensor_tensor(var, ve, vo, ALU.add).then_inc(s.mean_done, 1)
            dve.wait_ge(s.mean_done, 3)
            v.tensor_scalar(mean, mean, -0.5, None, ALU.mult).then_inc(s.mean_done, 1)
            v.tensor_tensor(tmp, tmp, tmp, ALU.mult).then_inc(s.mean_done, 1)
            v.tensor_scalar(var, var, 1.0 / C, LN_EPS, ALU.mult, ALU.add).then_inc(s.mean_done, 1)
            dve.wait_ge(s.mean_done, 6)
            v.scalar_tensor_tensor(var, tmp, 0.25, var, ALU.mult, ALU.add).then_inc(s.var_done, 1)
            dve.wait_ge(s.rstd_done, 1)
            v.tensor_tensor(nmr, mean, rstd, ALU.mult).then_inc(s.nmr_done, 1)

            def take_xT(t, sl):
                dve.wait_ge(s.xT_ready, t + 1)
                ge(dve, s.q_ready, t - 1)
                v.tensor_copy(xt[sl], psT[sl]).then_inc(s.xt_done, 1)
                for c in range(CC):
                    i_ = v.tensor_scalar(acc[:, c, ds(t * P, P)], psT[sl][:, c * P:(c + 1) * P],
                                         twoeps, b2c[:, c:c + 1], ALU.mult, ALU.add)
                i_.then_inc(s.xT_used, 1)

            def take_kvq(t, sl):
                dve.wait_ge(s.ek_done, t + 1)
                v.tensor_scalar(ek[sl], ek[sl], 1.0, None, ALU.min).then_inc(s.em_done, 1)
                ge(dve, s.ctx_done, t - 1)
                v.tensor_copy(vs[sl], psKV[sl][:, C:2 * C]).then_inc(s.v_done, 1)
                dve.wait_ge(s.em_done, t + 1)
                v.scalar_tensor_tensor(ks[sl], psKV[sl][:, 0:C], 0.0, ek[sl], ALU.max, ALU.add)\
                    .then_inc(s.k_done, 1)
                dve.wait_ge(s.eq_done, t + 1)
                v.tensor_scalar(eq[sl], eq[sl], 1.0, None, ALU.min).then_inc(s.eqm_done, 1)
                dve.wait_ge(s.eqm_done, t + 1)
                v.scalar_tensor_tensor(
                    qT[:, :, ds(t * P, P)], psQ[sl].rearrange("p (a b) -> p a b", b=P), 0.0,
                    eq[sl].rearrange("p (a b) -> p a b", b=P), ALU.max, ALU.add).then_inc(s.q_done, 1)

            def body(t, h, sl):
                take_xT(t + 1, 1 - sl)
                take_kvq(t, sl)

            take_xT(0, 0)
            body(0, 0, 0)
            body(1, 0, 1)
            in_pairs(dve, 2, NT - 1, body)
            take_kvq(NT - 1, (NT - 1) % 2)

            dve.wait_ge(s.ctx_done, NT)
            for c in range(CC):
                v.tensor_tensor(ctm[:, c, :], psX[:, c * P:(c + 1) * P], head, ALU.mult).then_inc(s.ctm_done, 1)
                v.tensor_scalar(ksb[:, c, :], head, psX[:, C + c:C + c + 1], None, ALU.mult).then_inc(s.ksb_done, 1)
            dve.wait_ge(s.ksb_done, CC)
            dve.wait_ge(s.m_ready, 1)
            for sl in range(2):
                dve.wait_ge(s.xn_stored[sl], 16 * ((NT + 1 - sl) // 2))
                dve.wait_ge(s.tab_stored[sl], 16 * ((NT + 1 - sl) // 2))
            v.tensor_copy(mixw, psM.rearrange("p (a b) -> p a b", b=C)).then_inc(s.front_done, 1)
            dve.wait_ge(s.front_done, 1)

            def one_hot(i, j, q):
                n = q * GPT + j
                ge(dve, s.scat_done, n - 1)
                for e in range(GE):
                    i_ = v.tensor_scalar(oh[j % 2][:, e, :], iota, rel[:, ds((i * GPT + j) * GE + e, 1)], None,
                                         ALU.is_equal)
                i_.then_inc(s.oh_done, 1)

            def low_part(j, q):
                n = q * GPT + j
                dve.wait_ge(s.hi_done, n + 1)
                v.scalar_tensor_tensor(hm[j % 2][:, 1, :], psH[j % 2], 0.0, hm[j % 2][:, 0, :], ALU.max,
                                       ALU.subtract).then_inc(s.lo_done, 1)

            def window(i, j, q):
                n = q * GPT + j
                base = dve.value_load(browi[0:1, ds(i * GPT + j, 1)], min_val=0, max_val=pl.np)
                dve.wait_ge(s.scat_done, n + 1)
                ge(dve, s.ev_done, n)
                v.tensor_tensor(acc[:, :, ds(base, W)], psS[j % 2].rearrange("p (a b) -> p a b", b=W),
                                acc[:, :, ds(base, W)], ALU.add).then_inc(s.ev_done, 1)

            def edges(i, q, mix=False):
                for j in range(GPT):
                    one_hot(i, j, q)
                    low_part(j, q)
                    if j:
                        window(i, j - 1, q)
                    if mix and j == 1:
                        dve.wait_ge(s.d_ready, i + 1)
                        ge(dve, s.xm_done, i)
                        v.tensor_scalar(dcl, psD, 1e-6, None, ALU.max).then_inc(s.dcl_done, 1)
                        dve.wait_ge(s.dcl_done, i + 1)
                        v.reciprocal(dcl, dcl).then_inc(s.rcp_done, 1)
                        dve.wait_ge(s.rcp_done, i + 1)
                        ge(dve, s.o_ready, i)
                        v.tensor_tensor(q2.rearrange("p (a b) -> p a b", b=P), qT[:, :, ds(i * P, P)],
                                        dcl.rearrange("p (a b) -> p a b", b=P), ALU.mult).then_inc(s.q2_done, 1)
                window(i, GPT - 1, q)
                if mix:
                    dve.wait_ge(s.xml_in, 16 * (i + 1))
                    dve.wait_ge(s.q2_done, i + 1)
                    v.tensor_tensor(dcl, xml, bprow, ALU.add).then_inc(s.xpb_done, 1)
                    dve.wait_ge(s.o_ready, i + 1)
                    dve.wait_ge(s.xpb_done, i + 1)
                    ge(dve, s.xm_stored, 16 * i)
                    v.tensor_tensor(xmo, psO, dcl, ALU.add).then_inc(s.xm_done, 1)

            edges(0, 0, True)
            with dve.Fori(1, NT) as i:
                edges(i, i, True)

            def next_window(p):
                v.tensor_scalar(rel, rel, -float(W), None, ALU.add).then_inc(s.win_done, 1)
                v.tensor_scalar(brow[0:1, :], brow[0:1, :], float(W), float(pl.np), ALU.add, ALU.min)\
                    .then_inc(s.win_done, 1)
                dve.wait_ge(s.win_done, 3 * p - 1)
                v.tensor_copy(browi[0:1, :], brow[0:1, 0:pl.groups]).then_inc(s.win_done, 1)
                dve.wait_ge(s.pass_done, 1)
                dve.wait_ge(s.win_done, 3 * p)

            passes(dve, edges, next_window)
            dve.wait_ge(s.xm_stored, 16 * NT)
            v.memset(oh[0], 0.0).then_inc(s.edges_done, 1)

            dve.wait_ge(s.late_in, n_late)
            dve.wait_ge(s.edges_done, 1)

            def bias_stats(t, src_, dst_, row, st, mv, rs, nm, ready, biased, stated, aggr, rstd_, nmr_):
                for n in range(HH):
                    dve.wait_ge(ready, HH * t + n + 1)
                    v.tensor_tensor(dst_[:, n * 512:(n + 1) * 512], src_[:, n, :], row[:, n * 512:(n + 1) * 512],
                                    ALU.add).then_inc(biased, 1)
                    dve.wait_ge(biased, HH * t + n + 1)
                    v.bn_stats(st[:, n, :], dst_[:, n * 512:(n + 1) * 512]).then_inc(stated, 1)
                dve.wait_ge(stated, HH * (t + 1))
                in_own(dve, s.dve_spare)
                v.bn_aggr(mv, st.rearrange("p a b -> p (a b)")).then_inc(nmr_, 1)
                dve.wait_ge(nmr_, 2 * t + 1)
                v.tensor_scalar(mv[:, 1:2], mv[:, 1:2], LN_EPS, None, ALU.add).then_inc(aggr, 1)
                dve.wait_ge(rstd_, t + 1)
                v.scalar_tensor_tensor(nm, mv[:, 0:1], -1.0, rs, ALU.mult, ALU.mult).then_inc(nmr_, 1)

            def body_n(t, do):
                if do[0]:
                    dve.wait_ge(s.hT_ready, t + 1)
                    ge(dve, s.z1_ready, HH * t)
                    v.tensor_tensor(hT.rearrange("p (a b) -> p a b", b=P), pHT.rearrange("p (a b) -> p a b", b=P),
                                    acc[:, 0:CC, ds(t * P, P)], ALU.add).then_inc(s.hT_done, 1)
                    ge(dve, s.t1_ready, t)
                    ge(dve, s.y2_ready, t - 3)
                    bias_stats(t, pA, z1, b1row, st1, mv1, rs1, nm1, s.z1_ready, s.z1_biased, s.z1_stats,
                               s.z1_aggr, s.z1_rstd, s.z1_nmr)
                if do[3]:
                    dve.wait_ge(s.x2T_ready, t - 2)
                    ge(dve, s.f1_ready, t - 3)
                    v.tensor_copy(xn2T, pXT.rearrange("p (a b) -> p a b", b=P)).then_inc(s.xn2T_done, 1)
                if do[1]:
                    if do[2]:
                        dve.wait_ge(s.t2_ready, t - 1)
                    bias_stats(t - 1, pB, z2, b2mrow, st2, mv2, rs2, nm2, s.z2_ready, s.z2_biased, s.z2_stats,
                               s.z2_aggr, s.z2_rstd, s.z2_nmr)
                if do[2]:
                    r = t - 2
                    dve.wait_ge(s.y_ready, r + 1)
                    dve.wait_ge(s.xres_done, r + 1)
                    v.tensor_tensor(u, pY, xres, ALU.add).then_inc(s.u_done, 1)
                    dve.wait_ge(s.u_done, r + 1)
                    v.bn_stats(st3, u).then_inc(s.u_stats, 1)
                    dve.wait_ge(s.u_stats, r + 1)
                    in_own(dve, s.dve_spare)
                    v.bn_aggr(mv3, st3).then_inc(s.u_nmr, 1)
                    dve.wait_ge(s.u_nmr, 2 * r + 1)
                    v.tensor_scalar(mv3[:, 1:2], mv3[:, 1:2], LN_EPS, None, ALU.add).then_inc(s.u_aggr, 1)
                    dve.wait_ge(s.u_rstd, r + 1)
                    v.scalar_tensor_tensor(nm3, mv3[:, 0:1], -1.0, rs3, ALU.mult, ALU.mult).then_inc(s.u_nmr, 1)
                    dve.wait_ge(s.u_nmr, 2 * r + 2)
                    v.tensor_scalar(u, u, rs3, nm3, ALU.mult, ALU.add).then_inc(s.u_norm, 1)
                    dve.wait_ge(s.u_affine, r + 1)
                    dve.wait_ge(s.xmix_in, 16 * (r + 1))
                    v.scalar_tensor_tensor(x2, u, 0.0, xmix, ALU.max, ALU.add).then_inc(s.x2_done, 1)
                    dve.wait_ge(s.x2_done, r + 1)
                    v.bn_stats(st4, x2).then_inc(s.x2_stats, 1)
                    dve.wait_ge(s.x2_stats, r + 1)
                    in_own(dve, s.dve_spare)
                    v.bn_aggr(mv4, st4).then_inc(s.x2_nmr, 1)
                    dve.wait_ge(s.x2_nmr, 2 * r + 1)
                    v.tensor_scalar(mv4[:, 1:2], mv4[:, 1:2], LN_EPS, None, ALU.add).then_inc(s.x2_aggr, 1)
                    dve.wait_ge(s.x2_rstd, r + 1)
                    v.scalar_tensor_tensor(nm4, mv4[:, 0:1], -1.0, rs4, ALU.mult, ALU.mult).then_inc(s.x2_nmr, 1)
                    dve.wait_ge(s.x2_nmr, 2 * r + 2)
                    v.tensor_scalar(xn2, x2, rs4, nm4, ALU.mult, ALU.add).then_inc(s.xn2_done, 1)
                    dve.wait_ge(s.xn2_done, r + 1)
                    v.tensor_tensor(acc[:, 0:CC, ds(r * P, P)], x2.rearrange("p (a b) -> p a b", b=P),
                                    xn2.rearrange("p (a b) -> p a b", b=P), ALU.add).then_inc(s.base_out, 1)
                    v.tensor_tensor_reduce(u, xn2, wrrow, 1.0, 0.0, ALU.mult, ALU.add, wcol).then_inc(s.w_done, 1)
                    dve.wait_ge(s.w_done, r + 1)
                    v.tensor_copy(wr_all[:, ds(r, 1)], wcol).then_inc(s.w_put, 1)
                if do[3]:
                    r = t - 3
                    dve.wait_ge(s.y2_ready, r + 1)
                    v.tensor_tensor(acc[:, CC:2 * CC, ds(r * P, P)], pY2.rearrange("p (a b) -> p a b", b=P),
                                    fb2row.rearrange("p (a b) -> p a b", b=P), ALU.add).then_inc(s.y3_done, 1)

            turns(dve, body_n)

            dve.wait_ge(s.w_put, NT)
            v.tensor_scalar(wv, wr_all[:], brc[:], None, ALU.add).then_inc(s.wv_done, 1)
            dve.wait_ge(s.wv_done, 1)
            v.tensor_tensor(wv, wv, valid[:], ALU.mult).then_inc(s.wv_done, 1)
            dve.wait_ge(s.wv_done, 2)
            v.tensor_tensor(wv, wv, below[:], ALU.add).then_inc(s.wv_done, 1)
            v.memset(pfx, 0).then_inc(s.bit_step, 1)
            dve.wait_ge(s.wv_done, 3)

            def as_float(key, step):
                v.tensor_scalar(t1, key, 31, 0x7FFFFFFF, ALU.arith_shift_right, ALU.bitwise_xor)\
                    .then_inc(s.bit_step, 1)
                dve.wait_ge(s.bit_step, step + 1)
                v.scalar_tensor_tensor(flt, t1, -2 ** 31, key, ALU.bitwise_or, ALU.bitwise_xor)\
                    .then_inc(s.bit_step, 1)
                dve.wait_ge(s.bit_step, step + 2)

            with dve.Fori(0, 32) as i:
                dve.wait_ge(s.bit_step, 6 * i + 1)
                v.tensor_tensor(cand, pfx, bits[:, ds(i, 1)], ALU.bitwise_or).then_inc(s.bit_step, 1)
                dve.wait_ge(s.bit_step, 6 * i + 2)
                as_float(cand, 6 * i + 2)
                v.tensor_scalar(junk, wv, flt.bitcast(f32), None, ALU.is_ge, ALU.add, accum_out=cnt)\
                    .then_inc(s.cnt_done, 1)
                dve.wait_ge(s.cnt_ready, i + 1)
                v.tensor_scalar(m, psCnt, float(KSEL), -1.0, ALU.is_ge, ALU.mult).then_inc(s.bit_step, 1)
                dve.wait_ge(s.bit_step, 6 * i + 5)
                v.tensor_tensor(m, m, bits[:, ds(i, 1)], ALU.bitwise_and).then_inc(s.bit_step, 1)
                dve.wait_ge(s.bit_step, 6 * i + 6)
                v.tensor_tensor(pfx, m, pfx, ALU.bitwise_or).then_inc(s.bit_step, 1)
            dve.wait_ge(s.bit_step, 6 * 32 + 1)
            as_float(pfx, 6 * 32 + 1)
            thr = flt.bitcast(f32)
            v.tensor_scalar(gtm, wv, thr, None, ALU.is_gt, ALU.add, accum_out=cnt).then_inc(s.cnt_done, 1)
            v.tensor_scalar(eqm, wv, thr, None, ALU.is_equal).then_inc(s.eqm2_done, 1)
            dve.wait_ge(s.thr_ready, 1)
            v.tensor_scalar(need, psCnt, -1.0, float(KSEL), ALU.mult, ALU.add).then_inc(s.pick_step, 1)
            dve.wait_ge(s.rank_ready, 1)
            v.tensor_copy(csum, psCol).then_inc(s.pick_step, 1)
            dve.wait_ge(s.pick_step, 2)
            v.tensor_tensor_scan(incl, csum, csum, 0.0, ALU.add, ALU.bypass).then_inc(s.pick_step, 1)
            dve.wait_ge(s.pick_step, 3)
            v.tensor_tensor(incl, incl, csum, ALU.subtract).then_inc(s.pick_step, 1)
            dve.wait_ge(s.pick_step, 4)
            v.tensor_tensor(rank, psRank, incl, ALU.add).then_inc(s.pick_step, 1)
            dve.wait_ge(s.pick_step, 5)
            dve.wait_ge(s.eqm2_done, 1)
            v.scalar_tensor_tensor(rank, rank, need, eqm, ALU.is_lt, ALU.mult).then_inc(s.pick_step, 1)
            dve.wait_ge(s.pick_step, 6)
            dve.wait_ge(s.cnt_done, 33)
            v.tensor_tensor(gtm, gtm, rank, ALU.add).then_inc(s.pick_step, 1)
            dve.wait_ge(s.pick_step, 7)
            v.tensor_tensor(mw, gtm, wv, ALU.mult).then_inc(s.pick_step, 1)
            dve.wait_ge(s.pick_step, 8)
            dve.wait_ge(s.base_out, NT)
            dve.wait_ge(s.y3_done, NT)
            def outputs(b):
                for j in range(BATCH):
                    t = b * BATCH + j
                    ge(dve, s.slab_in[j], LOADED + 16 * b)
                    v.scalar_tensor_tensor(ob[j].rearrange("p (a b) -> p a b", b=P), acc[:, CC:2 * CC, ds(t * P, P)],
                                           mw[:, ds(t, 1)], acc[:, 0:CC, ds(t * P, P)], ALU.mult, ALU.add)\
                        .then_inc(s.ob_done, 1)

            outputs(0)
            with dve.Fori(1, NBATCH) as b:
                outputs(b)


def kernel(**inputs):
    import concourse.bacc as _bacc
    from concourse.bass_utils import run_bass_kernel_spmd as _run

    g = {k[3:] if k.startswith("L0_") else k: np.asarray(v) for k, v in inputs.items()}
    n, e = g["x"].shape[0], g["src"].shape[0]
    pl = plan(n, e)
    ep = pl.tiles * P

    def chunks(w):
        return w.reshape(-1, P, w.shape[1]).transpose(1, 0, 2)

    def column(b):
        return b.reshape(-1, P).T

    dst = np.full(pl.nb * pl.gr * GE * P, n, np.int32)
    dst[:e] = g["dst"]
    src = np.zeros(ep, np.int32)
    src[:e] = g["src"]
    x = np.zeros((pl.np, C), np.float32)
    x[:n] = g["x"]
    ea = np.zeros((ED, ep), np.float32)
    ea[:, :e] = g["edge_attr_64"].T
    arrays = {
        "x": x, "ea": ea, "src": src.reshape(-1, P).T,
        "dst": dst.reshape(pl.nb, pl.gr, GE * P).transpose(1, 0, 2),
        "eps": g["gnn_eps"].reshape(1), "br": g["ffn_br"].reshape(1),
        "ee_w1": g["gnn_ee_w1"], "ee_b1": g["gnn_ee_b1"].reshape(1, -1),
        "ee_b1c": column(g["gnn_ee_b1"]), "ee_w2": chunks(g["gnn_ee_w2"]),
        "ee_b2": g["gnn_ee_b2"], "ee_b2c": column(g["gnn_ee_b2"]),
        "w1": chunks(g["gnn_w1"]), "w2": chunks(g["gnn_w2"]), "w3": chunks(g["gnn_w3"]),
        "b1": g["gnn_b1"], "b2": g["gnn_b2"], "b3": g["gnn_b3"],
        "g1": column(g["gnn_g1"]), "be1": column(g["gnn_be1"]),
        "g2": column(g["gnn_g2"]), "be2": column(g["gnn_be2"]),
        "bn_g": g["gnn_bn_g"], "bn_b": g["gnn_bn_b"],
        "wq": chunks(g["mix_Wq"].T), "wkv": chunks(g["mix_Wkv"].T), "wproj": chunks(g["mix_Wproj"].T),
        "bproj": g["mix_bproj"], "wr": g["ffn_wr"].reshape(-1),
        "fw1": chunks(g["ffn_w1"]), "fb1": column(g["ffn_b1"]),
        "fw2": chunks(g["ffn_w2"]), "fb2": g["ffn_b2"],
        "bits": np.tile((np.uint32(1) << np.arange(31, -1, -1).astype(np.uint32)).view(np.int32), (P, 1)),
        **constants(pl),
    }
    arrays = {k: np.ascontiguousarray(v) for k, v in arrays.items()}
    nc = _bacc.Bacc("TRN2", target_bir_lowering=False, num_devices=1)
    aps = namedtuple("Inputs", arrays)(**{
        k: nc.dram_tensor(f"in_{k}", v.shape, mybir.dt.from_np(v.dtype), kind="ExternalInput").ap()
        for k, v in arrays.items()})
    out = nc.dram_tensor("out_0", (pl.np, C), mybir.dt.float32, kind="ExternalOutput").ap()
    gps_kernel(nc, aps, out, pl)
    r = _run(nc, [{f"in_{k}": v for k, v in arrays.items()}], core_ids=[0])
    return r.results[0]["out_0"][:n]
```

```python
from collections import namedtuple
from contextlib import ExitStack

import numpy as np
import concourse.bass as bass
from concourse import mybir

P = 128
C = 256
CC = C // P
W = 128
GE = 4
PE2 = 2
WS = 256.0
HS = 1.0 / 32
TERMS = ((0, 0), (0, 1), (1, 0))
HEADS = 8
ED = 64
LN_EPS = 1e-5
CAPACITY = 0.5


Plan = namedtuple("Plan", "n nt np gpt groups tiles nb gr batch wid wcols wchunk")


def plan(n_nodes, n_edges, hidden):
    nt = -(-n_nodes // P)
    gpt = -(-n_edges // (GE * P * nt))
    gpt += gpt % 2
    groups = nt * gpt
    nb = -(-groups // P)
    gr = -(-groups // nb)
    batch = max(b for b in range(1, 9) if nt % b == 0 and nt > b)
    wcols = (2 * hidden // P) * C + (hidden // P) * hidden + 2 * (hidden // P) * C + hidden
    wchunk = -(-wcols // (2 * nt)) * 2
    return Plan(n=n_nodes, nt=nt, np=nt * P, gpt=gpt, groups=groups, tiles=groups * GE,
                nb=nb, gr=gr, batch=batch, wid=nt * P + W, wcols=wcols, wchunk=wchunk)


def constants(pl):
    i = np.arange(P)
    valid = (np.arange(pl.nt)[None, :] * P + i[:, None] < pl.n).astype(np.float32)
    return {
        "ident": np.eye(P, dtype=np.float32),
        "ones": np.ones((P, P), np.float32),
        "before": (i[:, None] < i[None, :]).astype(np.float32),
        "head": (i[:, None] // (C // HEADS) == i[None, :] // (C // HEADS)).astype(np.float32),
        "iota": np.tile(np.arange(W, dtype=np.float32), (P, 1)),
        "valid": valid,
        "below": (valid - 1.0) * np.float32(3e38),
        "expo": np.full((P, pl.nt), -0.5, np.float32),
    }


def ge(eng, sem, value):
    if isinstance(value, int) and value <= 0:
        return
    eng.wait_ge(sem, value)


def in_own(eng, spare):
    eng.sem_inc(spare, 1)


def in_pairs(eng, first, last, body):
    pairs = max(last - first, 0) // 2
    if pairs:
        with eng.Fori(0, pairs) as h:
            body(2 * h + first, h + first // 2, first % 2)
            body(2 * h + first + 1, h + (first + 1) // 2, (first + 1) % 2)
    for t in range(first + 2 * pairs, last):
        body(t, t // 2, t % 2)


def gps_kernel(nc, A, out, pl):
    f32, f16, i32 = mybir.dt.float32, mybir.dt.float16, mybir.dt.int32
    ALU, ACT, AX = mybir.AluOpType, mybir.ActivationFunctionType, mybir.AxisListType
    ds = bass.ds
    NT, GPT, TPB, PPB = pl.nt, pl.gpt, pl.gpt * GE, pl.gpt * GE // PE2
    WC = pl.wchunk
    BATCH, NBATCH = pl.batch, pl.nt // pl.batch
    H = A.g1.shape[1] * P
    HC, HH = H // P, H // 512
    HALF = GPT // 2
    KSEL = max(1, int(CAPACITY * pl.n))
    KSEL = KSEL - 1 if KSEL > 1 else 1

    x_rows = A.x.rearrange("(t p) c -> t p c", p=P)
    xn_d = nc.dram_tensor("xn_rows", (NT, P, C), f32, kind="Internal").ap()
    xm_d = nc.dram_tensor("mix_rows", (NT, P, C), f32, kind="Internal").ap()
    table = nc.dram_tensor("gather_table", (pl.np, 2 * C), f16, kind="Internal").ap()
    table_rows = table.rearrange("(t p) c -> t p c", p=P)
    wsplit = nc.dram_tensor("split_weights", (P, 2, NT * WC), f16, kind="Internal").ap()
    out_rows = out.rearrange("(t p) c -> t p c", p=P)

    ctx = ExitStack()
    with ctx:
        def sb(name, shape, dt=f32):
            return ctx.enter_context(nc.sbuf_tensor(name, shape, dt))

        def sem(name):
            return ctx.enter_context(nc.semaphore(name))

        acc = sb("acc", [P, 4, pl.wid])
        ident = sb("ident", [P, P])
        valid = sb("valid", [P, NT])
        below = sb("below", [P, NT])
        ee2 = sb("ee2", [P, CC, C])
        wr_all = sb("wr_all", [P, NT])
        epscol = sb("epscol", [P, 1])
        g1c, be1c, g2c, be2c, fb1c = [sb(n, [P, HC]) for n in ("g1c", "be1c", "g2c", "be2c", "fb1c")]
        bits = sb("bits", [P, 32], i32)
        brc = sb("brc", [P, 1])

        class Carver:
            def __init__(self, base):
                self.base, self.at = base, 0

            def __call__(self, *shape, dt=f32):
                n = int(np.prod(shape))
                words = n if dt in (f32, i32) else -(-n // 2)
                ap = self.base[:, self.at:self.at + words]
                self.at += words
                assert self.at <= self.base.shape[1], (self.at, self.base.shape)
                if dt is not f32:
                    ap = ap.bitcast(dt)
                if len(shape) == 2:
                    ap = ap.rearrange("p (a b) -> p a b", b=shape[1])
                if len(shape) == 3:
                    ap = ap.rearrange("p (a b c) -> p a b c", b=shape[1], c=shape[2])
                return ap

        big = sb("big", [P, max(CC * pl.np, 12544)])
        qT = Carver(big)(CC, pl.np)
        wts = Carver(big)
        w1, w2, w3 = wts(2, CC * H, dt=f16), wts(2, HC * H, dt=f16), wts(2, HC * C, dt=f16)
        ones, before = wts(P), wts(P)

        arena = sb("arena", [P, max(14144, 11800 + 2 * WC)])
        a = Carver(arena)
        early = Carver(big)
        slab, dsti = early(BATCH, C), early(pl.nb, GE * P, dt=i32)
        wqf, wkvf, stats = early(CC * C), early(CC * 2 * C), early(NT, 6)
        xs, xn, ek, eq, ks, vs = [[a(C) for _ in range(2)] for _ in range(6)]
        xt = [a(2, C, dt=f16) for _ in range(2)]
        tab = [a(2 * C, dt=f16) for _ in range(2)]
        xb, b2row = a(C), a(C)
        wproj = a(CC, C)
        wq, wkv = a(2, CC * C, dt=f16), a(2, CC * 2 * C, dt=f16)
        ctm = a(CC, P)
        mean, var, tmp = a(NT), a(NT), a(NT)
        rstd, nmr, expo = a(NT), a(NT), a(NT)
        span = a(4)
        bases, spans = a(pl.nb), a(pl.nb)
        b2c, twoeps, b1h = a(CC), a(1), a(CC)
        front_end = a.at

        a = Carver(arena)
        xg = a(TPB, 2 * C, dt=f16)
        ea = a(GPT, GE * P)
        hm = [a(2, PE2 * C, dt=f16) for _ in range(4)]
        oh = [a(GE, W, dt=f16) for _ in range(2)]
        dcl, q2, xml, xmo = a(C), a(C), a(C), a(C)
        idx = a(TPB, dt=i32)
        wst, wsp = a(WC), a(2, WC, dt=f16)
        a.at = max(a.at, front_end)
        mixw, ksb, ee1, iota, bprow, head = a(CC, C), a(CC, P), a(C), a(W), a(C), a(P)
        src, rel = a(pl.tiles, dt=i32), a(pl.tiles)
        brow = a(pl.nb * pl.gr)
        browi, npass = a(pl.groups, dt=i32), a(2, dt=i32)

        a = Carver(arena)
        fw1, fw2 = a(2, CC * H, dt=f16), a(2, HC * C, dt=f16)
        bias2, bones = a(H, dt=f16), a(P, dt=f16)
        b3row, bngrow, bnbrow, fb2row, wrrow = [a(C) for _ in range(5)]
        z1, z2, gf = a(H), a(H), a(H)
        z1T, z2T, gfT = (z.rearrange("p (a b) -> p a b", b=P) for z in (z1, z2, gf))
        aT1, aT2, gT = [a(2, H, dt=f16) for _ in range(3)]
        hTs, xn2T = a(2, C, dt=f16), a(2, C, dt=f16)
        hTs3 = [hTs[:, k, :].rearrange("p (a b) -> p a b", b=P) for k in range(2)]
        hT = acc[:, 0:CC, pl.np:pl.np + P]
        u, x2, xn2, xres, xmix = [a(C) for _ in range(5)]
        st1, st2, st3, st4 = a(2, 6), a(2, 6), a(6), a(6)
        mv1, mv2, mv3, mv4 = [a(2) for _ in range(4)]
        rs1, rs2, rs3, rs4, nm1, nm2, nm3, nm4, mh, wcol = [a(1) for _ in range(10)]
        a = Carver(arena)
        ob = [a(C) for _ in range(BATCH)]
        wv, gtm, eqm, csum, incl, rank, mw, junk = [a(NT) for _ in range(8)]
        pfx, cand, t1, flt, m = [a(1, dt=i32) for _ in range(5)]
        cnt, need = a(1), a(1)

        ps = ctx.enter_context(nc.psum_tensor("ps", [P, 8, 512], f32))
        psT = [ps[:, b, 0:C] for b in (0, 7)]
        psKV = [ps[:, 1 + s, :] for s in range(2)]
        psQ = [ps[:, b, 0:C] for b in (3, 6)]
        psX = ps[:, 4, 0:C + CC]
        psR = [ps[:, 5, :], ps[:, 6, :]]
        psM = ps[:, 5, :]
        psH = [ps[:, s, :] for s in range(2)]
        psS = [ps[:, 2 + s, :] for s in range(2)]
        psD, psO = ps[:, 4, 0:C], ps[:, 5, 0:C]
        pA, pB, pC = ps[:, 0:2, :], ps[:, 2:4, :], ps[:, 4:6, :]
        pHT, pXT = ps[:, 6, 0:C], ps[:, 6, C:2 * C]
        pY, pY2 = ps[:, 7, 0:C], ps[:, 2, 0:C]
        psCnt = ps[:, 0, 0:1]
        psRank, psCol = ps[:, 1, 0:NT], ps[:, 2, 0:NT]

        names = """const_in stats_done mean_done var_done rstd_done nmr_done dst_in dstf_done base_done
          rel_done relT_ready relT_done brow_ready brow_done browi_done span_done pass_done
          twoeps_done relu_b1_done acc_zero xn_done xT_ready xt_done xT_used kv_ready
          ek_done em_done k_done v_done q_ready eq_done eqm_done q_done ctx_done xb_done hi16_done
          tab_done ctm_done ksb_done m_ready mh_done ob_done front_done ea_ones idx_done
          hid_done hi_done lo_done oh_done scat_done ev_done d_ready dcl_done rcp_done q2_done
          o_ready xpb_done xm_done win_done edges_done wts_in late_in hT_ready hT_done z1_ready
          z1_stats z1_aggr z1_rstd z1_nmr z1_done t1_ready a1_done z2_ready           z2_stats z2_aggr z2_rstd z2_nmr z2_done t2_ready a2_done y_ready xres_done u_done
          u_stats u_aggr u_rstd u_nmr u_norm u_affine x2_done x2_stats x2_aggr x2_rstd
          x2_nmr xn2_done base_out w_done x2T_ready xn2T_done f1_ready g_done y2_ready
          y3_done wv_done cnt_done cnt_ready thr_ready eqm2_done rank_ready bit_step pick_step pool_spare dve_spare""".split()
        sems = {n: sem(n) for n in names + ["xml_in", "xm_stored", "xres_in", "xmix_in", "ws_in", "ws_stored", "wq_hi", "wq_split",
                                     "ws_hi", "ws_lo", "xt_hi", "hT_hi", "hT_split", "xn2T_hi",
                                     "a1_hi", "a1_split", "a2_hi", "a2_split", "g_hi", "g_split"]}
        for n, count in (("slab_in", BATCH), ("x_in", 2), ("xn_stored", 2), ("tab_stored", 2),
                         ("ea_in", GPT), ("xg_in", GPT)):
            sems[n] = [sem(f"{n}{j}") for j in range(count)]
        s = namedtuple("Semaphores", sems)(**sems)
        LOADED = 16 * NBATCH

        resident_loads = [(ident, A.ident), (valid, A.valid),
                          (below, A.below), (ee2, A.ee_w2), (g1c, A.g1), (be1c, A.be1),
                          (g2c, A.g2), (be2c, A.be2), (fb1c, A.fb1), (bits, A.bits)]
        front_loads = [(wqf, A.wq), (wkvf, A.wkv), (wproj, A.wproj), (expo, A.expo), (b2c, A.ee_b2c),
                       (b1h, A.ee_b1c), (ee1[0:ED, :], A.ee_w1), (ee1[ED:ED + 1, :], A.ee_b1),
                       (iota, A.iota), (head, A.head), (src, A.src)]
        front_rows = [(epscol, A.eps), (brc, A.br), (b2row, A.ee_b2), (bprow, A.bproj)]
        at, splits = 0, []
        for dst_, cols in ((w1, CC * H), (w2, HC * H), (w3, HC * C), (fw1, CC * H), (fw2, HC * C)):
            splits.append((dst_, wsplit[:, :, at:at + cols]))
            at += cols
        splits += [(bias2[32 * k:32 * k + 2, :], wsplit[k, :, at:at + H]) for k in range(2)]
        assert at + H == pl.wcols
        big_loads = splits[:3] + [(ones, A.ones), (before, A.before)]
        late_loads = splits[3:]
        late_rows = [(b3row, A.b3), (bngrow, A.bn_g),
                     (bnbrow, A.bn_b), (fb2row, A.fb2), (wrrow, A.wr)]
        n_const = 16 * (len(resident_loads) + len(front_loads) + len(front_rows))
        n_late = 16 * (len(late_loads) + len(late_rows))

        def passes(eng, edge_body, between=None):
            eng.wait_ge(s.pass_done, 1)
            n = eng.value_load(npass[0:1, 0:1], min_val=1, max_val=2 + pl.np // W)
            with eng.If(n > 1):
                with eng.Fori(1, n) as p:
                    if between is not None:
                        between(p)
                    with eng.Fori(0, NT) as i:
                        edge_body(i, p * NT + i)

        def turns(eng, body):
            for t in range(4):
                body(t, [0 <= t - k < NT for k in (0, 1, 2, 3, -1)])
            with eng.Fori(4, NT - 1) as t:
                body(t, [True] * 5)
            for t in range(NT - 1, NT + 3):
                body(t, [0 <= t - k < NT for k in (0, 1, 2, 3, -1)])

        block = ctx.enter_context(nc.Block())

        @block.sync
        def _(sp):
            for j in range(BATCH):
                sp.dma_start(slab[:, j, :], x_rows[j]).then_inc(s.slab_in[j], 16)
            sp.dma_start(dsti[0:pl.gr, :, :], A.dst).then_inc(s.dst_in, 16)
            for dst_, src_ in resident_loads + front_loads:
                sp.dma_start(dst_[:], src_).then_inc(s.const_in, 16)
            for dst_, src_ in front_rows:
                sp.dma_start(dst_[:], src_.partition_broadcast(P)).then_inc(s.const_in, 16)
            with sp.Fori(1, NBATCH) as b:
                for j in range(BATCH):
                    sp.wait_ge(s.stats_done, (b - 1) * BATCH + j + 1)
                    sp.dma_start(slab[:, j, :], x_rows[b * BATCH + j]).then_inc(s.slab_in[j], 16)

            def load(t, sl):
                ge(sp, s.xn_done, t - 1)
                sp.dma_start(xs[sl], x_rows[t]).then_inc(s.x_in[sl], 16)

            def store(t, sl):
                sp.wait_ge(s.xn_done, t + 1)
                sp.dma_start(xn_d[t], xn[sl]).then_inc(s.xn_stored[sl], 16)
                sp.wait_ge(s.tab_done, t + 1)
                sp.dma_start(table_rows[t], tab[sl]).then_inc(s.tab_stored[sl], 16)

            def body(t, h, sl):
                load(t + 1, 1 - sl)
                store(t, sl)

            load(0, 0)
            body(0, 0, 0)
            body(1, 0, 1)
            in_pairs(sp, 2, NT - 1, body)
            store(NT - 1, (NT - 1) % 2)

            sp.wait_ge(s.front_done, 1)

            def edges(i, q):
                for j in range(GPT):
                    ge(sp, s.hid_done, (q - 1) * PPB + (j + 1) * GE // PE2)
                    sp.dma_start(ea[0:ED, j, :], A.ea[:, ds((i * GPT + j) * GE * P, GE * P)])\
                        .then_inc(s.ea_in[j], 16)

            def load_weights(i):
                ge(sp, s.ws_lo, i)
                sp.dma_start(wst, A.wall[:, ds(i * WC, WC)]).then_inc(s.ws_in, 16)

            def store_weights(i):
                sp.wait_ge(s.ws_lo, i + 1)
                sp.dma_start(wsplit[:, :, ds(i * WC, WC)], wsp).then_inc(s.ws_stored, 16)

            load_weights(0)
            edges(0, 0)
            with sp.Fori(1, NT) as i:
                store_weights(i - 1)
                load_weights(i)
                edges(i, i)
            store_weights(NT - 1)
            passes(sp, edges)

            sp.wait_ge(s.q2_done, NT)
            sp.wait_ge(s.ws_stored, 16 * NT)
            for dst_, src_ in big_loads:
                sp.dma_start(dst_[:], src_).then_inc(s.wts_in, 16)
            sp.wait_ge(s.edges_done, 1)
            sp.wait_ge(s.xm_stored, 16 * NT)
            for dst_, src_ in late_loads:
                sp.dma_start(dst_[:], src_).then_inc(s.late_in, 16)
            for dst_, src_ in late_rows:
                sp.dma_start(dst_[:], src_.partition_broadcast(P)).then_inc(s.late_in, 16)

            def rows(t):
                ge(sp, s.u_done, t)
                sp.dma_start(xres, xn_d[t]).then_inc(s.xres_in, 16)
                ge(sp, s.x2_done, t)
                sp.dma_start(xmix, xm_d[t]).then_inc(s.xmix_in, 16)

            rows(0)
            with sp.Fori(1, NT) as t:
                rows(t)

            with sp.Fori(0, NBATCH) as b:
                for j in range(BATCH):
                    sp.wait_ge(s.ob_done, b * BATCH + j + 1)
                    sp.dma_start(out_rows[b * BATCH + j], ob[j]).then_inc(s.slab_in[j], 16)
            for j in range(BATCH):
                sp.wait_ge(s.slab_in[j], LOADED + 16 * NBATCH)

        @block.gpsimd
        def _(pool):
            g = nc.gpsimd
            pool.wait_ge(s.const_in, n_const)
            pool.wait_ge(s.var_done, 1)
            g.tensor_tensor(rstd, var, expo, ALU.pow).then_inc(s.rstd_done, 1)

            def tables(t, h, sl):
                pool.wait_ge(s.xn_done, t + 1)
                ge(pool, s.tab_done, t)
                g.tensor_tensor(xb, xn[sl], b2row, ALU.add).then_inc(s.xb_done, 1)
                ge(pool, s.tab_stored[sl], 16 * h)
                pool.wait_ge(s.xb_done, t + 1)
                in_own(pool, s.pool_spare)
                g.tensor_copy(tab[sl][:, 0:C], xb).then_inc(s.hi16_done, 1)
                pool.wait_ge(s.hi16_done, t + 1)
                g.tensor_tensor(tab[sl][:, C:2 * C], xb, tab[sl][:, 0:C], ALU.subtract)\
                    .then_inc(s.tab_done, 1)

            tables(0, 0, 0)
            tables(1, 0, 1)
            in_pairs(pool, 2, NT, tables)

            pool.wait_ge(s.front_done, 1)
            for sl in range(2):
                pool.wait_ge(s.tab_stored[sl], 16 * ((NT + 1 - sl) // 2))
            g.memset(ea[ED:ED + 1, :, :], 1.0).then_inc(s.ea_ones, 1)
            pool.wait_ge(s.ea_ones, 1)

            def edges(i, q):
                for half in range(GPT // HALF):
                    ge(pool, s.scat_done, (q - 1) * GPT + (half + 1) * HALF)
                    in_own(pool, s.pool_spare)
                    at = slice(half * HALF * GE, (half + 1) * HALF * GE)
                    g.tensor_copy(idx[:, at], src[:, ds(i * TPB + half * HALF * GE, HALF * GE)])\
                        .then_inc(s.idx_done, 1)
                    pool.wait_ge(s.idx_done, q * (GPT // HALF) + half + 1)
                    in_own(pool, s.pool_spare)
                    for j in range(half * HALF * GE, (half + 1) * HALF * GE):
                        g.indirect_dma_start(
                            xg[:, j, :], None, table,
                            bass.IndirectOffsetOnAxis(idx[:, j:j + 1].bitcast(mybir.dt.uint32), 0))\
                            .then_inc(s.xg_in[j // GE], 16)

            edges(0, 0)
            with pool.Fori(1, NT) as i:
                edges(i, i)
            passes(pool, edges)

            pool.wait_ge(s.late_in, n_late)

            def power(mv, rs, ready, done, t):
                pool.wait_ge(ready, t + 1)
                g.tensor_tensor(rs, mv[:, 1:2], mh, ALU.pow).then_inc(done, 1)

            g.memset(mh, -0.5).then_inc(s.mh_done, 1)
            g.memset(bones[0:2, :], HS).then_inc(s.mh_done, 1)
            pool.wait_ge(s.mh_done, 2)
            g.memset(bones[32:34, :], 1.0).then_inc(s.mh_done, 1)
            pool.wait_ge(s.mh_done, 3)

            def body(t, do):
                if do[0]:
                    power(mv1, rs1, s.z1_aggr, s.z1_rstd, t)
                if do[1]:
                    power(mv2, rs2, s.z2_aggr, s.z2_rstd, t - 1)
                if do[2]:
                    r = t - 2
                    pool.wait_ge(s.xres_in, 16 * (r + 1))
                    g.tensor_tensor(xres, xres, b3row, ALU.add).then_inc(s.xres_done, 1)
                    power(mv3, rs3, s.u_aggr, s.u_rstd, r)
                    pool.wait_ge(s.u_norm, r + 1)
                    g.tensor_tensor(u, u, bngrow, ALU.mult).then_inc(s.u_affine, 1)
                    pool.wait_ge(s.u_affine, 2 * r + 1)
                    g.tensor_tensor(u, u, bnbrow, ALU.add).then_inc(s.u_affine, 1)
                    power(mv4, rs4, s.x2_aggr, s.x2_rstd, r)

            turns(pool, body)

        @block.scalar
        def _(act):
            a_ = nc.scalar
            act.wait_ge(s.const_in, n_const)
            for c in range(CC):
                a_.activation(b1h[:, c:c + 1], b1h[:, c:c + 1], ACT.Relu).then_inc(s.relu_b1_done, 1)
            for part, full in ((wq[:, 0, :], wqf), (wkv[:, 0, :], wkvf)):
                a_.activation(part, full, ACT.Copy, scale=WS).then_inc(s.wq_hi, 1)
            act.wait_ge(s.nmr_done, 1)

            def normalize(t, h, sl):
                act.wait_ge(s.x_in[sl], 16 * (h + 1))
                ge(act, s.xT_ready, t - 1)
                ge(act, s.tab_done, t - 1)
                ge(act, s.xn_stored[sl], 16 * h)
                a_.activation(xn[sl], xs[sl], ACT.Identity, bias=nmr[:, ds(t, 1)],
                              scale=rstd[:, ds(t, 1)]).then_inc(s.xn_done, 1)

            def exps(t, sl):
                act.wait_ge(s.kv_ready, t + 1)
                ge(act, s.k_done, t - 1)
                a_.activation(ek[sl], psKV[sl][:, 0:C], ACT.Exp, scale=1 / WS).then_inc(s.ek_done, 1)
                ge(act, s.ctx_done, t - 1)
                a_.activation(vs[sl], psKV[sl][:, C:2 * C], ACT.Copy, scale=1 / WS).then_inc(s.v_done, 1)
                act.wait_ge(s.q_ready, t + 1)
                ge(act, s.q_done, t - 1)
                a_.activation(eq[sl], psQ[sl], ACT.Exp, scale=1 / WS).then_inc(s.eq_done, 1)

            def body(t, h, sl):
                normalize(t + 1, h + sl, 1 - sl)
                exps(t, sl)

            normalize(0, 0, 0)
            body(0, 0, 0)
            body(1, 0, 1)
            in_pairs(act, 2, NT - 1, body)
            exps(NT - 1, (NT - 1) % 2)

            act.wait_ge(s.front_done, 1)

            def load_mix(i):
                ge(act, s.xpb_done, i)
                act.dma_start(xml, x_rows[i]).then_inc(s.xml_in, 16)

            def store_mix(i):
                act.wait_ge(s.xm_done, i + 1)
                act.dma_start(xm_d[i], xmo).then_inc(s.xm_stored, 16)

            def edges(i, q, mix=None):
                for j in range(PPB):
                    n = q * PPB + j
                    if mix is not None and j == 1:
                        mix(i)
                        act.wait_ge(s.ws_in, 16 * (i + 1))
                        ge(act, s.ws_stored, 16 * i)
                        a_.activation(wsp[:, 0, :], wst, ACT.Copy, scale=WS).then_inc(s.ws_hi, 1)
                    act.wait_ge(s.hid_done, n + 1)
                    ge(act, s.scat_done, q * GPT + j // 2 - 1)
                    a_.activation(hm[j % 4][:, 0, :], psH[j % 2], ACT.Relu).then_inc(s.hi_done, 1)

            def move_mix(i):
                store_mix(i - 1)
                load_mix(i)

            edges(0, 0, load_mix)
            with act.Fori(1, NT) as i:
                edges(i, i, move_mix)
            store_mix(NT - 1)
            passes(act, edges)

            act.wait_ge(s.late_in, n_late)

            def affine(dst_, src_, gcol, bcol, done, func=ACT.Relu):
                for j in range(HC):
                    a_.activation(dst_[:, j, :], src_[:, j // 4, (j % 4) * P:(j % 4 + 1) * P], func,
                                  bias=bcol[:, j:j + 1], scale=1 / WS if gcol is None else gcol[:, j:j + 1])\
                        .then_inc(done, 1)

            def body_n(t, do):
                if do[2]:
                    act.wait_ge(s.t2_ready, t - 1)
                    affine(z2T, pC, g2c, be2c, s.a2_done)
                if do[0]:
                    act.wait_ge(s.z1_nmr, 2 * (t + 1))
                    ge(act, s.a1_split, t)
                    a_.activation(z1.rearrange("p (a b) -> p a b", b=512), pA, ACT.Identity, bias=nm1, scale=rs1).then_inc(s.z1_done, 1)
                if do[3]:
                    act.wait_ge(s.f1_ready, t - 2)
                    ge(act, s.g_split, t - 3)
                    affine(gfT, pA, None, fb1c, s.g_done, ACT.Gelu_apprx_tanh)
                if do[0]:
                    act.wait_ge(s.t1_ready, t + 1)
                    affine(z1T, pC, g1c, be1c, s.a1_done)
                if do[1]:
                    act.wait_ge(s.z2_nmr, 2 * t)
                    ge(act, s.a2_split, t - 1)
                    a_.activation(z2.rearrange("p (a b) -> p a b", b=512), pB, ACT.Identity, bias=nm2, scale=rs2).then_inc(s.z2_done, 1)

            turns(act, body_n)

        @block.tensor
        def _(pe):
            mm = nc.tensor.matmul
            pe.wait_ge(s.const_in, n_const)
            pe.wait_ge(s.rel_done, pl.nb)
            pe.wait_ge(s.span_done, 1)
            for b in range(pl.nb):
                for h in range(GE):
                    n = b * GE + h
                    ge(pe, s.relT_done, n - 1)
                    nc.tensor.transpose(psR[n % 2][:, 0:pl.gr], dsti.bitcast(f32)[0:pl.gr, b, h * P:(h + 1) * P],
                                        ident[0:pl.gr, 0:pl.gr]).then_inc(s.relT_ready, 1)
            pe.wait_ge(s.relT_done, pl.nb * GE)
            for b in range(pl.nb):
                for k in range(2):
                    last = mm(psR[k][0:1, b * pl.gr:(b + 1) * pl.gr], (bases, spans)[k][0:pl.gr, b:b + 1],
                              ident[0:pl.gr, 0:pl.gr], start=True, stop=True)
            last.then_inc(s.brow_ready, 1)
            pe.wait_ge(s.brow_done, 2)

            def transposes(t, sl):
                pe.wait_ge(s.xn_done, t + 1)
                ge(pe, s.xt_done, t - 1)
                ge(pe, s.xT_used, CC * (t - 1))
                for c in range(CC):
                    i_ = nc.tensor.transpose(psT[sl][:, c * P:(c + 1) * P], xn[sl][:, c * P:(c + 1) * P], ident[:])
                i_.then_inc(s.xT_ready, 1)

            def project(t, sl):
                pe.wait_ge(s.xt_done, t + 1)
                ge(pe, s.v_done, t - 1)
                ge(pe, s.k_done, t - 1)
                for c in range(CC):
                    for a_, b_ in TERMS:
                        i_ = mm(psKV[sl], xt[sl][:, a_, c * P:(c + 1) * P],
                                wkv[:, b_, c * 2 * C:(c + 1) * 2 * C],
                                start=c == 0 and a_ + b_ == 0, stop=c == CC - 1 and (a_, b_) == TERMS[-1])
                i_.then_inc(s.kv_ready, 1)
                ge(pe, s.q_done, t - 1)
                for o in range(CC):
                    for c in range(CC):
                        for a_, b_ in TERMS:
                            i_ = mm(psQ[sl][:, o * P:(o + 1) * P], wq[:, a_, c * C + o * P:c * C + (o + 1) * P],
                                    xt[sl][:, b_, c * P:(c + 1) * P],
                                    start=c == 0 and a_ + b_ == 0, stop=c == CC - 1 and (a_, b_) == TERMS[-1])
                i_.then_inc(s.q_ready, 1)

            def context(t, sl, first=False, last=False):
                pe.wait_ge(s.k_done, t + 1)
                pe.wait_ge(s.v_done, t + 1)
                for c in range(CC):
                    half = slice(c * P, (c + 1) * P)
                    mm(psX[:, half], vs[sl][:, half], ks[sl][:, half], start=first and c == 0,
                       stop=False, skip_group_check=True)
                for c in range(CC):
                    i_ = mm(psX[:, C + c:C + c + 1], ks[sl][:, c * P:(c + 1) * P], valid[:, ds(t, 1)],
                            start=False, stop=last and c == CC - 1, skip_group_check=True)
                i_.then_inc(s.ctx_done, 1)

            transposes(0, 0)
            transposes(1, 1)
            pe.wait_ge(s.wq_split, 2)
            project(0, 0)

            def body(t, h, sl):
                transposes(t + 1, 1 - sl)
                project(t, sl)
                context(t - 1, 1 - sl)

            transposes(2, 0)
            project(1, 1)
            context(0, 0, first=True)

            in_pairs(pe, 2, NT - 1, body)
            project(NT - 1, (NT - 1) % 2)
            context(NT - 2, (NT - 2) % 2)
            context(NT - 1, (NT - 1) % 2, last=True)

            pe.wait_ge(s.ctm_done, CC)
            for c in range(CC):
                i_ = mm(psM[:, c * C:(c + 1) * C], ctm[:, c, :], wproj[:, c, :], start=True, stop=True)
            i_.then_inc(s.m_ready, 1)
            pe.wait_ge(s.front_done, 1)
            pe.wait_ge(s.ea_ones, 1)

            def hidden(j, q):
                n = q * PPB + j
                group, at = j // (GE // PE2), j % (GE // PE2) * PE2 * P
                pe.wait_ge(s.ea_in[group], 16 * (q + 1))
                ge(pe, s.lo_done, n - 1)
                for e in range(PE2):
                    i_ = mm(psH[j % 2][:, e * C:(e + 1) * C], ea[0:ED + 1, group, at + e * P:at + (e + 1) * P],
                            ee1[0:ED + 1, :], start=True, stop=True)
                i_.then_inc(s.hid_done, 1)

            def scatter(j, q):
                n = q * GPT + j
                pe.wait_ge(s.xg_in[j], 16 * GE * (q + 1))
                pe.wait_ge(s.lo_done, (n + 1) * GE // PE2)
                pe.wait_ge(s.oh_done, n + 1)
                ge(pe, s.ev_done, n - 1)
                for c in range(2 * CC):
                    for e in range(GE):
                        for part in range(2):
                            if c < CC:
                                rows = xg[:, j * GE + e, part * C + c * P:part * C + (c + 1) * P]
                            else:
                                at = e % PE2 * C + (c - CC) * P
                                rows = hm[(2 * j + e // PE2) % 4][:, part, at:at + P]
                            i_ = mm(psS[j % 2][:, c * W:(c + 1) * W], rows, oh[j % 2][:, e, :],
                                    start=e == 0 and part == 0, stop=e == GE - 1 and part == 1)
                i_.then_inc(s.scat_done, 1)

            def denominators(i):
                ge(pe, s.rcp_done, i)
                for c in range(CC):
                    i_ = mm(psD[:, c * P:(c + 1) * P], ksb[:, c, :], qT[:, c, ds(i * P, P)],
                            start=True, stop=True)
                i_.then_inc(s.d_ready, 1)

            def attention(i):
                pe.wait_ge(s.q2_done, i + 1)
                ge(pe, s.xm_done, i)
                for c in range(CC):
                    i_ = mm(psO, q2[:, c * P:(c + 1) * P], mixw[:, c, :], start=c == 0, stop=c == CC - 1)
                i_.then_inc(s.o_ready, 1)

            def edges(i, q, mix=False):
                hidden(0, q)
                hidden(1, q)
                if mix:
                    denominators(i)
                for j in range(1, GPT):
                    hidden(2 * j, q)
                    hidden(2 * j + 1, q)
                    scatter(j - 1, q)
                if mix:
                    attention(i)
                scatter(GPT - 1, q)

            edges(0, 0, True)
            with pe.Fori(1, NT) as i:
                edges(i, i, True)
            passes(pe, edges)

            pe.wait_ge(s.edges_done, 1)
            pe.wait_ge(s.wts_in, 16 * len(big_loads))
            pe.wait_ge(s.late_in, n_late)
            pe.wait_ge(s.mh_done, 3)

            def node_sums(t):
                ge(pe, s.hT_done, t)
                for o in range(CC):
                    for c in range(CC):
                        i_ = mm(pHT[:, o * P:(o + 1) * P], ee2[:, c, o * P:(o + 1) * P],
                                acc[:, CC + c, ds(t * P, P)], start=c == 0, stop=c == CC - 1)
                i_.then_inc(s.hT_ready, 1)

            def bias(rows, layer, n):
                at = slice(32 * layer, 32 * layer + 2)
                mm(rows, bones[at, :], bias2[at, n * 512:(n + 1) * 512], start=True, stop=False)

            def layer2(t, n):
                bias(pB[:, n, :], 1, n)
                for k in range(HC):
                    for a_, b_ in TERMS:
                        i_ = mm(pB[:, n, :], aT1[:, a_, k * P:(k + 1) * P],
                                w2[:, b_, k * H + n * 512:k * H + (n + 1) * 512],
                                start=False, stop=k == HC - 1 and (a_, b_) == TERMS[-1])
                i_.then_inc(s.z2_ready, 1)

            def body_n(t, do):
                if do[0]:
                    pe.wait_ge(s.hT_split, t + 1)
                    ge(pe, s.g_done, HC * (t - 3))
                    for n in range(HH):
                        bias(pA[:, n, :], 0, n)
                        for c in range(CC):
                            for a_, b_ in TERMS:
                                i_ = mm(pA[:, n, :], hTs[:, a_, c * P:(c + 1) * P],
                                        w1[:, b_, c * H + n * 512:c * H + (n + 1) * 512],
                                        start=False, stop=c == CC - 1 and (a_, b_) == TERMS[-1])
                        i_.then_inc(s.z1_ready, 1)
                if do[2]:
                    pe.wait_ge(s.z2_done, t - 1)
                    pe.wait_ge(s.a1_done, HC * (min(t, NT) if isinstance(t, int) else t))
                    for j in range(HC):
                        i_ = nc.tensor.transpose(pC[:, j // 4, (j % 4) * P:(j % 4 + 1) * P],
                                                 z2[:, j * P:(j + 1) * P], ident[:])
                    i_.then_inc(s.t2_ready, 1)
                if do[1]:
                    pe.wait_ge(s.a1_split, t)
                    ge(pe, s.z2_done, t - 1)
                    ge(pe, s.y3_done, t - 4 + 1)
                    layer2(t - 1, 0)
                if do[3]:
                    pe.wait_ge(s.xn2_done, t - 2)
                    ge(pe, s.hT_done, min(t + 1, NT) if isinstance(t, int) else t + 1)
                    for c in range(CC):
                        i_ = nc.tensor.transpose(pXT[:, c * P:(c + 1) * P], xn2[:, c * P:(c + 1) * P], ident[:])
                    i_.then_inc(s.x2T_ready, 1)
                if do[1]:
                    for n in range(1, HH):
                        layer2(t - 1, n)
                if do[3]:
                    pe.wait_ge(s.xn2T_done, t - 2)
                    if do[0]:
                        pe.wait_ge(s.z1_done, t + 1)
                    for j in range(HC):
                        for c in range(CC):
                            for a_, b_ in TERMS:
                                i_ = mm(pA[:, j // 4, (j % 4) * P:(j % 4 + 1) * P],
                                        fw1[:, a_, c * H + j * P:c * H + (j + 1) * P],
                                        xn2T[:, b_, c * P:(c + 1) * P],
                                        start=c == 0 and a_ + b_ == 0, stop=c == CC - 1 and (a_, b_) == TERMS[-1])
                    i_.then_inc(s.f1_ready, 1)
                if do[0]:
                    pe.wait_ge(s.z1_done, t + 1)
                    ge(pe, s.a1_done, HC * t)
                    if do[2]:
                        pe.wait_ge(s.a2_done, HC * (t - 1))
                    for j in range(HC):
                        i_ = nc.tensor.transpose(pC[:, j // 4, (j % 4) * P:(j % 4 + 1) * P],
                                                 z1[:, j * P:(j + 1) * P], ident[:])
                    i_.then_inc(s.t1_ready, 1)
                if do[4]:
                    node_sums(t + 1)
                if do[2]:
                    ge(pe, s.u_done, t - 2)
                    pe.wait_ge(s.a2_split, t - 1)
                    for k in range(HC):
                        for a_, b_ in TERMS:
                            i_ = mm(pY, aT2[:, a_, k * P:(k + 1) * P], w3[:, b_, k * C:(k + 1) * C],
                                    start=k == 0 and a_ + b_ == 0, stop=k == HC - 1 and (a_, b_) == TERMS[-1])
                    i_.then_inc(s.y_ready, 1)
                if do[3]:
                    pe.wait_ge(s.z2_done, min(t, NT) if isinstance(t, int) else t)
                    pe.wait_ge(s.g_split, t - 2)
                    for k in range(HC):
                        for a_, b_ in TERMS:
                            i_ = mm(pY2, gT[:, a_, k * P:(k + 1) * P], fw2[:, b_, k * C:(k + 1) * C],
                                    start=k == 0 and a_ + b_ == 0, stop=k == HC - 1 and (a_, b_) == TERMS[-1])
                    i_.then_inc(s.y2_ready, 1)

            node_sums(0)
            turns(pe, body_n)

            with pe.Fori(0, 32) as i:
                pe.wait_ge(s.cnt_done, i + 1)
                mm(psCnt, ones[:], cnt, start=True, stop=True).then_inc(s.cnt_ready, 1)
            pe.wait_ge(s.cnt_done, 33)
            mm(psCnt, ones[:], cnt, start=True, stop=True).then_inc(s.thr_ready, 1)
            pe.wait_ge(s.eqm2_done, 1)
            mm(psRank, before[:], eqm, start=True, stop=True)
            mm(psCol, ones[:], eqm, start=True, stop=True).then_inc(s.rank_ready, 1)

        @block.vector
        def _(dve):
            v = nc.vector
            dve.wait_ge(s.dst_in, 16)
            dve.wait_ge(s.const_in, n_const)
            dstf = dsti.bitcast(f32)[0:pl.gr]
            v.tensor_copy(dstf, dsti[0:pl.gr]).then_inc(s.dstf_done, 1)
            dve.wait_ge(s.dstf_done, 1)
            v.tensor_reduce(bases[0:pl.gr, :], dstf, AX.X, ALU.min).then_inc(s.base_done, 1)
            v.tensor_reduce(spans[0:pl.gr, :], dstf, AX.X, ALU.max).then_inc(s.base_done, 1)
            dve.wait_ge(s.base_done, 2)
            v.tensor_tensor(spans[0:pl.gr, :], spans[0:pl.gr, :], bases[0:pl.gr, :], ALU.subtract)\
                .then_inc(s.span_done, 1)
            for b in range(pl.nb):
                i_ = v.tensor_scalar(dstf[:, b, :], dstf[:, b, :], bases[0:pl.gr, b:b + 1], None, ALU.subtract)
                i_.then_inc(s.rel_done, 1)
            v.memset(acc[:], 0.0).then_inc(s.acc_zero, 1)
            relv = rel.rearrange("p (g e) -> p e g", e=GE)
            for b in range(pl.nb):
                for h in range(GE):
                    n = b * GE + h
                    gn = min(pl.gr, pl.groups - b * pl.gr)
                    dve.wait_ge(s.relT_ready, n + 1)
                    v.tensor_copy(relv[:, h, b * pl.gr:b * pl.gr + gn], psR[n % 2][:, 0:gn]).then_inc(s.relT_done, 1)
            dve.wait_ge(s.brow_ready, 1)
            v.tensor_copy(brow[0:1, :], psR[0][0:1, 0:pl.nb * pl.gr]).then_inc(s.brow_done, 1)
            v.tensor_reduce(span[0:1, 0:1], psR[1][0:1, 0:pl.nb * pl.gr], AX.X, ALU.max).then_inc(s.brow_done, 1)
            dve.wait_ge(s.brow_done, 2)
            v.tensor_copy(browi[0:1, :], brow[0:1, 0:pl.groups]).then_inc(s.browi_done, 1)
            v.tensor_copy(npass[0:1, 1:2], span[0:1, 0:1]).then_inc(s.browi_done, 1)
            dve.wait_ge(s.browi_done, 2)
            v.tensor_scalar(npass[0:1, 1:2], npass[0:1, 1:2], W.bit_length() - 1, None, ALU.arith_shift_right)\
                .then_inc(s.browi_done, 1)
            dve.wait_ge(s.browi_done, 3)
            v.tensor_scalar(npass[0:1, 0:1], npass[0:1, 1:2], 1.0, None, ALU.add).then_inc(s.pass_done, 1)
            dve.wait_ge(s.wq_hi, 2)
            for w_, full in ((wq, wqf), (wkv, wkvf)):
                v.scalar_tensor_tensor(w_[:, 1, :], full, WS, w_[:, 0, :], ALU.mult, ALU.subtract)\
                    .then_inc(s.wq_split, 1)
            v.tensor_scalar(twoeps, epscol[:], 2.0, None, ALU.add).then_inc(s.twoeps_done, 1)
            dve.wait_ge(s.twoeps_done, 1)
            dve.wait_ge(s.acc_zero, 1)
            dve.wait_ge(s.relu_b1_done, CC)
            for c in range(CC):
                v.tensor_scalar(acc[:, CC + c, :], acc[:, CC + c, :], b1h[:, c:c + 1], None, ALU.add)\
                    .then_inc(s.acc_zero, 1)
            with dve.Fori(0, NBATCH) as b:
                for j in range(BATCH):
                    dve.wait_ge(s.slab_in[j], 16 * (b + 1))
                    v.bn_stats(stats[:, ds(b * BATCH + j, 1), :], slab[:, j, :]).then_inc(s.stats_done, 1)
            dve.wait_ge(s.stats_done, NT)
            me, ve, mo, vo = (stats[:, :, k] for k in (1, 2, 4, 5))
            v.tensor_tensor(mean, me, mo, ALU.add).then_inc(s.mean_done, 1)
            v.tensor_tensor(tmp, me, mo, ALU.subtract).then_inc(s.mean_done, 1)
            v.tensor_tensor(var, ve, vo, ALU.add).then_inc(s.mean_done, 1)
            dve.wait_ge(s.mean_done, 3)
            v.tensor_scalar(mean, mean, -0.5, None, ALU.mult).then_inc(s.mean_done, 1)
            v.tensor_tensor(tmp, tmp, tmp, ALU.mult).then_inc(s.mean_done, 1)
            v.tensor_scalar(var, var, 1.0 / C, LN_EPS, ALU.mult, ALU.add).then_inc(s.mean_done, 1)
            dve.wait_ge(s.mean_done, 6)
            v.scalar_tensor_tensor(var, tmp, 0.25, var, ALU.mult, ALU.add).then_inc(s.var_done, 1)
            dve.wait_ge(s.rstd_done, 1)
            v.tensor_tensor(nmr, mean, rstd, ALU.mult).then_inc(s.nmr_done, 1)

            def take_xT(t, sl):
                dve.wait_ge(s.xT_ready, t + 1)
                ge(dve, s.q_ready, t - 1)
                v.tensor_copy(xt[sl][:, 0, :], psT[sl]).then_inc(s.xt_hi, 1)
                for c in range(CC):
                    v.tensor_scalar(acc[:, c, ds(t * P, P)], psT[sl][:, c * P:(c + 1) * P],
                                    twoeps, b2c[:, c:c + 1], ALU.mult, ALU.add).then_inc(s.xT_used, 1)
                dve.wait_ge(s.xt_hi, t + 1)
                v.tensor_tensor(xt[sl][:, 1, :], psT[sl], xt[sl][:, 0, :], ALU.subtract).then_inc(s.xt_done, 1)

            def take_kvq(t, sl):
                dve.wait_ge(s.ek_done, t + 1)
                v.tensor_scalar(ek[sl], ek[sl], 1.0, WS, ALU.min, ALU.mult).then_inc(s.em_done, 1)
                ge(dve, s.ctx_done, t - 1)
                dve.wait_ge(s.em_done, t + 1)
                dve.wait_ge(s.v_done, t + 1)
                v.scalar_tensor_tensor(ks[sl], psKV[sl][:, 0:C], 0.0, ek[sl], ALU.max, ALU.add)\
                    .then_inc(s.k_done, 1)
                dve.wait_ge(s.eq_done, t + 1)
                v.tensor_scalar(eq[sl], eq[sl], 1.0, WS, ALU.min, ALU.mult).then_inc(s.eqm_done, 1)
                dve.wait_ge(s.eqm_done, t + 1)
                v.scalar_tensor_tensor(
                    qT[:, :, ds(t * P, P)], psQ[sl].rearrange("p (a b) -> p a b", b=P), 0.0,
                    eq[sl].rearrange("p (a b) -> p a b", b=P), ALU.max, ALU.add).then_inc(s.q_done, 1)

            def body(t, h, sl):
                take_xT(t + 1, 1 - sl)
                take_kvq(t, sl)

            take_xT(0, 0)
            body(0, 0, 0)
            body(1, 0, 1)
            in_pairs(dve, 2, NT - 1, body)
            take_kvq(NT - 1, (NT - 1) % 2)

            dve.wait_ge(s.ctx_done, NT)
            for c in range(CC):
                v.tensor_tensor(ctm[:, c, :], psX[:, c * P:(c + 1) * P], head, ALU.mult).then_inc(s.ctm_done, 1)
                v.tensor_scalar(ksb[:, c, :], head, psX[:, C + c:C + c + 1], None, ALU.mult).then_inc(s.ksb_done, 1)
            dve.wait_ge(s.ksb_done, CC)
            dve.wait_ge(s.m_ready, 1)
            for sl in range(2):
                dve.wait_ge(s.xn_stored[sl], 16 * ((NT + 1 - sl) // 2))
                dve.wait_ge(s.tab_stored[sl], 16 * ((NT + 1 - sl) // 2))
            v.tensor_copy(mixw, psM.rearrange("p (a b) -> p a b", b=C)).then_inc(s.front_done, 1)
            dve.wait_ge(s.front_done, 1)

            def one_hot(i, j, q):
                n = q * GPT + j
                ge(dve, s.scat_done, n - 1)
                for e in range(GE):
                    i_ = v.tensor_scalar(oh[j % 2][:, e, :], iota, rel[:, ds((i * GPT + j) * GE + e, 1)], None,
                                         ALU.is_equal)
                i_.then_inc(s.oh_done, 1)

            def low_part(j, q):
                n = q * PPB + j
                dve.wait_ge(s.hi_done, n + 1)
                v.scalar_tensor_tensor(hm[j % 4][:, 1, :], psH[j % 2], 0.0, hm[j % 4][:, 0, :], ALU.max,
                                       ALU.subtract).then_inc(s.lo_done, 1)

            def window(i, j, q):
                n = q * GPT + j
                base = dve.value_load(browi[0:1, ds(i * GPT + j, 1)], min_val=0, max_val=pl.np)
                dve.wait_ge(s.scat_done, n + 1)
                ge(dve, s.ev_done, n)
                v.tensor_tensor(acc[:, :, ds(base, W)], psS[j % 2].rearrange("p (a b) -> p a b", b=W),
                                acc[:, :, ds(base, W)], ALU.add).then_inc(s.ev_done, 1)

            def attention_rows(i, j):
                if j == 0:
                    dve.wait_ge(s.d_ready, i + 1)
                    ge(dve, s.xm_done, i)
                    v.tensor_scalar(dcl, psD, 1e-6 * WS * WS, None, ALU.max).then_inc(s.dcl_done, 1)
                    dve.wait_ge(s.dcl_done, i + 1)
                    v.reciprocal(dcl, dcl).then_inc(s.rcp_done, 1)
                    dve.wait_ge(s.rcp_done, i + 1)
                    ge(dve, s.o_ready, i)
                    v.tensor_tensor(q2.rearrange("p (a b) -> p a b", b=P), qT[:, :, ds(i * P, P)],
                                    dcl.rearrange("p (a b) -> p a b", b=P), ALU.mult).then_inc(s.q2_done, 1)
                if j == 1:
                    dve.wait_ge(s.ws_hi, i + 1)
                    v.scalar_tensor_tensor(wsp[:, 1, :], wst, WS, wsp[:, 0, :], ALU.mult, ALU.subtract)\
                        .then_inc(s.ws_lo, 1)
                if j == GPT - 1:
                    dve.wait_ge(s.xml_in, 16 * (i + 1))
                    dve.wait_ge(s.q2_done, i + 1)
                    v.tensor_tensor(dcl, xml, bprow, ALU.add).then_inc(s.xpb_done, 1)
                    dve.wait_ge(s.o_ready, i + 1)
                    dve.wait_ge(s.xpb_done, i + 1)
                    ge(dve, s.xm_stored, 16 * i)
                    v.tensor_tensor(xmo, psO, dcl, ALU.add).then_inc(s.xm_done, 1)

            def edges(i, q, mix=False):
                for j in range(GPT):
                    one_hot(i, j, q)
                    low_part(2 * j, q)
                    low_part(2 * j + 1, q)
                    if j:
                        window(i, j - 1, q)
                    if mix:
                        attention_rows(i, j)
                window(i, GPT - 1, q)

            edges(0, 0, True)
            with dve.Fori(1, NT) as i:
                edges(i, i, True)

            def next_window(p):
                v.tensor_scalar(rel, rel, -float(W), None, ALU.add).then_inc(s.win_done, 1)
                v.tensor_scalar(brow[0:1, :], brow[0:1, :], float(W), float(pl.np), ALU.add, ALU.min)\
                    .then_inc(s.win_done, 1)
                dve.wait_ge(s.win_done, 3 * p - 1)
                v.tensor_copy(browi[0:1, :], brow[0:1, 0:pl.groups]).then_inc(s.win_done, 1)
                dve.wait_ge(s.pass_done, 1)
                dve.wait_ge(s.win_done, 3 * p)

            passes(dve, edges, next_window)
            dve.wait_ge(s.xm_stored, 16 * NT)
            v.memset(oh[0], 0.0).then_inc(s.edges_done, 1)

            dve.wait_ge(s.late_in, n_late)
            dve.wait_ge(s.edges_done, 1)

            def row_stats(t, scale, rows, st, mv, rs, nm, ready, stated, aggr, rstd_, nmr_):
                for n in range(HH):
                    dve.wait_ge(ready, HH * t + n + 1)
                    v.bn_stats(st[:, n, :], rows[:, n, :]).then_inc(stated, 1)
                dve.wait_ge(stated, HH * (t + 1))
                in_own(dve, s.dve_spare)
                v.bn_aggr(mv, st.rearrange("p a b -> p (a b)")).then_inc(nmr_, 1)
                dve.wait_ge(nmr_, 2 * t + 1)
                v.tensor_scalar(mv[:, 1:2], mv[:, 1:2], LN_EPS * scale * scale, None, ALU.add).then_inc(aggr, 1)
                dve.wait_ge(rstd_, t + 1)
                v.scalar_tensor_tensor(nm, mv[:, 0:1], -1.0, rs, ALU.mult, ALU.mult).then_inc(nmr_, 1)

            def split(parts, full, src_ready, hi_done, done, n):
                dve.wait_ge(src_ready, HC * n)
                v.tensor_copy(parts[:, 0, :], full).then_inc(hi_done, 1)
                dve.wait_ge(hi_done, n)
                v.tensor_tensor(parts[:, 1, :], full, parts[:, 0, :], ALU.subtract).then_inc(done, 1)

            def node_sums(t):
                dve.wait_ge(s.hT_ready, t + 1)
                ge(dve, s.z1_ready, HH * t)
                v.tensor_tensor(hT, pHT.rearrange("p (a b) -> p a b", b=P),
                                acc[:, 0:CC, ds(t * P, P)], ALU.add).then_inc(s.hT_done, 1)
                dve.wait_ge(s.hT_done, t + 1)
                v.tensor_scalar(hTs3[0], hT, HS, None, ALU.mult).then_inc(s.hT_hi, 1)
                dve.wait_ge(s.hT_hi, t + 1)
                v.scalar_tensor_tensor(hTs3[1], hT, HS, hTs3[0], ALU.mult, ALU.subtract)\
                    .then_inc(s.hT_split, 1)

            def body_n(t, do):
                if do[0]:
                    ge(dve, s.z1_done, t)
                    row_stats(t, WS * HS, pA, st1, mv1, rs1, nm1, s.z1_ready, s.z1_stats, s.z1_aggr,
                              s.z1_rstd, s.z1_nmr)
                if do[2]:
                    ge(dve, s.y_ready, t - 2)
                    split(aT2, z2, s.a2_done, s.a2_hi, s.a2_split, t - 1)
                if do[3]:
                    dve.wait_ge(s.x2T_ready, t - 2)
                    ge(dve, s.f1_ready, t - 3)
                    v.tensor_copy(xn2T[:, 0, :], pXT).then_inc(s.xn2T_hi, 1)
                    dve.wait_ge(s.xn2T_hi, t - 2)
                    v.tensor_tensor(xn2T[:, 1, :], pXT, xn2T[:, 0, :], ALU.subtract).then_inc(s.xn2T_done, 1)
                if do[1]:
                    ge(dve, s.z2_done, t - 1)
                    row_stats(t - 1, WS, pB, st2, mv2, rs2, nm2, s.z2_ready, s.z2_stats, s.z2_aggr,
                              s.z2_rstd, s.z2_nmr)
                if do[4]:
                    node_sums(t + 1)
                if do[3]:
                    ge(dve, s.y2_ready, t - 3)
                    split(gT, gf, s.g_done, s.g_hi, s.g_split, t - 2)
                if do[0]:
                    ge(dve, s.z2_ready, HH * t)
                    split(aT1, z1, s.a1_done, s.a1_hi, s.a1_split, t + 1)
                if do[2]:
                    r = t - 2
                    dve.wait_ge(s.y_ready, r + 1)
                    dve.wait_ge(s.xres_done, r + 1)
                    v.scalar_tensor_tensor(u, pY, 1 / WS, xres, ALU.mult, ALU.add).then_inc(s.u_done, 1)
                    dve.wait_ge(s.u_done, r + 1)
                    v.bn_stats(st3, u).then_inc(s.u_stats, 1)
                    dve.wait_ge(s.u_stats, r + 1)
                    in_own(dve, s.dve_spare)
                    v.bn_aggr(mv3, st3).then_inc(s.u_nmr, 1)
                    dve.wait_ge(s.u_nmr, 2 * r + 1)
                    v.tensor_scalar(mv3[:, 1:2], mv3[:, 1:2], LN_EPS, None, ALU.add).then_inc(s.u_aggr, 1)
                    dve.wait_ge(s.u_rstd, r + 1)
                    v.scalar_tensor_tensor(nm3, mv3[:, 0:1], -1.0, rs3, ALU.mult, ALU.mult).then_inc(s.u_nmr, 1)
                    dve.wait_ge(s.u_nmr, 2 * r + 2)
                    v.tensor_scalar(u, u, rs3, nm3, ALU.mult, ALU.add).then_inc(s.u_norm, 1)
                if do[3]:
                    dve.wait_ge(s.y2_ready, t - 2)
                    v.scalar_tensor_tensor(acc[:, CC:2 * CC, ds((t - 3) * P, P)], pY2.rearrange("p (a b) -> p a b", b=P),
                                           1 / WS, fb2row.rearrange("p (a b) -> p a b", b=P), ALU.mult, ALU.add)\
                        .then_inc(s.y3_done, 1)
                if do[2]:
                    dve.wait_ge(s.u_affine, 2 * (r + 1))
                    dve.wait_ge(s.xmix_in, 16 * (r + 1))
                    v.scalar_tensor_tensor(x2, u, 0.0, xmix, ALU.max, ALU.add).then_inc(s.x2_done, 1)
                    dve.wait_ge(s.x2_done, r + 1)
                    v.bn_stats(st4, x2).then_inc(s.x2_stats, 1)
                    dve.wait_ge(s.x2_stats, r + 1)
                    in_own(dve, s.dve_spare)
                    v.bn_aggr(mv4, st4).then_inc(s.x2_nmr, 1)
                    dve.wait_ge(s.x2_nmr, 2 * r + 1)
                    v.tensor_scalar(mv4[:, 1:2], mv4[:, 1:2], LN_EPS, None, ALU.add).then_inc(s.x2_aggr, 1)
                    dve.wait_ge(s.x2_rstd, r + 1)
                    v.scalar_tensor_tensor(nm4, mv4[:, 0:1], -1.0, rs4, ALU.mult, ALU.mult).then_inc(s.x2_nmr, 1)
                    dve.wait_ge(s.x2_nmr, 2 * r + 2)
                    ge(dve, s.x2T_ready, r)
                    v.tensor_scalar(xn2, x2, rs4, nm4, ALU.mult, ALU.add).then_inc(s.xn2_done, 1)
                    dve.wait_ge(s.xn2_done, r + 1)
                    v.tensor_tensor(acc[:, 0:CC, ds(r * P, P)], x2.rearrange("p (a b) -> p a b", b=P),
                                    xn2.rearrange("p (a b) -> p a b", b=P), ALU.add).then_inc(s.base_out, 1)
                    v.tensor_tensor_reduce(u, xn2, wrrow, 1.0, 0.0, ALU.mult, ALU.add, wcol).then_inc(s.w_done, 1)
                    dve.wait_ge(s.w_done, 2 * r + 1)
                    v.tensor_copy(wr_all[:, ds(r, 1)], wcol).then_inc(s.w_done, 1)

            node_sums(0)
            turns(dve, body_n)

            dve.wait_ge(s.w_done, 2 * NT)
            v.tensor_scalar(wv, wr_all[:], brc[:], None, ALU.add).then_inc(s.wv_done, 1)
            dve.wait_ge(s.wv_done, 1)
            v.tensor_tensor(wv, wv, valid[:], ALU.mult).then_inc(s.wv_done, 1)
            dve.wait_ge(s.wv_done, 2)
            v.tensor_tensor(wv, wv, below[:], ALU.add).then_inc(s.wv_done, 1)
            v.memset(pfx, 0).then_inc(s.bit_step, 1)
            dve.wait_ge(s.wv_done, 3)

            def as_float(key, step):
                v.tensor_scalar(t1, key, 31, 0x7FFFFFFF, ALU.arith_shift_right, ALU.bitwise_xor)\
                    .then_inc(s.bit_step, 1)
                dve.wait_ge(s.bit_step, step + 1)
                v.scalar_tensor_tensor(flt, t1, -2 ** 31, key, ALU.bitwise_or, ALU.bitwise_xor)\
                    .then_inc(s.bit_step, 1)
                dve.wait_ge(s.bit_step, step + 2)

            with dve.Fori(0, 32) as i:
                dve.wait_ge(s.bit_step, 6 * i + 1)
                v.tensor_tensor(cand, pfx, bits[:, ds(i, 1)], ALU.bitwise_or).then_inc(s.bit_step, 1)
                dve.wait_ge(s.bit_step, 6 * i + 2)
                as_float(cand, 6 * i + 2)
                v.tensor_scalar(junk, wv, flt.bitcast(f32), None, ALU.is_ge, ALU.add, accum_out=cnt)\
                    .then_inc(s.cnt_done, 1)
                dve.wait_ge(s.cnt_ready, i + 1)
                v.tensor_scalar(m, psCnt, float(KSEL), -1.0, ALU.is_ge, ALU.mult).then_inc(s.bit_step, 1)
                dve.wait_ge(s.bit_step, 6 * i + 5)
                v.tensor_tensor(m, m, bits[:, ds(i, 1)], ALU.bitwise_and).then_inc(s.bit_step, 1)
                dve.wait_ge(s.bit_step, 6 * i + 6)
                v.tensor_tensor(pfx, m, pfx, ALU.bitwise_or).then_inc(s.bit_step, 1)
            dve.wait_ge(s.bit_step, 6 * 32 + 1)
            as_float(pfx, 6 * 32 + 1)
            thr = flt.bitcast(f32)
            v.tensor_scalar(gtm, wv, thr, None, ALU.is_gt, ALU.add, accum_out=cnt).then_inc(s.cnt_done, 1)
            v.tensor_scalar(eqm, wv, thr, None, ALU.is_equal).then_inc(s.eqm2_done, 1)
            dve.wait_ge(s.thr_ready, 1)
            v.tensor_scalar(need, psCnt, -1.0, float(KSEL), ALU.mult, ALU.add).then_inc(s.pick_step, 1)
            dve.wait_ge(s.rank_ready, 1)
            v.tensor_copy(csum, psCol).then_inc(s.pick_step, 1)
            dve.wait_ge(s.pick_step, 2)
            v.tensor_tensor_scan(incl, csum, csum, 0.0, ALU.add, ALU.bypass).then_inc(s.pick_step, 1)
            dve.wait_ge(s.pick_step, 3)
            v.tensor_tensor(incl, incl, csum, ALU.subtract).then_inc(s.pick_step, 1)
            dve.wait_ge(s.pick_step, 4)
            v.tensor_tensor(rank, psRank, incl, ALU.add).then_inc(s.pick_step, 1)
            dve.wait_ge(s.pick_step, 5)
            dve.wait_ge(s.eqm2_done, 1)
            v.scalar_tensor_tensor(rank, rank, need, eqm, ALU.is_lt, ALU.mult).then_inc(s.pick_step, 1)
            dve.wait_ge(s.pick_step, 6)
            dve.wait_ge(s.cnt_done, 33)
            v.tensor_tensor(gtm, gtm, rank, ALU.add).then_inc(s.pick_step, 1)
            dve.wait_ge(s.pick_step, 7)
            v.tensor_tensor(mw, gtm, wv, ALU.mult).then_inc(s.pick_step, 1)
            dve.wait_ge(s.pick_step, 8)
            dve.wait_ge(s.base_out, NT)
            dve.wait_ge(s.y3_done, NT)
            def outputs(b):
                for j in range(BATCH):
                    t = b * BATCH + j
                    ge(dve, s.slab_in[j], LOADED + 16 * b)
                    v.scalar_tensor_tensor(ob[j].rearrange("p (a b) -> p a b", b=P), acc[:, CC:2 * CC, ds(t * P, P)],
                                           mw[:, ds(t, 1)], acc[:, 0:CC, ds(t * P, P)], ALU.mult, ALU.add)\
                        .then_inc(s.ob_done, 1)

            outputs(0)
            with dve.Fori(1, NBATCH) as b:
                outputs(b)


def kernel(**inputs):
    import concourse.bacc as _bacc
    from concourse.bass_utils import run_bass_kernel_spmd as _run

    g = {k[3:] if k.startswith("L0_") else k: np.asarray(v) for k, v in inputs.items()}
    n, e = g["x"].shape[0], g["src"].shape[0]
    pl = plan(n, e, g["gnn_w1"].shape[1])
    ep = pl.tiles * P

    def chunks(w):
        return w.reshape(-1, P, w.shape[1]).transpose(1, 0, 2)

    def flat(w):
        return chunks(w).reshape(P, -1)

    def column(b):
        return b.reshape(-1, P).T

    dst = np.full(pl.nb * pl.gr * GE * P, n, np.int32)
    dst[:e] = g["dst"]
    src = np.zeros(ep, np.int32)
    src[:e] = g["src"]
    x = np.zeros((pl.np, C), np.float32)
    x[:n] = g["x"]
    ea = np.zeros((ED, ep), np.float32)
    ea[:, :e] = g["edge_attr_64"].T
    wall = np.zeros((P, pl.nt * pl.wchunk), np.float32)
    mats = np.concatenate([flat(g[k]) for k in ("gnn_w1", "gnn_w2", "gnn_w3", "ffn_w1", "ffn_w2")], 1)
    wall[:, :mats.shape[1]] = mats
    wall[0:2, mats.shape[1]:pl.wcols] = g["gnn_b1"], g["gnn_b2"]
    arrays = {
        "x": x, "ea": ea, "src": src.reshape(-1, P).T,
        "dst": dst.reshape(pl.nb, pl.gr, GE * P).transpose(1, 0, 2),
        "eps": g["gnn_eps"].reshape(1), "br": g["ffn_br"].reshape(1),
        "ee_w1": g["gnn_ee_w1"], "ee_b1": g["gnn_ee_b1"].reshape(1, -1),
        "ee_b1c": column(g["gnn_ee_b1"]), "ee_w2": chunks(g["gnn_ee_w2"]),
        "ee_b2": g["gnn_ee_b2"], "ee_b2c": column(g["gnn_ee_b2"]),
        "wall": wall,
        "b3": g["gnn_b3"],
        "g1": column(g["gnn_g1"]), "be1": column(g["gnn_be1"]),
        "g2": column(g["gnn_g2"]), "be2": column(g["gnn_be2"]),
        "bn_g": g["gnn_bn_g"], "bn_b": g["gnn_bn_b"],
        "wq": flat(g["mix_Wq"].T), "wkv": flat(g["mix_Wkv"].T), "wproj": chunks(g["mix_Wproj"].T),
        "bproj": g["mix_bproj"], "wr": g["ffn_wr"].reshape(-1),
        "fb1": column(g["ffn_b1"]),
        "fb2": g["ffn_b2"],
        "bits": np.tile((np.uint32(1) << np.arange(31, -1, -1).astype(np.uint32)).view(np.int32), (P, 1)),
        **constants(pl),
    }
    arrays = {k: np.ascontiguousarray(v) for k, v in arrays.items()}
    nc = _bacc.Bacc("TRN2", target_bir_lowering=False, num_devices=1)
    aps = namedtuple("Inputs", arrays)(**{
        k: nc.dram_tensor(f"in_{k}", v.shape, mybir.dt.from_np(v.dtype), kind="ExternalInput").ap()
        for k, v in arrays.items()})
    out = nc.dram_tensor("out_0", (pl.np, C), mybir.dt.float32, kind="ExternalOutput").ap()
    gps_kernel(nc, aps, out, pl)
    r = _run(nc, [{f"in_{k}": v for k, v in arrays.items()}], core_ids=[0])
    return r.results[0]["out_0"][:n]
```

```python
from collections import namedtuple
from contextlib import ExitStack

import numpy as np
import concourse.bass as bass
from concourse import mybir

P = 128
C = 256
CC = C // P
W = 128
GE = 4
PE2 = 2
WS = 256.0
HS = 1.0 / 32
TERMS = ((0, 0), (0, 1), (1, 0))
HEADS = 8
ED = 64
LN_EPS = 1e-5
CAPACITY = 0.5
DIGITS = 11
CANDS = 8


Plan = namedtuple("Plan", "n nt np gpt groups tiles nb gr batch wid wcols wchunk")


def plan(n_nodes, n_edges, hidden):
    nt = -(-n_nodes // P)
    gpt = -(-n_edges // (GE * P * nt))
    gpt += gpt % 2
    groups = nt * gpt
    nb = -(-groups // P)
    gr = -(-groups // nb)
    batch = max(b for b in range(1, 9) if nt % b == 0 and nt > b)
    wcols = CC * hidden + hidden // P * hidden + hidden // P * C
    wcols += CC * hidden + hidden // P * C + hidden
    wchunk = -(-wcols // (2 * nt)) * 2
    return Plan(n=n_nodes, nt=nt, np=nt * P, gpt=gpt, groups=groups, tiles=groups * GE,
                nb=nb, gr=gr, batch=batch, wid=nt * P + W, wcols=wcols, wchunk=wchunk)


def constants(pl):
    i = np.arange(P)
    valid = (np.arange(pl.nt)[None, :] * P + i[:, None] < pl.n).astype(np.float32)
    return {
        "ident": np.eye(P, dtype=np.float32),
        "ones": np.ones((P, P), np.float32),
        "before": (i[:, None] < i[None, :]).astype(np.float32),
        "head": (i[:, None] // (C // HEADS) == i[None, :] // (C // HEADS)).astype(np.float32),
        "iota": np.tile(np.arange(W, dtype=np.float32), (P, 1)),
        "valid": valid,
        "below": (valid - 1.0) * np.float32(3e38),
    }


def digit_steps():
    shift = 3 * (DIGITS - 1 - np.arange(DIGITS, dtype=np.uint64))[:, None]
    k = np.arange(1, CANDS + 1, dtype=np.uint64)[None, :]
    real = (k < CANDS) & ((k << shift) < 2 ** 32)
    value = np.where(real, k << shift, 0).max(1, keepdims=True)
    value = np.where(real, k << shift, value)
    change = np.where(real, (k << shift) ^ ((k - 1) << shift), 0)
    return np.concatenate([value, change], 1).astype(np.uint32).view(np.int32)


def ge(eng, sem, value):
    if isinstance(value, int) and value <= 0:
        return
    eng.wait_ge(sem, value)


def in_own(eng, spare):
    eng.sem_inc(spare, 1)


def in_pairs(eng, first, last, body):
    pairs = max(last - first, 0) // 2
    if pairs:
        with eng.Fori(0, pairs) as h:
            body(2 * h + first, h + first // 2, first % 2)
            body(2 * h + first + 1, h + (first + 1) // 2, (first + 1) % 2)
    for t in range(first + 2 * pairs, last):
        body(t, t // 2, t % 2)


def gps_kernel(nc, A, out, pl):
    f32, f16, i32 = mybir.dt.float32, mybir.dt.float16, mybir.dt.int32
    ALU, ACT, AX = mybir.AluOpType, mybir.ActivationFunctionType, mybir.AxisListType
    ds = bass.ds
    NT, GPT, TPB, PPB = pl.nt, pl.gpt, pl.gpt * GE, pl.gpt * GE // PE2
    WC = pl.wchunk
    BATCH, NBATCH = pl.batch, pl.nt // pl.batch
    H = A.g1.shape[1] * P
    HC, HH = H // P, H // 512
    HALF = GPT // 2
    KSEL = max(1, int(CAPACITY * pl.n))
    KSEL = KSEL - 1 if KSEL > 1 else 1

    x_rows = A.x.rearrange("(t p) c -> t p c", p=P)
    xn_d = nc.dram_tensor("xn_rows", (NT, P, C), f32, kind="Internal").ap()
    xm_d = nc.dram_tensor("mix_rows", (NT, P, C), f32, kind="Internal").ap()
    table = nc.dram_tensor("gather_table", (pl.np, 2 * C), f16, kind="Internal").ap()
    table_rows = table.rearrange("(t p) c -> t p c", p=P)
    wsplit = nc.dram_tensor("split_weights", (P, 2, NT * WC), f16, kind="Internal").ap()
    out_rows = out.rearrange("(t p) c -> t p c", p=P)

    ctx = ExitStack()
    with ctx:
        def sb(name, shape, dt=f32):
            return ctx.enter_context(nc.sbuf_tensor(name, shape, dt))

        def sem(name):
            return ctx.enter_context(nc.semaphore(name))

        acc = sb("acc", [P, 4, pl.wid])
        ident = sb("ident", [P, P])
        valid = sb("valid", [P, NT])
        below = sb("below", [P, NT])
        ee2 = sb("ee2", [P, CC, C])
        wr_all = sb("wr_all", [P, NT])
        epscol = sb("epscol", [P, 1])
        g1c, be1c, g2c, be2c, fb1c = [sb(n, [P, HC]) for n in ("g1c", "be1c", "g2c", "be2c", "fb1c")]
        brc = sb("brc", [P, 1])
        mh = sb("mh", [P, 1])

        class Carver:
            def __init__(self, base):
                self.base, self.at = base, 0

            def __call__(self, *shape, dt=f32):
                n = int(np.prod(shape))
                words = n if dt in (f32, i32) else -(-n // 2)
                ap = self.base[:, self.at:self.at + words]
                self.at += words
                assert self.at <= self.base.shape[1], (self.at, self.base.shape)
                if dt is not f32:
                    ap = ap.bitcast(dt)
                if len(shape) == 2:
                    ap = ap.rearrange("p (a b) -> p a b", b=shape[1])
                if len(shape) == 3:
                    ap = ap.rearrange("p (a b c) -> p a b c", b=shape[1], c=shape[2])
                return ap

        big = sb("big", [P, max(CC * pl.np, 12544)])
        qT = Carver(big)(NT * C)
        wts = Carver(big)
        w1, w2, w3 = wts(2, CC * H, dt=f16), wts(2, HC * H, dt=f16), wts(2, HC * C, dt=f16)
        ones, before = wts(P), wts(P)

        arena = sb("arena", [P, max(14144, 11800 + 2 * WC)])
        a = Carver(arena)
        early = Carver(big)
        dsti, wqf, wkvf = early(pl.nb, GE * P, dt=i32), early(CC * C), early(CC * 2 * C)
        xs, xn, ek, eq, ks, vs = [[a(C) for _ in range(2)] for _ in range(6)]
        xt = [a(2, C, dt=f16) for _ in range(2)]
        tab = [a(2 * C, dt=f16) for _ in range(2)]
        xb, b2row = [a(C) for _ in range(2)], a(C)
        wproj = a(CC, C)
        wq, wkv = a(2, CC * C, dt=f16), a(2, CC * 2 * C, dt=f16)
        ctm = a(CC, P)
        stx, mvx = [a(6) for _ in range(2)], [a(2) for _ in range(2)]
        rsx, nmx = [a(1) for _ in range(2)], [a(1) for _ in range(2)]
        span = a(4)
        bases, spans = a(pl.nb), a(pl.nb)
        b2c, twoeps, b1h = a(CC), a(1), a(CC)
        front_end = a.at

        a = Carver(arena)
        xg = a(TPB, 2 * C, dt=f16)
        ea = a(GPT, GE * P)
        hm = [a(2, PE2 * C, dt=f16) for _ in range(4)]
        oh = [a(GE, W, dt=f16) for _ in range(2)]
        dcl, q2, xml, xmo = a(C), a(C), a(C), a(C)
        idx = a(TPB, dt=i32)
        wst, wsp = a(WC), a(2, WC, dt=f16)
        a.at = max(a.at, front_end)
        mixw, ksb, ee1, iota, bprow, head = a(CC, C), a(CC, P), a(C), a(W), a(C), a(P)
        rel = a(pl.tiles)
        brow = a(pl.nb * pl.gr)
        browi, npass = a(pl.groups, dt=i32), a(2, dt=i32)

        a = Carver(arena)
        fw1, fw2 = a(2, CC * H, dt=f16), a(2, HC * C, dt=f16)
        bias2, bones = a(H, dt=f16), a(P, dt=f16)
        b3row, bngrow, bnbrow, fb2row, wrrow = [a(C) for _ in range(5)]
        z1, z2, gf = a(H), a(H), a(H)
        z1T, z2T, gfT = (z.rearrange("p (a b) -> p a b", b=P) for z in (z1, z2, gf))
        aT1, aT2, gT = [a(2, H, dt=f16) for _ in range(3)]
        hTs, xn2T = a(2, C, dt=f16), a(2, C, dt=f16)
        hTs3 = [hTs[:, k, :].rearrange("p (a b) -> p a b", b=P) for k in range(2)]
        hT = acc[:, 0:CC, pl.np:pl.np + P]
        u, x2, xn2, xres, xmix = [a(C) for _ in range(5)]
        st1, st2, st3, st4 = a(2, 6), a(2, 6), a(6), a(6)
        mv1, mv2, mv3, mv4 = [a(2) for _ in range(4)]
        rs1, rs2, rs3, rs4, nm1, nm2, nm3, nm4, wcol = [a(1) for _ in range(9)]
        steps = a(DIGITS, 2 * CANDS, dt=i32)
        a = Carver(arena)
        ob = [a(C) for _ in range(BATCH)]
        a = Carver(z1)
        wv, gtm, eqm, csum, incl, rank, mw = [a(NT) for _ in range(7)]
        reach = a(CANDS, NT)
        pfx, cand, t1, flt, m, m4, m2 = [a(CANDS, dt=i32) for _ in range(7)]
        cnt, cnt1, need = a(CANDS), a(1), a(1)

        ps = ctx.enter_context(nc.psum_tensor("ps", [P, 8, 512], f32))
        psT = [ps[:, b, 0:C] for b in (0, 7)]
        psKV = [ps[:, 1 + s, :] for s in range(2)]
        psQ = [ps[:, b, 0:C] for b in (3, 6)]
        psX = ps[:, 4, 0:C + CC]
        psR = [ps[:, 5, :], ps[:, 6, :]]
        psM = ps[:, 5, :]
        psH = [ps[:, b, :] for b in (0, 1, 6, 7)]
        psS = [ps[:, 2 + s, :] for s in range(2)]
        psD, psO = ps[:, 4, 0:C], ps[:, 5, 0:C]
        pA, pB, pC = ps[:, 0:2, :], ps[:, 2:4, :], ps[:, 4:6, :]
        pHT, pXT = ps[:, 6, 0:C], ps[:, 6, C:2 * C]
        pY, pY2 = ps[:, 7, 0:C], ps[:, 2, 0:C]
        psCnt, psCnt1 = ps[:, 4, 0:CANDS], ps[:, 4, 0:1]
        psRank, psCol = ps[:, 5, 0:NT], ps[:, 3, 0:NT]

        names = """const_in front_in x_stats x_aggr x_mv x_rstd x_nmr acc_init dst_in dstf_done base_done rel_done
          relT_ready relT_done brow_ready brow_done browi_done span_done pass_done twoeps_done
          relu_b1_done xn_done xT_ready xt_done xT_used kv_ready ek_done em_done k_done v_done
          q_ready eq_done eqm_done q_done ctx_done xb_done hi16_done tab_done ctm_done ksb_done
          m_ready mh_done ob_done front_done ea_ones hid_done hi_done lo_done oh_done scat_done
          ev_done d_ready dcl_done rcp_done q2_done o_ready xpb_done xm_done win_done edges_done
          wts_in late_in ffn_in hT_ready hT_done z1_ready z1_stats z1_aggr z1_rstd z1_nmr
          z1_done t1_ready a1_done z2_ready z2_stats z2_aggr z2_rstd z2_nmr z2_done t2_ready
          a2_done y_ready xres_done u_done u_stats u_aggr u_rstd u_nmr u_norm u_affine x2_done
          x2_stats x2_aggr x2_rstd x2_nmr xn2_done base_out w_done x2T_ready xn2T_done f1_ready
          g_done y2_ready y3_done wv_done cnt_done cnt_ready thr_ready eqm2_done rank_ready
          bit_step pick_step pool_spare dve_spare xml_in xm_stored xres_in xmix_in ws_in
          ws_stored wq_hi wq_split ws_hi ws_lo xt_hi hT_hi hT_split xn2T_hi a1_hi a1_split a2_hi
          a2_split g_hi g_split""".split()
        sems = {n: sem(n) for n in names}
        for n, count in (("ob_stored", BATCH), ("x_in", 2), ("xn_stored", 2), ("tab_stored", 2),
                         ("ea_in", GPT), ("xg_in", GPT), ("idx_in", 2)):
            sems[n] = [sem(f"{n}{j}") for j in range(count)]
        s = namedtuple("Semaphores", sems)(**sems)

        front_loads = [(wkvf, A.wkv), (wqf, A.wq), (b2c, A.ee_b2c), (b1h, A.ee_b1c), (valid, A.valid)]
        front_rows = [(epscol, A.eps), (b2row, A.ee_b2)]
        const_loads = [(wproj, A.wproj), (head, A.head), (ee1[0:ED, :], A.ee_w1), (ee1[ED:ED + 1, :], A.ee_b1),
                       (iota, A.iota), (below, A.below), (ee2, A.ee_w2), (g1c, A.g1), (be1c, A.be1),
                       (g2c, A.g2), (be2c, A.be2), (fb1c, A.fb1)]
        const_rows = [(brc, A.br), (bprow, A.bproj)]
        pieces, at = [], 0
        for w_, cols in ((w1, CC * H), (w2, HC * H), (w3, HC * C)):
            for c in range(0, cols, H):
                for k in range(2):
                    words = (2 * at + k * cols + c + H) // 2
                    after = max(-(-words // C), -(-(at + c + H) // WC))
                    pieces.append((w_[:, k, c:c + H], wsplit[:, k, at + c:at + c + H], min(after, NT)))
            at += cols
        pieces += [(ones, A.ones, NT), (before, A.before, NT)]
        late_loads, ffn_loads = [(steps.rearrange("p a b -> p (a b)"), A.steps)], []
        for dst_, cols in ((fw1, CC * H), (fw2, HC * C)):
            ffn_loads.append((dst_, wsplit[:, :, at:at + cols]))
            at += cols
        bias_loads = [(bias2[32 * k:32 * k + 2, :], wsplit[k, :, at:at + H]) for k in range(2)]
        assert at + H == pl.wcols
        late_rows = [(b3row, A.b3), (bngrow, A.bn_g),
                     (bnbrow, A.bn_b), (fb2row, A.fb2), (wrrow, A.wr)]
        n_front = 16 * (len(front_loads) + len(front_rows))
        n_const = 16 * (len(const_loads) + len(const_rows))
        n_late = 16 * (len(late_loads) + len(late_rows))

        def passes(eng, edge_body, between=None):
            eng.wait_ge(s.pass_done, 1)
            n = eng.value_load(npass[0:1, 0:1], min_val=1, max_val=2 + pl.np // W)
            with eng.If(n > 1):
                with eng.Fori(1, n) as p:
                    if between is not None:
                        between(p)
                    with eng.Fori(0, NT) as i:
                        edge_body(i, p * NT + i)

        def norm_turns(eng, body):
            body(0, 0, 0, 3)
            body(1, 0, 1, 3)
            in_pairs(eng, 2, NT - 3, body)
            for t in range(NT - 3, NT):
                body(t, t // 2, t % 2, NT - 1 - t)

        def started(t):
            return min(t + 1, NT) if isinstance(t, int) else t + 1

        def is_last(t):
            return isinstance(t, int) and t == NT + 2

        def turns(eng, body):
            for t in range(4):
                body(t, [0 <= t - k < NT for k in (0, 1, 2, 3, -1)])
            with eng.Fori(4, NT - 1) as t:
                body(t, [True] * 5)
            for t in range(NT - 1, NT + 3):
                body(t, [0 <= t - k < NT for k in (0, 1, 2, 3, -1)])

        block = ctx.enter_context(nc.Block())

        @block.sync
        def _(sp):
            def load(t, h, sl):
                ge(sp, s.xn_done, t - 1)
                sp.dma_start(xs[sl], x_rows[t]).then_inc(s.x_in[sl], 16)

            def store_xn(t, sl):
                sp.wait_ge(s.xn_done, t + 1)
                sp.dma_start(xn_d[t], xn[sl]).then_inc(s.xn_stored[sl], 16)

            def body(t, h, sl, ahead=3):
                if ahead >= 3:
                    load(t + 3, h + 1 + sl, 1 - sl)
                if ahead >= 1:
                    store_xn(t + 1, 1 - sl)
                sp.wait_ge(s.tab_done, t + 1)
                sp.dma_start(table_rows[t], tab[sl]).then_inc(s.tab_stored[sl], 16)

            sp.dma_start(dsti[0:pl.gr, :, :], A.dst).then_inc(s.dst_in, 16)
            sp.dma_start(ident[:], A.ident).then_inc(s.dst_in, 16)
            for t in range(2):
                load(t, 0, t)
            for dst_, src_ in front_loads:
                sp.dma_start(dst_[:], src_).then_inc(s.front_in, 16)
            for dst_, src_ in front_rows:
                sp.dma_start(dst_[:], src_.partition_broadcast(P)).then_inc(s.front_in, 16)
            for dst_, src_ in const_loads:
                sp.dma_start(dst_[:], src_).then_inc(s.const_in, 16)
            for dst_, src_ in const_rows:
                sp.dma_start(dst_[:], src_.partition_broadcast(P)).then_inc(s.const_in, 16)
            load(2, 1, 0)
            store_xn(0, 0)
            norm_turns(sp, body)

            sp.wait_ge(s.front_done, 1)

            def edges(i, q):
                for j in range(GPT):
                    if j == HALF:
                        load_indices(i, 1, q)
                    ge(sp, s.hid_done, (q - 1) * PPB + (j + 1) * GE // PE2)
                    sp.dma_start(ea[0:ED, j, :], A.ea[:, ds((i * GPT + j) * GE * P, GE * P)])\
                        .then_inc(s.ea_in[j], 16)
                load_indices(i + 1, 0, q + 1)

            def load_indices(i, half, q):
                for j in range(half * HALF, (half + 1) * HALF):
                    ge(sp, s.xg_in[j], 16 * GE * q)
                sp.dma_start(idx[:, half * HALF * GE:(half + 1) * HALF * GE],
                             A.src[:, ds(i * TPB + half * HALF * GE, HALF * GE)]).then_inc(s.idx_in[half], 16)

            def load_weights(i):
                ge(sp, s.ws_lo, i)
                sp.dma_start(wst, A.wall[:, ds(i * WC, WC)]).then_inc(s.ws_in, 16)

            def store_weights(i):
                sp.wait_ge(s.ws_lo, i + 1)
                sp.dma_start(wsplit[:, :, ds(i * WC, WC)], wsp).then_inc(s.ws_stored, 16)

            load_indices(0, 0, 0)
            edges(0, 0)

            def move_weights(i):
                store_weights(i - 1)
                load_weights(i)
                edges(i, i)

            def big_pieces(first, last):
                for dst_, src_, after in pieces:
                    if first <= after < last:
                        sp.wait_ge(s.q2_done, after)
                        sp.wait_ge(s.ws_stored, 16 * after)
                        sp.dma_start(dst_[:], src_).then_inc(s.wts_in, 16)

            load_weights(0)
            done = 1
            for stop in sorted({after + 2 for _, _, after in pieces if after + 2 < NT}):
                with sp.Fori(done, stop) as i:
                    move_weights(i)
                big_pieces(done - 1, stop - 1)
                done = stop
            with sp.Fori(done, NT) as i:
                move_weights(i)
            store_weights(NT - 1)
            passes(sp, edges)
            big_pieces(done - 1, NT + 1)
            sp.wait_ge(s.edges_done, 1)
            for dst_, src_ in bias_loads:
                sp.dma_start(dst_[:], src_).then_inc(s.wts_in, 16)
            for dst_, src_ in late_loads:
                sp.dma_start(dst_[:], src_).then_inc(s.late_in, 16)
            for dst_, src_ in late_rows:
                sp.dma_start(dst_[:], src_.partition_broadcast(P)).then_inc(s.late_in, 16)
            for dst_, src_ in ffn_loads:
                sp.dma_start(dst_[:], src_).then_inc(s.ffn_in, 16)

            def rows(t):
                ge(sp, s.u_done, t)
                sp.dma_start(xres, xn_d[t]).then_inc(s.xres_in, 16)
                ge(sp, s.x2_done, t)
                sp.dma_start(xmix, xm_d[t]).then_inc(s.xmix_in, 16)

            rows(0)
            with sp.Fori(1, NT) as t:
                rows(t)

            with sp.Fori(0, NBATCH) as b:
                for j in range(BATCH):
                    sp.wait_ge(s.ob_done, b * BATCH + j + 1)
                    sp.dma_start(out_rows[b * BATCH + j], ob[j]).then_inc(s.ob_stored[j], 16)
            for j in range(BATCH):
                sp.wait_ge(s.ob_stored[j], 16 * NBATCH)

        @block.gpsimd
        def _(pool):
            g = nc.gpsimd
            def power(mv, rs, ready, done, t):
                pool.wait_ge(ready, t + 1)
                g.tensor_tensor(rs, mv[:, 1:2], mh[:], ALU.pow).then_inc(done, 1)

            g.memset(mh[:], -0.5).then_inc(s.mh_done, 1)
            pool.wait_ge(s.mh_done, 1)

            def norm(t, h, sl):
                ge(pool, s.xn_done, t - 1)
                power(mvx[sl], rsx[sl], s.x_mv, s.x_rstd, t)
                pool.wait_ge(s.x_rstd, t + 1)
                g.tensor_tensor(nmx[sl], mvx[sl][:, 0:1], rsx[sl], ALU.mult).then_inc(s.x_nmr, 1)

            def biased(t, h, sl):
                pool.wait_ge(s.xn_done, t + 1)
                ge(pool, s.tab_done, t - 1)
                g.tensor_tensor(xb[sl], xn[sl], b2row, ALU.add).then_inc(s.xb_done, 1)

            def low(t, h, sl):
                pool.wait_ge(s.hi16_done, t + 1)
                g.tensor_tensor(tab[sl][:, C:2 * C], xb[sl], tab[sl][:, 0:C], ALU.subtract).then_inc(s.tab_done, 1)

            norm(0, 0, 0)
            norm(1, 0, 1)
            pool.wait_ge(s.front_in, n_front)
            biased(0, 0, 0)
            norm(2, 1, 0)

            def body_b(t, h, sl, ahead=3):
                if ahead >= 1:
                    biased(t + 1, h + sl, 1 - sl)
                low(t, h, sl)
                if ahead >= 3:
                    norm(t + 3, h + 1 + sl, 1 - sl)

            norm_turns(pool, body_b)

            pool.wait_ge(s.front_done, 1)
            for sl in range(2):
                pool.wait_ge(s.tab_stored[sl], 16 * ((NT + 1 - sl) // 2))
            g.memset(ea[ED:ED + 1, :, :], 1.0).then_inc(s.ea_ones, 1)
            pool.wait_ge(s.ea_ones, 1)

            def edges(i, q):
                for j in range(GPT):
                    if j % HALF == 0:
                        pool.wait_ge(s.idx_in[j // HALF], 16 * (q + 1))
                    ge(pool, s.scat_done, (q - 1) * GPT + j + 1)
                    in_own(pool, s.pool_spare)
                    for e in range(j * GE, (j + 1) * GE):
                        g.indirect_dma_start(
                            xg[:, e, :], None, table,
                            bass.IndirectOffsetOnAxis(idx[:, e:e + 1].bitcast(mybir.dt.uint32), 0))\
                            .then_inc(s.xg_in[j], 16)

            edges(0, 0)
            with pool.Fori(1, NT) as i:
                edges(i, i)
            passes(pool, edges)

            pool.wait_ge(s.edges_done, 1)

            g.memset(bones[0:2, :], HS).then_inc(s.mh_done, 1)
            pool.wait_ge(s.mh_done, 2)
            g.memset(bones[32:34, :], 1.0).then_inc(s.mh_done, 1)
            pool.wait_ge(s.late_in, n_late)
            pool.wait_ge(s.mh_done, 3)

            def body(t, do):
                if do[0]:
                    power(mv1, rs1, s.z1_aggr, s.z1_rstd, t)
                if do[1]:
                    power(mv2, rs2, s.z2_aggr, s.z2_rstd, t - 1)
                if do[2]:
                    r = t - 2
                    pool.wait_ge(s.xres_in, 16 * (r + 1))
                    g.tensor_tensor(xres, xres, b3row, ALU.add).then_inc(s.xres_done, 1)
                    power(mv3, rs3, s.u_aggr, s.u_rstd, r)
                    pool.wait_ge(s.u_norm, r + 1)
                    g.tensor_tensor(u, u, bngrow, ALU.mult).then_inc(s.u_affine, 1)
                    pool.wait_ge(s.u_affine, 2 * r + 1)
                    g.tensor_tensor(u, u, bnbrow, ALU.add).then_inc(s.u_affine, 1)
                    power(mv4, rs4, s.x2_aggr, s.x2_rstd, r)

            turns(pool, body)

        @block.scalar
        def _(act):
            a_ = nc.scalar
            def normalize(t, h, sl):
                act.wait_ge(s.x_in[sl], 16 * (h + 1))
                act.wait_ge(s.x_nmr, t + 1)
                ge(act, s.xT_ready, t - 1)
                ge(act, s.xb_done, t - 1)
                ge(act, s.xn_stored[sl], 16 * h)
                a_.activation(xn[sl], xs[sl], ACT.Identity, bias=nmx[sl], scale=rsx[sl]).then_inc(s.xn_done, 1)

            def high(t, h, sl):
                act.wait_ge(s.xb_done, t + 1)
                ge(act, s.tab_stored[sl], 16 * h)
                a_.activation(tab[sl][:, 0:C], xb[sl], ACT.Copy).then_inc(s.hi16_done, 1)

            def start_sums(columns):
                for c in range(CC):
                    a_.activation(acc[:, CC + c, columns], ident[:], ACT.Identity, bias=b1h[:, c:c + 1], scale=0.0)\
                        .then_inc(s.acc_init, 1)

            def start_nodes(t, sl):
                act.wait_ge(s.xt_done, t + 1)
                for c in range(CC):
                    a_.activation(acc[:, c, ds(t * P, P)], psT[sl][:, c * P:(c + 1) * P], ACT.Identity,
                                  bias=b2c[:, c:c + 1], scale=twoeps).then_inc(s.xT_used, 1)

            def body(t, h, sl, ahead=3):
                start_nodes(t, sl)
                act.wait_ge(s.kv_ready, t + 1)
                ge(act, s.k_done, t - 1)
                a_.activation(ek[sl], psKV[sl][:, 0:C], ACT.Exp, scale=1 / WS).then_inc(s.ek_done, 1)
                ge(act, s.ctx_done, t - 1)
                a_.activation(vs[sl], psKV[sl][:, C:2 * C], ACT.Copy, scale=1 / WS).then_inc(s.v_done, 1)
                act.wait_ge(s.q_ready, t + 1)
                ge(act, s.q_done, t - 1)
                a_.activation(eq[sl], psQ[sl], ACT.Exp, scale=1 / WS).then_inc(s.eq_done, 1)
                if ahead >= 2:
                    normalize(t + 2, h + 1, sl)
                if ahead >= 1:
                    high(t + 1, h + sl, 1 - sl)
                start_sums(ds(t * P, P))

            act.wait_ge(s.dst_in, 32)
            normalize(0, 0, 0)
            normalize(1, 0, 1)
            act.wait_ge(s.front_in, n_front)
            for c in range(CC):
                a_.activation(b1h[:, c:c + 1], b1h[:, c:c + 1], ACT.Relu).then_inc(s.relu_b1_done, 1)
            for part, full in ((wkv[:, 0, :], wkvf), (wq[:, 0, :], wqf)):
                a_.activation(part, full, ACT.Copy, scale=WS).then_inc(s.wq_hi, 1)
            high(0, 0, 0)
            act.wait_ge(s.relu_b1_done, CC)
            start_sums(slice(pl.np, pl.wid))
            act.wait_ge(s.twoeps_done, 1)
            for c in range(CC):
                a_.activation(acc[:, c, pl.np:pl.wid], ident[:], ACT.Copy, scale=0.0).then_inc(s.acc_init, 1)
            norm_turns(act, body)

            act.wait_ge(s.const_in, n_const)
            act.wait_ge(s.front_done, 1)

            def load_mix(i):
                ge(act, s.xpb_done, i)
                act.dma_start(xml, x_rows[i]).then_inc(s.xml_in, 16)

            def store_mix(i):
                act.wait_ge(s.xm_done, i + 1)
                act.dma_start(xm_d[i], xmo).then_inc(s.xm_stored, 16)

            def edges(i, q, mix=None):
                for j in range(PPB):
                    n = q * PPB + j
                    if mix is not None and j == 3:
                        mix(i)
                    if mix is not None and j == 4:
                        act.wait_ge(s.ws_in, 16 * (i + 1))
                        ge(act, s.ws_stored, 16 * i)
                        a_.activation(wsp[:, 0, :], wst, ACT.Copy, scale=WS).then_inc(s.ws_hi, 1)
                    act.wait_ge(s.hid_done, n + 1)
                    ge(act, s.scat_done, q * GPT + j // 2 - 1)
                    a_.activation(hm[j % 4][:, 0, :], psH[j % 4], ACT.Relu).then_inc(s.hi_done, 1)

            def move_mix(i):
                store_mix(i - 1)
                load_mix(i)

            edges(0, 0, load_mix)
            with act.Fori(1, NT) as i:
                edges(i, i, move_mix)
            store_mix(NT - 1)
            passes(act, edges)

            act.wait_ge(s.late_in, n_late)

            def affine(dst_, src_, gcol, bcol, done, func=ACT.Relu):
                for j in range(HC):
                    a_.activation(dst_[:, j, :], src_[:, j // 4, (j % 4) * P:(j % 4 + 1) * P], func,
                                  bias=bcol[:, j:j + 1], scale=1 / WS if gcol is None else gcol[:, j:j + 1])\
                        .then_inc(done, 1)

            def body_n(t, do):
                if do[2]:
                    act.wait_ge(s.t2_ready, t - 1)
                    affine(z2T, pC, g2c, be2c, s.a2_done)
                if do[0]:
                    act.wait_ge(s.z1_nmr, 2 * (t + 1))
                    ge(act, s.a1_split, t)
                    a_.activation(z1.rearrange("p (a b) -> p a b", b=512), pA, ACT.Identity, bias=nm1, scale=rs1)\
                        .then_inc(s.z1_done, 1)
                if do[1]:
                    act.wait_ge(s.z2_nmr, 2 * t)
                    ge(act, s.a2_split, t - 1)
                    a_.activation(z2.rearrange("p (a b) -> p a b", b=512), pB, ACT.Identity, bias=nm2, scale=rs2)\
                        .then_inc(s.z2_done, 1)
                if do[3]:
                    act.wait_ge(s.f1_ready, t - 2)
                    ge(act, s.g_split, 2 * (t - 3))
                    affine(gfT, pA, None, fb1c, s.g_done, ACT.Gelu_apprx_tanh)
                if do[0]:
                    act.wait_ge(s.t1_ready, t + 1)
                    affine(z1T, pC, g1c, be1c, s.a1_done)


            turns(act, body_n)

        @block.tensor
        def _(pe):
            mm = nc.tensor.matmul
            pe.wait_ge(s.dst_in, 32)
            pe.wait_ge(s.rel_done, pl.nb)
            pe.wait_ge(s.span_done, 1)
            for b in range(pl.nb):
                for h in range(GE):
                    n = b * GE + h
                    ge(pe, s.relT_done, n - 1)
                    nc.tensor.transpose(psR[n % 2][:, 0:pl.gr], dsti.bitcast(f32)[0:pl.gr, b, h * P:(h + 1) * P],
                                        ident[0:pl.gr, 0:pl.gr]).then_inc(s.relT_ready, 1)
            pe.wait_ge(s.relT_done, pl.nb * GE)
            for b in range(pl.nb):
                for k in range(2):
                    last = mm(psR[k][0:1, b * pl.gr:(b + 1) * pl.gr], (bases, spans)[k][0:pl.gr, b:b + 1],
                              ident[0:pl.gr, 0:pl.gr], start=True, stop=True)
            last.then_inc(s.brow_ready, 1)
            pe.wait_ge(s.brow_done, 2)

            def transposes(t, sl):
                pe.wait_ge(s.xn_done, t + 1)
                ge(pe, s.xT_used, CC * (t - 1))
                for c in range(CC):
                    i_ = nc.tensor.transpose(psT[sl][:, c * P:(c + 1) * P], xn[sl][:, c * P:(c + 1) * P], ident[:])
                i_.then_inc(s.xT_ready, 1)

            def project(t, sl):
                pe.wait_ge(s.xt_done, t + 1)
                ge(pe, s.v_done, t - 1)
                ge(pe, s.k_done, t - 1)
                for c in range(CC):
                    for a_, b_ in TERMS:
                        i_ = mm(psKV[sl], xt[sl][:, a_, c * P:(c + 1) * P],
                                wkv[:, b_, c * 2 * C:(c + 1) * 2 * C],
                                start=c == 0 and a_ + b_ == 0, stop=c == CC - 1 and (a_, b_) == TERMS[-1])
                i_.then_inc(s.kv_ready, 1)
                ge(pe, s.q_done, t - 1)
                for o in range(CC):
                    for c in range(CC):
                        for a_, b_ in TERMS:
                            i_ = mm(psQ[sl][:, o * P:(o + 1) * P], wq[:, a_, c * C + o * P:c * C + (o + 1) * P],
                                    xt[sl][:, b_, c * P:(c + 1) * P],
                                    start=c == 0 and a_ + b_ == 0, stop=c == CC - 1 and (a_, b_) == TERMS[-1])
                i_.then_inc(s.q_ready, 1)

            def context(t, sl, first=False, last=False):
                pe.wait_ge(s.k_done, t + 1)
                pe.wait_ge(s.v_done, t + 1)
                for c in range(CC):
                    half = slice(c * P, (c + 1) * P)
                    mm(psX[:, half], vs[sl][:, half], ks[sl][:, half], start=first and c == 0,
                       stop=False, skip_group_check=True)
                for c in range(CC):
                    i_ = mm(psX[:, C + c:C + c + 1], ks[sl][:, c * P:(c + 1) * P], valid[:, ds(t, 1)],
                            start=False, stop=last and c == CC - 1, skip_group_check=True)
                i_.then_inc(s.ctx_done, 1)

            transposes(0, 0)
            transposes(1, 1)
            pe.wait_ge(s.wq_split, 2)
            pe.wait_ge(s.front_in, n_front)
            project(0, 0)

            def body(t, h, sl):
                transposes(t + 1, 1 - sl)
                project(t, sl)
                context(t - 1, 1 - sl)

            transposes(2, 0)
            project(1, 1)
            context(0, 0, first=True)

            in_pairs(pe, 2, NT - 1, body)
            project(NT - 1, (NT - 1) % 2)
            context(NT - 2, (NT - 2) % 2)
            context(NT - 1, (NT - 1) % 2, last=True)

            pe.wait_ge(s.const_in, n_const)
            pe.wait_ge(s.ctm_done, CC)
            for c in range(CC):
                i_ = mm(psM[:, c * C:(c + 1) * C], ctm[:, c, :], wproj[:, c, :], start=True, stop=True)
            i_.then_inc(s.m_ready, 1)
            pe.wait_ge(s.front_done, 1)
            pe.wait_ge(s.ea_ones, 1)

            def hidden(j, q):
                n = q * PPB + j
                group, at = j // (GE // PE2), j % (GE // PE2) * PE2 * P
                pe.wait_ge(s.ea_in[group], 16 * (q + 1))
                ge(pe, s.lo_done, n - 3)
                for e in range(PE2):
                    i_ = mm(psH[j % 4][:, e * C:(e + 1) * C], ea[0:ED + 1, group, at + e * P:at + (e + 1) * P],
                            ee1[0:ED + 1, :], start=True, stop=True)
                i_.then_inc(s.hid_done, 1)

            def scatter(j, q):
                n = q * GPT + j
                pe.wait_ge(s.xg_in[j], 16 * GE * (q + 1))
                pe.wait_ge(s.lo_done, (n + 1) * GE // PE2)
                pe.wait_ge(s.oh_done, n + 1)
                ge(pe, s.ev_done, n - 1)
                for c in range(2 * CC):
                    for e in range(GE):
                        for part in range(2):
                            if c < CC:
                                rows = xg[:, j * GE + e, part * C + c * P:part * C + (c + 1) * P]
                            else:
                                at = e % PE2 * C + (c - CC) * P
                                rows = hm[(2 * j + e // PE2) % 4][:, part, at:at + P]
                            i_ = mm(psS[j % 2][:, c * W:(c + 1) * W], rows, oh[j % 2][:, e, :],
                                    start=e == 0 and part == 0, stop=e == GE - 1 and part == 1)
                i_.then_inc(s.scat_done, 1)

            def denominators(i):
                ge(pe, s.dcl_done, i)
                for c in range(CC):
                    i_ = mm(psD[:, c * P:(c + 1) * P], ksb[:, c, :], qT[:, ds(i * C + c * P, P)],
                            start=True, stop=True)
                i_.then_inc(s.d_ready, 1)

            def attention(i):
                pe.wait_ge(s.q2_done, i + 1)
                ge(pe, s.xm_done, i)
                for c in range(CC):
                    i_ = mm(psO, q2[:, c * P:(c + 1) * P], mixw[:, c, :], start=c == 0, stop=c == CC - 1)
                i_.then_inc(s.o_ready, 1)

            def edges(i, q, mix=False):
                hidden(0, q)
                hidden(1, q)
                if mix:
                    denominators(i)
                for j in range(1, GPT):
                    hidden(2 * j, q)
                    hidden(2 * j + 1, q)
                    scatter(j - 1, q)
                if mix:
                    attention(i)
                scatter(GPT - 1, q)

            edges(0, 0, True)
            with pe.Fori(1, NT) as i:
                edges(i, i, True)
            passes(pe, edges)

            pe.wait_ge(s.edges_done, 1)

            def node_sums(t):
                ge(pe, s.hT_done, t)
                for o in range(CC):
                    for c in range(CC):
                        i_ = mm(pHT[:, o * P:(o + 1) * P], ee2[:, c, o * P:(o + 1) * P],
                                acc[:, CC + c, ds(t * P, P)], start=c == 0, stop=c == CC - 1)
                i_.then_inc(s.hT_ready, 1)

            def bias(rows, layer, n):
                at = slice(32 * layer, 32 * layer + 2)
                mm(rows, bones[at, :], bias2[at, n * 512:(n + 1) * 512], start=True, stop=False)

            def layer2(t, n):
                bias(pB[:, n, :], 1, n)
                for k in range(HC):
                    for a_, b_ in TERMS:
                        i_ = mm(pB[:, n, :], aT1[:, a_, k * P:(k + 1) * P],
                                w2[:, b_, k * H + n * 512:k * H + (n + 1) * 512],
                                start=False, stop=k == HC - 1 and (a_, b_) == TERMS[-1])
                i_.then_inc(s.z2_ready, 1)

            def count(i):
                pe.wait_ge(s.cnt_done, CANDS * (i + 1))
                mm(psCnt, ones[:], cnt, start=True, stop=True).then_inc(s.cnt_ready, 1)

            def body_n(t, do):
                if do[0]:
                    pe.wait_ge(s.hT_split, t + 1)
                    ge(pe, s.g_done, HC * (t - 3))
                    for n in range(HH):
                        bias(pA[:, n, :], 0, n)
                        for c in range(CC):
                            for a_, b_ in TERMS:
                                i_ = mm(pA[:, n, :], hTs[:, a_, c * P:(c + 1) * P],
                                        w1[:, b_, c * H + n * 512:c * H + (n + 1) * 512],
                                        start=False, stop=c == CC - 1 and (a_, b_) == TERMS[-1])
                        i_.then_inc(s.z1_ready, 1)
                if do[2]:
                    pe.wait_ge(s.z2_done, t - 1)
                    pe.wait_ge(s.a1_done, HC * started(t - 1))
                    for j in range(HC):
                        i_ = nc.tensor.transpose(pC[:, j // 4, (j % 4) * P:(j % 4 + 1) * P],
                                                 z2[:, j * P:(j + 1) * P], ident[:])
                    i_.then_inc(s.t2_ready, 1)
                if do[1]:
                    pe.wait_ge(s.a1_split, t)
                    ge(pe, s.z2_done, t - 1)
                    ge(pe, s.y3_done, t - 4 + 1)
                    layer2(t - 1, 0)
                if do[3]:
                    pe.wait_ge(s.xn2_done, t - 2)
                    ge(pe, s.hT_done, started(t))
                    for c in range(CC):
                        i_ = nc.tensor.transpose(pXT[:, c * P:(c + 1) * P], xn2[:, c * P:(c + 1) * P], ident[:])
                    i_.then_inc(s.x2T_ready, 1)
                if do[1]:
                    for n in range(1, HH):
                        layer2(t - 1, n)
                if do[3]:
                    pe.wait_ge(s.ffn_in, 16 * len(ffn_loads))
                    pe.wait_ge(s.xn2T_done, t - 2)
                    if do[0]:
                        pe.wait_ge(s.z1_done, t + 1)
                    for j in range(HC):
                        for c in range(CC):
                            for a_, b_ in TERMS:
                                i_ = mm(pA[:, j // 4, (j % 4) * P:(j % 4 + 1) * P],
                                        fw1[:, a_, c * H + j * P:c * H + (j + 1) * P],
                                        xn2T[:, b_, c * P:(c + 1) * P],
                                        start=c == 0 and a_ + b_ == 0, stop=c == CC - 1 and (a_, b_) == TERMS[-1])
                    i_.then_inc(s.f1_ready, 1)
                if do[0]:
                    pe.wait_ge(s.z1_done, t + 1)
                    ge(pe, s.a1_done, HC * t)
                    if do[2]:
                        pe.wait_ge(s.a2_done, HC * (t - 1))
                    for j in range(HC):
                        i_ = nc.tensor.transpose(pC[:, j // 4, (j % 4) * P:(j % 4 + 1) * P],
                                                 z1[:, j * P:(j + 1) * P], ident[:])
                    i_.then_inc(s.t1_ready, 1)
                if do[4]:
                    node_sums(t + 1)
                if do[2]:
                    ge(pe, s.u_done, t - 2)
                    pe.wait_ge(s.a2_split, t - 1)
                    for k in range(HC):
                        for a_, b_ in TERMS:
                            i_ = mm(pY, aT2[:, a_, k * P:(k + 1) * P], w3[:, b_, k * C:(k + 1) * C],
                                    start=k == 0 and a_ + b_ == 0, stop=k == HC - 1 and (a_, b_) == TERMS[-1])
                    i_.then_inc(s.y_ready, 1)
                if do[3]:
                    pe.wait_ge(s.z2_done, started(t - 1))
                    if is_last(t):
                        count(0)
                    pe.wait_ge(s.g_split, 2 * (t - 2))
                    for k in range(HC):
                        if is_last(t) and k == HC // 2:
                            count(1)
                        for a_, b_ in TERMS:
                            i_ = mm(pY2, gT[:, a_, k * P:(k + 1) * P], fw2[:, b_, k * C:(k + 1) * C],
                                    start=k == 0 and a_ + b_ == 0, stop=k == HC - 1 and (a_, b_) == TERMS[-1])
                    i_.then_inc(s.y2_ready, 1)

            node_sums(0)
            pe.wait_ge(s.wts_in, 16 * len(pieces + bias_loads))
            pe.wait_ge(s.mh_done, 3)
            turns(pe, body_n)

            with pe.Fori(2, DIGITS) as i:
                count(i)
            pe.wait_ge(s.cnt_done, CANDS * DIGITS + 1)
            mm(psCnt1, ones[:], cnt1, start=True, stop=True).then_inc(s.thr_ready, 1)
            pe.wait_ge(s.eqm2_done, 1)
            mm(psRank, before[:], eqm, start=True, stop=True)
            mm(psCol, ones[:], eqm, start=True, stop=True).then_inc(s.rank_ready, 1)

        @block.vector
        def _(dve):
            v = nc.vector
            def statistics(t, h, sl):
                dve.wait_ge(s.x_in[sl], 16 * (h + 1))
                v.bn_stats(stx[sl], xs[sl]).then_inc(s.x_stats, 1)
                dve.wait_ge(s.x_stats, t + 1)
                ge(dve, s.x_nmr, t - 1)
                in_own(dve, s.dve_spare)
                v.bn_aggr(mvx[sl], stx[sl]).then_inc(s.x_aggr, 1)
                dve.wait_ge(s.x_aggr, t + 1)
                v.tensor_scalar(mvx[sl][:, 0:1], mvx[sl][:, 0:1], -1.0, None, ALU.mult)
                v.tensor_scalar(mvx[sl][:, 1:2], mvx[sl][:, 1:2], LN_EPS, None, ALU.add).then_inc(s.x_mv, 1)

            statistics(0, 0, 0)
            statistics(1, 0, 1)
            dve.wait_ge(s.dst_in, 32)
            dstf = dsti.bitcast(f32)[0:pl.gr]
            v.tensor_copy(dstf, dsti[0:pl.gr]).then_inc(s.dstf_done, 1)
            dve.wait_ge(s.dstf_done, 1)
            v.tensor_reduce(bases[0:pl.gr, :], dstf, AX.X, ALU.min).then_inc(s.base_done, 1)
            v.tensor_reduce(spans[0:pl.gr, :], dstf, AX.X, ALU.max).then_inc(s.base_done, 1)
            dve.wait_ge(s.base_done, 2)
            v.tensor_tensor(spans[0:pl.gr, :], spans[0:pl.gr, :], bases[0:pl.gr, :], ALU.subtract)\
                .then_inc(s.span_done, 1)
            for b in range(pl.nb):
                i_ = v.tensor_scalar(dstf[:, b, :], dstf[:, b, :], bases[0:pl.gr, b:b + 1], None, ALU.subtract)
                i_.then_inc(s.rel_done, 1)
            relv = rel.rearrange("p (g e) -> p e g", e=GE)
            for b in range(pl.nb):
                for h in range(GE):
                    n = b * GE + h
                    gn = min(pl.gr, pl.groups - b * pl.gr)
                    dve.wait_ge(s.relT_ready, n + 1)
                    v.tensor_copy(relv[:, h, b * pl.gr:b * pl.gr + gn], psR[n % 2][:, 0:gn]).then_inc(s.relT_done, 1)
            dve.wait_ge(s.brow_ready, 1)
            v.tensor_copy(brow[0:1, :], psR[0][0:1, 0:pl.nb * pl.gr]).then_inc(s.brow_done, 1)
            v.tensor_reduce(span[0:1, 0:1], psR[1][0:1, 0:pl.nb * pl.gr], AX.X, ALU.max).then_inc(s.brow_done, 1)
            dve.wait_ge(s.brow_done, 2)
            v.tensor_copy(browi[0:1, :], brow[0:1, 0:pl.groups]).then_inc(s.browi_done, 1)
            v.tensor_copy(npass[0:1, 1:2], span[0:1, 0:1]).then_inc(s.browi_done, 1)
            dve.wait_ge(s.browi_done, 2)
            v.tensor_scalar(npass[0:1, 1:2], npass[0:1, 1:2], W.bit_length() - 1, None, ALU.arith_shift_right)\
                .then_inc(s.browi_done, 1)
            dve.wait_ge(s.browi_done, 3)
            v.tensor_scalar(npass[0:1, 0:1], npass[0:1, 1:2], 1.0, None, ALU.add).then_inc(s.pass_done, 1)
            dve.wait_ge(s.front_in, n_front)
            dve.wait_ge(s.wq_hi, 2)
            for w_, full in ((wkv, wkvf), (wq, wqf)):
                v.scalar_tensor_tensor(w_[:, 1, :], full, WS, w_[:, 0, :], ALU.mult, ALU.subtract)\
                    .then_inc(s.wq_split, 1)
            v.tensor_scalar(twoeps, epscol[:], 2.0, None, ALU.add).then_inc(s.twoeps_done, 1)
            dve.wait_ge(s.twoeps_done, 1)

            def take_xT(t, sl):
                dve.wait_ge(s.xT_ready, t + 1)
                ge(dve, s.q_ready, t - 1)
                v.tensor_copy(xt[sl][:, 0, :], psT[sl]).then_inc(s.xt_hi, 1)
                dve.wait_ge(s.xt_hi, t + 1)
                v.tensor_tensor(xt[sl][:, 1, :], psT[sl], xt[sl][:, 0, :], ALU.subtract).then_inc(s.xt_done, 1)

            def take_kvq(t, sl):
                dve.wait_ge(s.ek_done, t + 1)
                v.tensor_scalar(ek[sl], ek[sl], 1.0, WS, ALU.min, ALU.mult).then_inc(s.em_done, 1)
                ge(dve, s.ctx_done, t - 1)
                dve.wait_ge(s.em_done, t + 1)
                dve.wait_ge(s.v_done, t + 1)
                v.scalar_tensor_tensor(ks[sl], psKV[sl][:, 0:C], 0.0, ek[sl], ALU.max, ALU.add)\
                    .then_inc(s.k_done, 1)
                dve.wait_ge(s.eq_done, t + 1)
                v.tensor_scalar(eq[sl], eq[sl], 1.0, WS, ALU.min, ALU.mult).then_inc(s.eqm_done, 1)
                dve.wait_ge(s.eqm_done, t + 1)
                v.scalar_tensor_tensor(
                    qT[:, ds(t * C, C)], psQ[sl], 0.0, eq[sl], ALU.max, ALU.add).then_inc(s.q_done, 1)

            def body(t, h, sl, ahead=3):
                if ahead >= 1:
                    take_xT(t + 1, 1 - sl)
                take_kvq(t, sl)
                if ahead >= 3:
                    statistics(t + 3, h + 1 + sl, 1 - sl)

            take_xT(0, 0)
            statistics(2, 1, 0)
            norm_turns(dve, body)
            dve.wait_ge(s.xT_used, CC * NT)
            dve.wait_ge(s.acc_init, CC * NT + 2 * CC)
            dve.wait_ge(s.const_in, n_const)

            dve.wait_ge(s.ctx_done, NT)
            for c in range(CC):
                v.tensor_tensor(ctm[:, c, :], psX[:, c * P:(c + 1) * P], head, ALU.mult).then_inc(s.ctm_done, 1)
                v.tensor_scalar(ksb[:, c, :], head, psX[:, C + c:C + c + 1], None, ALU.mult).then_inc(s.ksb_done, 1)
            dve.wait_ge(s.ksb_done, CC)
            dve.wait_ge(s.m_ready, 1)
            for sl in range(2):
                dve.wait_ge(s.xn_stored[sl], 16 * ((NT + 1 - sl) // 2))
                dve.wait_ge(s.tab_stored[sl], 16 * ((NT + 1 - sl) // 2))
            v.tensor_copy(mixw, psM.rearrange("p (a b) -> p a b", b=C)).then_inc(s.front_done, 1)
            dve.wait_ge(s.front_done, 1)

            def one_hot(i, j, q):
                n = q * GPT + j
                ge(dve, s.scat_done, n - 1)
                for e in range(GE):
                    i_ = v.tensor_scalar(oh[j % 2][:, e, :], iota, rel[:, ds((i * GPT + j) * GE + e, 1)], None,
                                         ALU.is_equal)
                i_.then_inc(s.oh_done, 1)

            def low_part(j, q):
                n = q * PPB + j
                dve.wait_ge(s.hi_done, n + 1)
                v.scalar_tensor_tensor(hm[j % 4][:, 1, :], psH[j % 4], 0.0, hm[j % 4][:, 0, :], ALU.max,
                                       ALU.subtract).then_inc(s.lo_done, 1)

            def window(i, j, q):
                n = q * GPT + j
                base = dve.value_load(browi[0:1, ds(i * GPT + j, 1)], min_val=0, max_val=pl.np)
                dve.wait_ge(s.scat_done, n + 1)
                ge(dve, s.ev_done, n)
                v.tensor_tensor(acc[:, :, ds(base, W)], psS[j % 2].rearrange("p (a b) -> p a b", b=W),
                                acc[:, :, ds(base, W)], ALU.add).then_inc(s.ev_done, 1)

            def attention_rows(i, j):
                if j == 0:
                    dve.wait_ge(s.d_ready, i + 1)
                    ge(dve, s.xm_done, i)
                    v.tensor_scalar(dcl, psD, 1e-6 * WS * WS, None, ALU.max).then_inc(s.dcl_done, 1)
                if j in (0, 1):
                    dve.wait_ge(s.dcl_done, i + 1)
                    half = dcl[:, j * P:(j + 1) * P]
                    v.reciprocal(half, half).then_inc(s.rcp_done, 1)
                if j == 1:
                    dve.wait_ge(s.rcp_done, 2 * (i + 1))
                    ge(dve, s.o_ready, i)
                    v.tensor_tensor(q2, qT[:, ds(i * C, C)],
                                    dcl.rearrange("p (a b) -> p a b", b=P), ALU.mult).then_inc(s.q2_done, 1)
                if j == 2:
                    dve.wait_ge(s.ws_hi, i + 1)
                    v.scalar_tensor_tensor(wsp[:, 1, :], wst, WS, wsp[:, 0, :], ALU.mult, ALU.subtract)\
                        .then_inc(s.ws_lo, 1)
                if j == GPT - 1:
                    dve.wait_ge(s.xml_in, 16 * (i + 1))
                    dve.wait_ge(s.q2_done, i + 1)
                    v.tensor_tensor(dcl, xml, bprow, ALU.add).then_inc(s.xpb_done, 1)
                    dve.wait_ge(s.o_ready, i + 1)
                    dve.wait_ge(s.xpb_done, i + 1)
                    ge(dve, s.xm_stored, 16 * i)
                    v.tensor_tensor(xmo, psO, dcl, ALU.add).then_inc(s.xm_done, 1)

            def edges(i, q, mix=False):
                for j in range(GPT):
                    one_hot(i, j, q)
                    low_part(2 * j, q)
                    low_part(2 * j + 1, q)
                    if j:
                        window(i, j - 1, q)
                    if mix:
                        attention_rows(i, j)
                window(i, GPT - 1, q)

            edges(0, 0, True)
            with dve.Fori(1, NT) as i:
                edges(i, i, True)

            def next_window(p):
                v.tensor_scalar(rel, rel, -float(W), None, ALU.add).then_inc(s.win_done, 1)
                v.tensor_scalar(brow[0:1, :], brow[0:1, :], float(W), float(pl.np), ALU.add, ALU.min)\
                    .then_inc(s.win_done, 1)
                dve.wait_ge(s.win_done, 3 * p - 1)
                v.tensor_copy(browi[0:1, :], brow[0:1, 0:pl.groups]).then_inc(s.win_done, 1)
                dve.wait_ge(s.pass_done, 1)
                dve.wait_ge(s.win_done, 3 * p)

            passes(dve, edges, next_window)
            dve.wait_ge(s.xm_stored, 16 * NT)
            dve.wait_ge(s.ws_stored, 16 * NT)
            v.memset(oh[0], 0.0).then_inc(s.edges_done, 1)

            dve.wait_ge(s.edges_done, 1)

            def row_stats(t, scale, rows, st, mv, rs, nm, ready, stated, aggr, rstd_, nmr_):
                for n in range(HH):
                    dve.wait_ge(ready, HH * t + n + 1)
                    v.bn_stats(st[:, n, :], rows[:, n, :]).then_inc(stated, 1)
                dve.wait_ge(stated, HH * (t + 1))
                in_own(dve, s.dve_spare)
                v.bn_aggr(mv, st.rearrange("p a b -> p (a b)")).then_inc(nmr_, 1)
                dve.wait_ge(nmr_, 2 * t + 1)
                v.tensor_scalar(mv[:, 1:2], mv[:, 1:2], LN_EPS * scale * scale, None, ALU.add).then_inc(aggr, 1)
                dve.wait_ge(rstd_, t + 1)
                v.scalar_tensor_tensor(nm, mv[:, 0:1], -1.0, rs, ALU.mult, ALU.mult).then_inc(nmr_, 1)

            def split(parts, full, src_ready, hi_done, done, n, cuts=1):
                for k in range(cuts):
                    at = slice(k * H // cuts, (k + 1) * H // cuts)
                    dve.wait_ge(src_ready, HC * (n - 1) + HC * (k + 1) // cuts)
                    v.tensor_copy(parts[:, 0, at], full[:, at]).then_inc(hi_done, 1)
                    dve.wait_ge(hi_done, cuts * (n - 1) + k + 1)
                    v.tensor_tensor(parts[:, 1, at], full[:, at], parts[:, 0, at], ALU.subtract).then_inc(done, 1)

            def node_sums(t):
                dve.wait_ge(s.hT_ready, t + 1)
                ge(dve, s.z1_ready, HH * t)
                v.tensor_tensor(hT, pHT.rearrange("p (a b) -> p a b", b=P),
                                acc[:, 0:CC, ds(t * P, P)], ALU.add).then_inc(s.hT_done, 1)
                dve.wait_ge(s.hT_done, t + 1)
                v.tensor_scalar(hTs3[0], hT, HS, None, ALU.mult).then_inc(s.hT_hi, 1)
                dve.wait_ge(s.hT_hi, t + 1)
                v.scalar_tensor_tensor(hTs3[1], hT, HS, hTs3[0], ALU.mult, ALU.subtract)\
                    .then_inc(s.hT_split, 1)

            def router_weights():
                dve.wait_ge(s.w_done, 2 * NT)
                v.tensor_scalar(wv, wr_all[:], brc[:], None, ALU.add).then_inc(s.wv_done, 1)
                dve.wait_ge(s.wv_done, 1)
                v.tensor_tensor(wv, wv, valid[:], ALU.mult).then_inc(s.wv_done, 1)
                dve.wait_ge(s.wv_done, 2)
                v.tensor_tensor(wv, wv, below[:], ALU.add).then_inc(s.wv_done, 1)
                v.memset(pfx, 0).then_inc(s.bit_step, 1)
                dve.wait_ge(s.wv_done, 3)

            def as_float(key, step):
                v.tensor_scalar(t1, key, 31, 0x7FFFFFFF, ALU.arith_shift_right, ALU.bitwise_xor)\
                    .then_inc(s.bit_step, 1)
                dve.wait_ge(s.bit_step, step + 1)
                v.scalar_tensor_tensor(flt, t1, -2 ** 31, key, ALU.bitwise_or, ALU.bitwise_xor)\
                    .then_inc(s.bit_step, 1)
                dve.wait_ge(s.bit_step, step + 2)

            def digit(i):
                value, change = steps[:, ds(i, 1), 0:CANDS], steps[:, ds(i, 1), CANDS:2 * CANDS]
                dve.wait_ge(s.bit_step, 8 * i + 1)
                v.tensor_tensor(cand, pfx, value.rearrange("p a b -> p (a b)"), ALU.bitwise_or)\
                    .then_inc(s.bit_step, 1)
                dve.wait_ge(s.bit_step, 8 * i + 2)
                as_float(cand, 8 * i + 2)
                for k in range(CANDS):
                    v.tensor_scalar(reach[:, k, :], wv, flt.bitcast(f32)[:, k:k + 1], None, ALU.is_ge, ALU.add,
                                    accum_out=cnt[:, k:k + 1]).then_inc(s.cnt_done, 1)
                dve.wait_ge(s.cnt_ready, i + 1)
                v.tensor_scalar(m, psCnt, float(KSEL), -1.0, ALU.is_ge, ALU.mult).then_inc(s.bit_step, 1)
                dve.wait_ge(s.bit_step, 8 * i + 5)
                v.tensor_tensor(m, m, change.rearrange("p a b -> p (a b)"), ALU.bitwise_and).then_inc(s.bit_step, 1)
                dve.wait_ge(s.bit_step, 8 * i + 6)
                v.tensor_tensor(m4[:, 0:4], m[:, 0:4], m[:, 4:8], ALU.bitwise_xor).then_inc(s.bit_step, 1)
                dve.wait_ge(s.bit_step, 8 * i + 7)
                v.tensor_tensor(m2[:, 0:2], m4[:, 0:2], m4[:, 2:4], ALU.bitwise_xor).then_inc(s.bit_step, 1)
                dve.wait_ge(s.bit_step, 8 * i + 8)
                v.tensor_scalar(pfx, pfx, m2[:, 0:1], m2[:, 1:2], ALU.bitwise_xor, ALU.bitwise_xor)\
                    .then_inc(s.bit_step, 1)

            def body_n(t, do):
                if do[0]:
                    ge(dve, s.z1_done, t)
                    row_stats(t, WS * HS, pA, st1, mv1, rs1, nm1, s.z1_ready, s.z1_stats, s.z1_aggr,
                              s.z1_rstd, s.z1_nmr)
                if do[2]:
                    ge(dve, s.y_ready, t - 2)
                    split(aT2, z2, s.a2_done, s.a2_hi, s.a2_split, t - 1)
                if do[3]:
                    dve.wait_ge(s.x2T_ready, t - 2)
                    ge(dve, s.f1_ready, t - 3)
                    v.tensor_copy(xn2T[:, 0, :], pXT).then_inc(s.xn2T_hi, 1)
                    dve.wait_ge(s.xn2T_hi, t - 2)
                    v.tensor_tensor(xn2T[:, 1, :], pXT, xn2T[:, 0, :], ALU.subtract).then_inc(s.xn2T_done, 1)
                    if is_last(t):
                        router_weights()
                        digit(0)
                if do[1]:
                    ge(dve, s.z2_done, t - 1)
                    row_stats(t - 1, WS, pB, st2, mv2, rs2, nm2, s.z2_ready, s.z2_stats, s.z2_aggr,
                              s.z2_rstd, s.z2_nmr)
                if do[3]:
                    ge(dve, s.y2_ready, t - 3)
                    split(gT, gf, s.g_done, s.g_hi, s.g_split, t - 2, cuts=2)
                    if is_last(t):
                        digit(1)
                if do[4]:
                    node_sums(t + 1)
                if do[0]:
                    ge(dve, s.z2_ready, HH * t)
                    split(aT1, z1, s.a1_done, s.a1_hi, s.a1_split, t + 1)
                if do[2]:
                    r = t - 2
                    dve.wait_ge(s.y_ready, r + 1)
                    dve.wait_ge(s.xres_done, r + 1)
                    v.scalar_tensor_tensor(u, pY, 1 / WS, xres, ALU.mult, ALU.add).then_inc(s.u_done, 1)
                    dve.wait_ge(s.u_done, r + 1)
                    v.bn_stats(st3, u).then_inc(s.u_stats, 1)
                    dve.wait_ge(s.u_stats, r + 1)
                    in_own(dve, s.dve_spare)
                    v.bn_aggr(mv3, st3).then_inc(s.u_nmr, 1)
                    dve.wait_ge(s.u_nmr, 2 * r + 1)
                    v.tensor_scalar(mv3[:, 1:2], mv3[:, 1:2], LN_EPS, None, ALU.add).then_inc(s.u_aggr, 1)
                    dve.wait_ge(s.u_rstd, r + 1)
                    v.scalar_tensor_tensor(nm3, mv3[:, 0:1], -1.0, rs3, ALU.mult, ALU.mult).then_inc(s.u_nmr, 1)
                    dve.wait_ge(s.u_nmr, 2 * r + 2)
                    v.tensor_scalar(u, u, rs3, nm3, ALU.mult, ALU.add).then_inc(s.u_norm, 1)
                if do[3]:
                    dve.wait_ge(s.y2_ready, t - 2)
                    v.scalar_tensor_tensor(acc[:, CC:2 * CC, ds((t - 3) * P, P)],
                                           pY2.rearrange("p (a b) -> p a b", b=P), 1 / WS,
                                           fb2row.rearrange("p (a b) -> p a b", b=P), ALU.mult, ALU.add)\
                        .then_inc(s.y3_done, 1)
                if do[2]:
                    dve.wait_ge(s.u_affine, 2 * (r + 1))
                    dve.wait_ge(s.xmix_in, 16 * (r + 1))
                    v.scalar_tensor_tensor(x2, u, 0.0, xmix, ALU.max, ALU.add).then_inc(s.x2_done, 1)
                    dve.wait_ge(s.x2_done, r + 1)
                    v.bn_stats(st4, x2).then_inc(s.x2_stats, 1)
                    dve.wait_ge(s.x2_stats, r + 1)
                    in_own(dve, s.dve_spare)
                    v.bn_aggr(mv4, st4).then_inc(s.x2_nmr, 1)
                    dve.wait_ge(s.x2_nmr, 2 * r + 1)
                    v.tensor_scalar(mv4[:, 1:2], mv4[:, 1:2], LN_EPS, None, ALU.add).then_inc(s.x2_aggr, 1)
                    dve.wait_ge(s.x2_rstd, r + 1)
                    v.scalar_tensor_tensor(nm4, mv4[:, 0:1], -1.0, rs4, ALU.mult, ALU.mult).then_inc(s.x2_nmr, 1)
                    dve.wait_ge(s.x2_nmr, 2 * r + 2)
                    ge(dve, s.x2T_ready, r)
                    v.tensor_scalar(xn2, x2, rs4, nm4, ALU.mult, ALU.add).then_inc(s.xn2_done, 1)
                    dve.wait_ge(s.xn2_done, r + 1)
                    v.tensor_tensor(acc[:, 0:CC, ds(r * P, P)], x2.rearrange("p (a b) -> p a b", b=P),
                                    xn2.rearrange("p (a b) -> p a b", b=P), ALU.add).then_inc(s.base_out, 1)
                    v.tensor_tensor_reduce(u, xn2, wrrow, 1.0, 0.0, ALU.mult, ALU.add, wcol).then_inc(s.w_done, 1)
                    dve.wait_ge(s.w_done, 2 * r + 1)
                    v.tensor_copy(wr_all[:, ds(r, 1)], wcol).then_inc(s.w_done, 1)

            node_sums(0)
            turns(dve, body_n)

            with dve.Fori(2, DIGITS) as i:
                digit(i)
            dve.wait_ge(s.bit_step, 8 * DIGITS + 1)
            as_float(pfx, 8 * DIGITS + 1)
            thr = flt.bitcast(f32)[:, 0:1]
            v.tensor_scalar(gtm, wv, thr, None, ALU.is_gt, ALU.add, accum_out=cnt1).then_inc(s.cnt_done, 1)
            v.tensor_scalar(eqm, wv, thr, None, ALU.is_equal).then_inc(s.eqm2_done, 1)
            dve.wait_ge(s.thr_ready, 1)
            v.tensor_scalar(need, psCnt1, -1.0, float(KSEL), ALU.mult, ALU.add).then_inc(s.pick_step, 1)
            dve.wait_ge(s.rank_ready, 1)
            v.tensor_copy(csum, psCol).then_inc(s.pick_step, 1)
            dve.wait_ge(s.pick_step, 2)
            v.tensor_tensor_scan(incl, csum, csum, 0.0, ALU.add, ALU.bypass).then_inc(s.pick_step, 1)
            dve.wait_ge(s.pick_step, 3)
            v.tensor_tensor(incl, incl, csum, ALU.subtract).then_inc(s.pick_step, 1)
            dve.wait_ge(s.pick_step, 4)
            v.tensor_tensor(rank, psRank, incl, ALU.add).then_inc(s.pick_step, 1)
            dve.wait_ge(s.pick_step, 5)
            dve.wait_ge(s.eqm2_done, 1)
            v.scalar_tensor_tensor(rank, rank, need, eqm, ALU.is_lt, ALU.mult).then_inc(s.pick_step, 1)
            dve.wait_ge(s.pick_step, 6)
            dve.wait_ge(s.cnt_done, CANDS * DIGITS + 1)
            v.tensor_tensor(gtm, gtm, rank, ALU.add).then_inc(s.pick_step, 1)
            dve.wait_ge(s.pick_step, 7)
            v.tensor_tensor(mw, gtm, wv, ALU.mult).then_inc(s.pick_step, 1)
            dve.wait_ge(s.pick_step, 8)
            dve.wait_ge(s.base_out, NT)
            dve.wait_ge(s.y3_done, NT)
            def outputs(b):
                for j in range(BATCH):
                    t = b * BATCH + j
                    ge(dve, s.ob_stored[j], 16 * b)
                    v.scalar_tensor_tensor(ob[j].rearrange("p (a b) -> p a b", b=P), acc[:, CC:2 * CC, ds(t * P, P)],
                                           mw[:, ds(t, 1)], acc[:, 0:CC, ds(t * P, P)], ALU.mult, ALU.add)\
                        .then_inc(s.ob_done, 1)

            outputs(0)
            with dve.Fori(1, NBATCH) as b:
                outputs(b)


def kernel(**inputs):
    import concourse.bacc as _bacc
    from concourse.bass_utils import run_bass_kernel_spmd as _run

    g = {k[3:] if k.startswith("L0_") else k: np.asarray(v) for k, v in inputs.items()}
    n, e = g["x"].shape[0], g["src"].shape[0]
    pl = plan(n, e, g["gnn_w1"].shape[1])
    ep = pl.tiles * P

    def chunks(w):
        return w.reshape(-1, P, w.shape[1]).transpose(1, 0, 2)

    def flat(w):
        return chunks(w).reshape(P, -1)

    def column(b):
        return b.reshape(-1, P).T

    dst = np.full(pl.nb * pl.gr * GE * P, n, np.int32)
    dst[:e] = g["dst"]
    src = np.zeros(ep, np.int32)
    src[:e] = g["src"]
    x = np.zeros((pl.np, C), np.float32)
    x[:n] = g["x"]
    ea = np.zeros((ED, ep), np.float32)
    ea[:, :e] = g["edge_attr_64"].T
    wall = np.zeros((P, pl.nt * pl.wchunk), np.float32)
    mats = np.concatenate([flat(g[k]) for k in ("gnn_w1", "gnn_w2", "gnn_w3", "ffn_w1", "ffn_w2")], 1)
    wall[:, :mats.shape[1]] = mats
    wall[0:2, mats.shape[1]:pl.wcols] = g["gnn_b1"], g["gnn_b2"]
    arrays = {
        "x": x, "ea": ea, "src": np.concatenate([src, src[:pl.gpt * GE * P // 2]]).reshape(-1, P).T,
        "dst": dst.reshape(pl.nb, pl.gr, GE * P).transpose(1, 0, 2),
        "eps": g["gnn_eps"].reshape(1), "br": g["ffn_br"].reshape(1),
        "ee_w1": g["gnn_ee_w1"], "ee_b1": g["gnn_ee_b1"].reshape(1, -1),
        "ee_b1c": column(g["gnn_ee_b1"]), "ee_w2": chunks(g["gnn_ee_w2"]),
        "ee_b2": g["gnn_ee_b2"], "ee_b2c": column(g["gnn_ee_b2"]),
        "wall": wall,
        "b3": g["gnn_b3"],
        "g1": column(g["gnn_g1"]), "be1": column(g["gnn_be1"]),
        "g2": column(g["gnn_g2"]), "be2": column(g["gnn_be2"]),
        "bn_g": g["gnn_bn_g"], "bn_b": g["gnn_bn_b"],
        "wq": flat(g["mix_Wq"].T), "wkv": flat(g["mix_Wkv"].T), "wproj": chunks(g["mix_Wproj"].T),
        "bproj": g["mix_bproj"], "wr": g["ffn_wr"].reshape(-1),
        "fb1": column(g["ffn_b1"]),
        "fb2": g["ffn_b2"],
        "steps": np.tile(digit_steps().reshape(-1), (P, 1)),
        **constants(pl),
    }
    arrays = {k: np.ascontiguousarray(v) for k, v in arrays.items()}
    nc = _bacc.Bacc("TRN2", target_bir_lowering=False, num_devices=1)
    aps = namedtuple("Inputs", arrays)(**{
        k: nc.dram_tensor(f"in_{k}", v.shape, mybir.dt.from_np(v.dtype), kind="ExternalInput").ap()
        for k, v in arrays.items()})
    out = nc.dram_tensor("out_0", (pl.np, C), mybir.dt.float32, kind="ExternalOutput").ap()
    gps_kernel(nc, aps, out, pl)
    r = _run(nc, [{f"in_{k}": v for k, v in arrays.items()}], core_ids=[0])
    return r.results[0]["out_0"][:n]
```
